# Optimizing a Trainium2 kernel written in Bass

```python
import numpy as np
import jax
import jax.numpy as jnp

def _softmax(x, axis=-1):
    return jax.nn.softmax(x, axis=axis)

def _gelu(x):
    return jax.nn.gelu(x, approximate=True)

def _silu(x):
    return jax.nn.silu(x)

def _sigmoid(x):
    return jax.nn.sigmoid(x)

def _layernorm(x, axis=-1, eps=1e-05):
    m = jnp.mean(x, axis=axis, keepdims=True)
    v = jnp.var(x, axis=axis, keepdims=True)
    return (x - m) / jnp.sqrt(v + eps)

def _scatter_add(tgt, idx, src, axis=0):
    return tgt.at[idx].add(src)

def _segment_sum(src, seg, n):
    return jax.ops.segment_sum(src, seg, n)
kernel_name = 'mk_seq_postln_d1_jaxref_r4_2bd950'

def setup_inputs(seed: int=0):
    np.random.seed(seed)
    _w = jnp.asarray

    def _L0_attn_setup():
        import jax, jax.numpy as jnp
        import numpy as np
        import math
        B, T, C = (32, 64, 256)
        LAYER_ID, NUM_LAYERS = (12, 24)
        NEG_INF = -1e+38

        def wkv(time_decay, time_first, k, v):
            w = -jnp.exp(time_decay)
            u = time_first
            kT = jnp.swapaxes(k, 0, 1)
            vT = jnp.swapaxes(v, 0, 1)

            def step(carry, kv):
                p, q, o = carry
                kt, vt = kv
                no = jnp.maximum(o, u + kt)
                A = jnp.exp(o - no)
                Bc = jnp.exp(u + kt - no)
                y = (A * p + Bc * vt) / (A * q + Bc)
                no2 = jnp.maximum(w + o, kt)
                A2 = jnp.exp(w + o - no2)
                B2 = jnp.exp(kt - no2)
                return ((A2 * p + B2 * vt, A2 * q + B2, no2), y)
            init = (jnp.zeros((k.shape[0], k.shape[2]), k.dtype), jnp.zeros((k.shape[0], k.shape[2]), k.dtype), jnp.full((k.shape[0], k.shape[2]), NEG_INF, k.dtype))
            _, yT = jax.lax.scan(step, init, (kT, vT))
            return jnp.swapaxes(yT, 0, 1)
        key = jax.random.key(seed)
        ks = jax.random.split(key, 5)
        x = jax.random.normal(ks[0], (B, T, C), dtype=jnp.float32)
        r01 = LAYER_ID / (NUM_LAYERS - 1)
        r10 = 1.0 - LAYER_ID / NUM_LAYERS
        h = jnp.arange(C, dtype=jnp.float32)
        time_decay = -5.0 + 8.0 * (h / (C - 1)) ** (0.7 + 1.3 * r01)
        tf = (jnp.arange(C) + 1) % 3 - 1
        time_first = jnp.full((C,), math.log(0.3), jnp.float32) + 0.5 * tf.astype(jnp.float32)
        xr = (jnp.arange(C, dtype=jnp.float32) / C)[None, None, :]
        time_mix_k = xr ** r10
        time_mix_v = xr ** r10 + 0.3 * r01
        time_mix_r = xr ** (0.5 * r10)
        s = 1.0 / math.sqrt(C)
        Wk = jax.random.normal(ks[1], (C, C), jnp.float32) * s
        Wv = jax.random.normal(ks[2], (C, C), jnp.float32) * s
        Wr = jax.random.normal(ks[3], (C, C), jnp.float32) * s
        Wo = jax.random.normal(ks[4], (C, C), jnp.float32) * s
        return {'x': x, 'time_decay': time_decay, 'time_first': time_first, 'time_mix_k': time_mix_k, 'time_mix_v': time_mix_v, 'time_mix_r': time_mix_r, 'Wk': Wk, 'Wv': Wv, 'Wr': Wr, 'Wo': Wo}
    _L0_attn_in = _L0_attn_setup()

    def _L0_ffn_setup():
        import jax, jax.numpy as jnp
        import numpy as np
        D_MODEL, D_FF, N_EXPERTS, TOP_K = (256, 1024, 8, 2)
        B, S = (2, 512)
        key = jax.random.key(seed)
        ks = jax.random.split(key, 7)
        scale = 0.02
        return {'x': jax.random.normal(ks[0], (B, S, D_MODEL), dtype=jnp.float32), 'W1': jax.random.normal(ks[1], (N_EXPERTS, D_MODEL, D_FF), dtype=jnp.float32) * scale, 'b1': jnp.zeros((N_EXPERTS, D_FF), dtype=jnp.float32), 'W2': jax.random.normal(ks[2], (N_EXPERTS, D_FF, D_MODEL), dtype=jnp.float32) * scale, 'b2': jnp.zeros((N_EXPERTS, D_MODEL), dtype=jnp.float32), 'Wg': jax.random.normal(ks[3], (D_MODEL, N_EXPERTS), dtype=jnp.float32) * scale, 'bg': jnp.zeros((N_EXPERTS,), dtype=jnp.float32)}
    _L0_ffn_in = _L0_ffn_setup()
    _d = {'L0_attn_x': _L0_attn_in['x'], 'L0_attn_time_decay': _L0_attn_in['time_decay'], 'L0_attn_time_first': _L0_attn_in['time_first'], 'L0_attn_time_mix_k': _L0_attn_in['time_mix_k'], 'L0_attn_time_mix_v': _L0_attn_in['time_mix_v'], 'L0_attn_time_mix_r': _L0_attn_in['time_mix_r'], 'L0_attn_Wk': _L0_attn_in['Wk'], 'L0_attn_Wv': _L0_attn_in['Wv'], 'L0_attn_Wr': _L0_attn_in['Wr'], 'L0_attn_Wo': _L0_attn_in['Wo'], 'L0_ffn_W1': _L0_ffn_in['W1'], 'L0_ffn_b1': _L0_ffn_in['b1'], 'L0_ffn_W2': _L0_ffn_in['W2'], 'L0_ffn_b2': _L0_ffn_in['b2'], 'L0_ffn_Wg': _L0_ffn_in['Wg'], 'L0_ffn_bg': _L0_ffn_in['bg']}
    _x0 = _d['L0_attn_x']
    _d['L0_attn_x'] = jax.random.normal(jax.random.fold_in(jax.random.key(seed), 1), (2, 2048, 256), dtype=_x0.dtype)
    del _x0
    return _d

def reference(L0_attn_x, L0_attn_time_decay, L0_attn_time_first, L0_attn_time_mix_k, L0_attn_time_mix_v, L0_attn_time_mix_r, L0_attn_Wk, L0_attn_Wv, L0_attn_Wr, L0_attn_Wo, L0_ffn_W1, L0_ffn_b1, L0_ffn_W2, L0_ffn_b2, L0_ffn_Wg, L0_ffn_bg):

    def _L0_attn_ref(x, time_decay, time_first, time_mix_k, time_mix_v, time_mix_r, Wk, Wv, Wr, Wo):
        import jax, jax.numpy as jnp
        import numpy as np
        import math
        B, T, C = (32, 64, 256)
        LAYER_ID, NUM_LAYERS = (12, 24)
        NEG_INF = -1e+38

        def wkv(time_decay, time_first, k, v):
            w = -jnp.exp(time_decay)
            u = time_first
            kT = jnp.swapaxes(k, 0, 1)
            vT = jnp.swapaxes(v, 0, 1)

            def step(carry, kv):
                p, q, o = carry
                kt, vt = kv
                no = jnp.maximum(o, u + kt)
                A = jnp.exp(o - no)
                Bc = jnp.exp(u + kt - no)
                y = (A * p + Bc * vt) / (A * q + Bc)
                no2 = jnp.maximum(w + o, kt)
                A2 = jnp.exp(w + o - no2)
                B2 = jnp.exp(kt - no2)
                return ((A2 * p + B2 * vt, A2 * q + B2, no2), y)
            init = (jnp.zeros((k.shape[0], k.shape[2]), k.dtype), jnp.zeros((k.shape[0], k.shape[2]), k.dtype), jnp.full((k.shape[0], k.shape[2]), NEG_INF, k.dtype))
            _, yT = jax.lax.scan(step, init, (kT, vT))
            return jnp.swapaxes(yT, 0, 1)
        xx = jnp.pad(x, ((0, 0), (1, 0), (0, 0)))[:, :-1, :]
        xk = x * time_mix_k + xx * (1.0 - time_mix_k)
        xv = x * time_mix_v + xx * (1.0 - time_mix_v)
        xr = x * time_mix_r + xx * (1.0 - time_mix_r)
        k = jnp.einsum('btc,dc->btd', xk, Wk)
        v = jnp.einsum('btc,dc->btd', xv, Wv)
        r = jnp.einsum('btc,dc->btd', xr, Wr)
        sr = jax.nn.sigmoid(r)
        rwkv = sr * wkv(time_decay, time_first, k, v)
        return jnp.einsum('btc,dc->btd', rwkv, Wo)

    def _L0_ffn_ref(x, W1, b1, W2, b2, Wg, bg):
        import jax, jax.numpy as jnp
        import numpy as np
        D_MODEL, D_FF, N_EXPERTS, TOP_K = (256, 1024, 8, 2)
        B, S = (2, 512)
        Bx, Sx, d = x.shape
        E = W1.shape[0]
        logits = jnp.einsum('bsd,de->bse', x, Wg) + bg
        topk_scores, topk_idx = jax.lax.top_k(logits, TOP_K)
        topk_scores = jax.nn.softmax(topk_scores, axis=-1)
        tokens = x.reshape(-1, d)
        idx_flat = topk_idx.reshape(-1, TOP_K)
        sc_flat = topk_scores.reshape(-1, TOP_K)
        comb = (jax.nn.one_hot(idx_flat, E, dtype=x.dtype) * sc_flat[..., None]).sum(axis=1)
        h = jnp.einsum('td,edf->etf', tokens, W1) + b1[:, None, :]
        even = (jnp.arange(E) % 2 == 0)[:, None, None]
        a = jnp.where(even, jax.nn.gelu(h, approximate=False), jax.nn.silu(h))
        y = jnp.einsum('etf,efd->etd', a, W2) + b2[:, None, :]
        out = jnp.einsum('te,etd->td', comb, y)
        return out.reshape(Bx, Sx, d)
    x = L0_attn_x
    x = _layernorm(x + _L0_attn_ref(x, L0_attn_time_decay, L0_attn_time_first, L0_attn_time_mix_k, L0_attn_time_mix_v, L0_attn_time_mix_r, L0_attn_Wk, L0_attn_Wv, L0_attn_Wr, L0_attn_Wo), axis=-1)
    x = _layernorm(x + _L0_ffn_ref(x, L0_ffn_W1, L0_ffn_b1, L0_ffn_W2, L0_ffn_b2, L0_ffn_Wg, L0_ffn_bg), axis=-1)
    return x

_drawn_inputs = setup_inputs


def setup_inputs(seed=0):
    import zlib

    import numpy as np

    out = dict(_drawn_inputs(seed))
    spreads = {'L0_ffn_b1': (0.0, 0.325), 'L0_ffn_b2': (0.0, 0.1), 'L0_ffn_bg': (0.0, 0.1)}
    factors = {}
    for name, (base, spread) in spreads.items():
        noise = np.random.default_rng([zlib.crc32(name.encode()), seed]).standard_normal(out[name].shape)
        drawn = base * np.exp(spread * noise) if base else spread * noise
        out[name] = jnp.asarray(drawn.astype(out[name].dtype))
    for name, factor in factors.items():
        out[name] = (out[name] * factor).astype(out[name].dtype)
    return out
```

```python
from contextlib import ExitStack

import numpy as np

import concourse.bass as bass
from concourse import mybir

ALU = mybir.AluOpType
ACT = mybir.ActivationFunctionType
AX = mybir.AxisListType
F32 = mybir.dt.float32
F32R = mybir.dt.float32r
I32 = mybir.dt.int32
U32 = mybir.dt.uint32

P = 128


class Step:

    def __init__(self, m, off, every, count):
        self.m, self.off, self.every, self.count = m, off, every, count

    def __add__(self, k):
        return Step(self.m, self.off + k, self.every, self.count)

    def __sub__(self, k):
        return self + -k

    @property
    def fixed(self):
        return self.m is None

    @property
    def number(self):
        return self.off if self.fixed else self.m * self.every + self.off

    @property
    def exists(self):
        return not self.fixed or 0 <= self.off < self.count

    @property
    def slot(self):
        return self.off % self.every

    def turn(self, n=1, more=0):
        if self.fixed:
            return self.off // self.every * n + more
        return self.m * n + (self.off // self.every * n + more)

    def turn4(self, n, more):
        return (self.off // 4) * n + more if self.fixed else self.m * (self.every // 4 * n) + (self.off // 4 * n + more)

    def upto(self, each, n=None):
        n = each if n is None else n
        if self.fixed:
            return self.off * each + n
        return self.m * (self.every * each) + (self.off * each + n)


def build(nc, x, decay, first, mix_k, mix_v, mix_r, wkT, wvT, wrT, woT, w1, b1, w2, b2, wgT, bg, out):
    B, T, C = x.shape
    E, _, F = w1.shape
    CC = C // P
    TC = 256
    NCH = T // TC
    TH = TC // P
    J = B * TH
    N = B * TC
    W = CC * N
    TOKENS = B * T
    TILES = (2 * TOKENS + E * (P - 1)) // P
    REGION = TOKENS + P
    DUMMY = E * REGION
    REC = C + 1
    NOWHERE = 1 << 20
    FC = F // P
    RING = 8
    W1E, W2E = CC * F, FC * C
    WE = W1E + W2E
    LOWEST = -1e38
    EPS = 1e-5

    xs = nc.dram_tensor("records_dram", (DUMMY + P, REC), F32, kind="Internal").ap()
    ys = nc.dram_tensor("expert_out_dram", (2 * TOKENS, C), F32, kind="Internal").ap()
    x1d = nc.dram_tensor("x1_dram", (B, T, C), F32, kind="Internal").ap()

    with ExitStack() as ctx:
        def sb(name, shape, dt=F32, where=ctx):
            return where.enter_context(nc.sbuf_tensor(name, shape, dt))

        def sem(name):
            return ctx.enter_context(nc.semaphore(name))

        ident = sb("ident", [P, P])
        before = sb("before", [P, P])
        ones = sb("ones", [P, P])
        decay_c = sb("decay_c", [P, CC])
        first_c = sb("first_c", [P, CC])
        mix_c = sb("mix_c", [P, 3, CC])
        unmix_c = sb("unmix_c", [P, 3, CC])
        bg_b = sb("bg_b", [P, E])
        expert_no = sb("expert_no", [P, E])
        region_no = sb("region_no", [P, E])
        dest_all = sb("dest_all", [P, NCH * J * 2], I32)
        half_neg = sb("half_neg", [P, J])
        eps_b = sb("eps_b", [P, J])
        top2 = sb("top2", [P, NCH, J, 2])
        score = sb("score", [P, NCH * J, 2])
        score_t = sb("score_t", [P, NCH * J, 2])
        pad_rec = sb("pad_rec", [P, REC])
        cnt_f = sb("cnt_f", [1, E])
        cnt_i = sb("cnt_i", [1, E], I32)
        tiles_i = sb("tiles_i", [1, E], I32)
        tiles_f = sb("tiles_f", [1, E])
        ends_f = sb("ends_f", [1, E])
        starts_f = sb("starts_f", [1, E])
        rowbase = sb("rowbase", [1, E])
        pad_row = sb("pad_row", [1, E], I32)
        ends = sb("ends", [1, E], I32)
        RECS = J * 2 * REC
        staging = sb("staging", [P, max(WE, 2 * RECS)])
        raw = staging[:, 0:WE]
        rec = [staging[:, n * RECS:(n + 1) * RECS].rearrange("p (j k c) -> p j k c", j=J, k=2) for n in range(2)]
        var_e = sb("var_e", [P, J])
        rstd = sb("rstd", [P, 2, J])
        stats = sb("stats", [P, J, 6])
        mv = sb("mv", [P, J, 2])

        phase_a = ExitStack()
        sb("w_slot0_place", [P, 2 * WE], F32, phase_a)
        xin = [sb(f"xin{n}", [P, B, TH, C], F32, phase_a) for n in range(2)]
        xres = [sb(f"xres{n}", [P, B, TH, C], F32, phase_a) for n in range(2)]
        xh = [sb(f"xh{n}", [P, CC, B, TC + 2], F32R, phase_a) for n in range(2)]
        xl = [sb(f"xl{n}", [P, CC, B, TC + 2], F32R, phase_a) for n in range(2)]
        wq = sb("wq", [P, 3, 2, 2, CC, C], F32R, phase_a)
        wo = sb("wo", [P, CC, C], F32, phase_a)
        wg = sb("wg", [P, CC, E], F32, phase_a)
        w_row = sb("w_row", [P, CC, TC], F32, phase_a)
        o_all = sb("o_all", [P, CC, B, TC + 1], F32, phase_a)
        p_all = sb("p_all", [P, CC, B, TC + 1], F32, phase_a)
        q_all = sb("q_all", [P, CC, B, TC + 1], F32, phase_a)
        s_buf = sb("s_buf", [P, CC, B, TC], F32, phase_a)
        A1 = sb("A1", [P, CC, B, TC], F32, phase_a)
        B1 = sb("B1", [P, CC, B, TC], F32, phase_a)
        A2 = sb("A2", [P, CC, B, TC], F32, phase_a)
        B2 = sb("B2", [P, CC, B, TC], F32, phase_a)
        v = [sb(f"v{n}", [P, CC, B, TC], F32, phase_a) for n in range(2)]
        gate = [sb(f"gate{n}", [P, CC, B, TC], F32, phase_a) for n in range(2)]
        b2v = sb("b2v", [P, CC, B, TC], F32, phase_a)
        bv = sb("bv", [P, CC, B, TC], F32, phase_a)
        num = sb("num", [P, CC, B, TC], F32, phase_a)
        den = sb("den", [P, CC, B, TC], F32, phase_a)
        r0 = sb("r0", [P, CC, B, TC], F32, phase_a)
        newton = sb("newton", [P, CC, B, TC], F32, phase_a)
        mixed = newton
        wraw = [s_buf, A1, B1]
        wscaled = [num, den, r0]
        x1T = sb("x1T", [P, CC, N], F32, phase_a)
        lg = sb("lg", [P, J, E], F32, phase_a)
        m8 = sb("m8", [P, J, 8], F32, phase_a)
        i8 = sb("i8", [P, J, 8], U32, phase_a)
        idxf = sb("idxf", [P, J, 2], F32, phase_a)
        hot = sb("hot", [P, J, 2, E], F32, phase_a)
        seen = sb("seen", [P, J + 1, E], F32, phase_a)
        picks = sb("picks", [P, J, E], F32, phase_a)
        rank = sb("rank", [P, J, E], F32, phase_a)
        spread = sb("spread", [P, J, 2, E], F32, phase_a)
        slot_f = sb("slot_f", [P, J, 2], F32, phase_a)
        slot_i = [sb(f"slot_i{n}", [P, J * 2], I32, phase_a) for n in range(2)]

        def ps(name, shape, where):
            return where.enter_context(nc.psum_tensor(name, shape, F32))

        xT_ps = ps("xT_ps", [P, CC, N], phase_a)
        k_ps = ps("k_ps", [P, CC, N], phase_a)
        vr_ps = [ps(f"vr_ps{n}", [P, N], phase_a) for n in range(2)]
        wo_ps = ps("wo_ps", [P, TH, C], phase_a)
        small_ps = ps("small_ps", [P, 512], phase_a)
        lg_ps = small_ps[:, 0:J * E].rearrange("p (j e) -> p j e", j=J)
        rank_ps = small_ps[:, 64:64 + J * E].rearrange("p (j e) -> p j e", j=J)
        cnt_ps = small_ps[:, 128:128 + E]
        phase_a.close()

        phase_b = ctx.enter_context(ExitStack())
        wx = sb("wx", [P, 2, 2, WE], F32R, phase_b)
        b1_b = sb("b1_b", [P, 2 * F], F32, phase_b)
        b2_b = sb("b2_b", [P, 2 * C], F32, phase_b)
        recs = [sb(f"recs{n}", [P, REC], F32, phase_b) for n in range(4)]
        dest = [sb(f"dest{n}", [P, 1], I32, phase_b) for n in range(RING)]
        xTh = [sb(f"xTh{n}", [P, CC, P], F32R, phase_b) for n in range(2)]
        xTl = [sb(f"xTl{n}", [P, CC, P], F32R, phase_b) for n in range(2)]
        hid = [sb(f"hid{n}", [P, F], F32, phase_b) for n in range(2)]
        aTh = [sb(f"aTh{n}", [P, FC, P], F32R, phase_b) for n in range(2)]
        aTl = [sb(f"aTl{n}", [P, FC, P], F32R, phase_b) for n in range(2)]
        y_sb = [sb(f"y_sb{n}", [P, C], F32, phase_b) for n in range(RING)]
        tile_f = sb("tile_f", [1, TILES, E], F32, phase_b)
        past_s = sb("past_s", [1, TILES, E], F32, phase_b)
        past_e = sb("past_e", [1, TILES, E], F32, phase_b)
        tile_row = sb("tile_row", [1, TILES], F32, phase_b)
        row_f = sb("row_f", [1, TILES], F32, phase_b)
        ex_f = sb("ex_f", [1, TILES], F32, phase_b)
        real_f = sb("real_f", [1, TILES], F32, phase_b)
        row_t = sb("row_t", [1, TILES], I32, phase_b)
        ex_t = sb("ex_t", [1, TILES], I32, phase_b)
        par_t = sb("par_t", [1, TILES], I32, phase_b)
        yy = [sb(f"yy{n}", [P, B, TH, 2 * C], F32, phase_b) for n in range(2)]
        xx = [sb(f"xx{n}", [P, B, TH, C], F32, phase_b) for n in range(2)]
        zz = sb("zz", [P, J, C], F32, phase_b)
        res = [sb(f"res{n}", [P, B, TH, C], F32, phase_b) for n in range(2)]
        h_ps = [ps(f"h_ps{n}", [P, F], phase_b) for n in range(2)]
        aT_ps = ps("aT_ps", [P, FC, P], phase_b)
        xT2_ps = ps("xT2_ps", [P, 4, P], phase_b)[:, 0:CC, :]
        y_ps = ps("y_ps", [P, 512], phase_b)[:, 0:C]

        carried = sem("carried")
        consts_in, weights_in, gate_in, raw_in = sem("consts_in"), sem("weights_in"), sem("gate_in"), sem("raw_in")
        made, made2, padded = sem("made"), sem("made2"), sem("padded")
        setup_act, setup_dve = sem("setup_act"), sem("setup_dve")
        scaled, w_hi, w_lo = sem("scaled"), sem("w_hi"), sem("w_lo")
        xin_in = [sem(f"xin_in{n}") for n in range(2)]
        xres_in = [sem(f"xres_in{n}") for n in range(2)]
        xT_done, xh_done, xl_done = sem("xT_done"), sem("xh_done"), sem("xl_done")
        vr_done, k_done, v_out, gate_out = sem("vr_done"), sem("k_done"), sem("v_out"), sem("gate_out")
        o_carry, o_done, s_done, d3_done, d2_done = (sem(n) for n in ("o_carry", "o_done", "s_done", "d3_done", "d2_done"))
        relu_done, a1_done, b1_done, a2_done, b2_done = (sem(n) for n in ("relu_done", "a1_done", "b1_done", "a2_done", "b2_done"))
        qp_carry, q_done, p_done = sem("qp_carry"), sem("q_done"), sem("p_done")
        b2v_done, bv_done, aq_done, den_done, num_done = (sem(n) for n in ("b2v_done", "bv_done", "aq_done", "den_done", "num_done"))
        ln_done, r0_done, div_done, mixed_done = sem("ln_done"), sem("r0_done"), sem("div_done"), sem("mixed_done")
        wo_done, res_done, bn_done, mv_done = sem("wo_done"), sem("res_done"), sem("bn_done"), sem("mv_done")
        vare_done, rstd_done, x1_done, rec2_done = sem("vare_done"), sem("rstd_done"), sem("x1_done"), sem("rec2_done")
        x1T_done, x1T_out, lg_done = sem("x1T_done"), sem("x1T_out"), sem("lg_done")
        route, rank_done, slots = sem("route"), sem("rank_done"), sem("slots")
        rec_out = [sem(f"rec_out{n}") for n in range(2)]
        x1_out = [sem(f"x1_out{n}") for n in range(2)]
        cnt_done, table, table_done, pads_out = sem("cnt_done"), sem("table"), sem("table_done"), sem("pads_out")
        bias0_in, bias_in, hi_done, weights_ready = sem("bias0_in"), sem("bias_in"), sem("hi_done"), sem("weights_ready")
        rec_in = [sem(f"rec_in{n}") for n in range(4)]
        y_out = [sem(f"y_out{n}") for n in range(RING)]
        tx_done, txh_done, txl_done = sem("tx_done"), sem("txh_done"), sem("txl_done")
        mm1_done, hid_done, act_done = sem("mm1_done"), sem("hid_done"), sem("act_done")
        aT_done, aTh_done, aTl_done = sem("aT_done"), sem("aTh_done"), sem("aTl_done")
        mm2_done, y_done = sem("mm2_done"), sem("y_done")
        exp_done, score_done = sem("exp_done"), sem("score_done")
        yy_in = [sem(f"yy_in{n}") for n in range(2)]
        res_out = [sem(f"res_out{n}") for n in range(2)]
        c_sum, c_bn, c_mv, c_var, c_rstd, c_res = (sem(n) for n in ("c_sum", "c_bn", "c_mv", "c_var", "c_rstd", "c_res"))

        BG = 16
        REC_DMAS = 2 * J * 16
        ROUTE1, ROUTE2 = 3 * J + 4, 6

        def chunks(eng, body):
            plain = lambda n: Step(None, n, 2, NCH)
            for n in range(-2, 2):
                body(plain(n))
            with eng.Fori(1, NCH // 2 - 1) as m:
                body(Step(m, 0, 2, NCH))
                body(Step(m, 1, 2, NCH))
            for n in range(NCH - 2, NCH + 2):
                body(plain(n))

        LAST = (TILES + 1) // RING * RING - RING

        def tiles(eng, body):
            plain = lambda n: Step(None, n, RING, TILES)
            for n in range(-2, RING):
                body(plain(n))
            with eng.Fori(1, LAST // RING) as m:
                for n in range(RING):
                    body(Step(m, n, RING, TILES))
            for n in range(LAST, TILES + 1):
                body(plain(n))

        def after(eng, semaphore, value):
            if not isinstance(value, int) or value > 0:
                eng.wait_ge(semaphore, value)

        def take_wait(eng):
            eng.sem_inc(carried, 1)

        def load_chunk(sp, to, ap, i, done):
            for b in range(B):
                sp.dma_start(to[:, b], ap[b, bass.ds(i.number * TC, TC), :].rearrange("(h p) c -> p h c", p=P)).then_inc(done, 16)

        def store_chunk(sp, ap, i, rows, done):
            for b in range(B):
                sp.dma_start(ap[b, bass.ds(i.number * TC, TC), :].rearrange("(h p) c -> p h c", p=P), rows[:, b]).then_inc(done, 16)

        def phase_b_may_start(eng):
            eng.wait_ge(table_done, 1)
            for n in range(2):
                eng.wait_ge(rec_out[n], NCH // 2 * REC_DMAS + BG)
                eng.wait_ge(x1_out[n], NCH // 2 * B * 16 + BG)

        block = ctx.enter_context(nc.Block())

        @block.sync
        def _(sp):
            plain = lambda n: Step(None, n, 2, NCH)
            load_chunk(sp, xin[0], x, plain(0), xin_in[0])
            for n, w in enumerate((wvT, wrT, wkT)):
                sp.dma_start(wraw[n][:].rearrange("p c b t -> p (c b t)")[:, 0:CC * C].rearrange("p (c d) -> p c d", c=CC),
                             w.rearrange("(c p) d -> p c d", p=P)).then_inc(weights_in, 16)
            for n, m in enumerate((mix_v, mix_r, mix_k)):
                sp.dma_start(mix_c[:, n, :], m.rearrange("a b (c p) -> p (a b c)", p=P),
                             allow_slow_non_contiguous=True).then_inc(consts_in, 16)
            sp.dma_start(decay_c[:], decay.rearrange("(c p) -> p c", p=P),
                             allow_slow_non_contiguous=True).then_inc(consts_in, 16)
            sp.dma_start(first_c[:], first.rearrange("(c p) -> p c", p=P),
                             allow_slow_non_contiguous=True).then_inc(consts_in, 16)
            sp.dma_start(bg_b[:], bg.rearrange("(a e) -> a e", a=1).broadcast_to([P, E])).then_inc(consts_in, 16)
            load_chunk(sp, xin[1], x, plain(1), xin_in[1])
            sp.dma_start(wo[:], woT.rearrange("(c p) d -> p c d", p=P)).then_inc(gate_in, 16)
            sp.dma_start(wg[:], wgT.rearrange("(c p) e -> p c e", p=P)).then_inc(gate_in, 16)

            def load_raw(e):
                sp.dma_start(raw[:, 0:W1E].rearrange("p (c f) -> p c f", c=CC),
                             w1[e].rearrange("(c p) f -> p c f", p=P)).then_inc(raw_in, 16)
                sp.dma_start(raw[:, W1E:WE].rearrange("p (c d) -> p c d", c=FC),
                             w2[e].rearrange("(c p) d -> p c d", p=P)).then_inc(raw_in, 16)

            load_raw(0)
            sp.wait_ge(padded, 2)
            for n in range(2):
                sp.dma_start(xs[DUMMY + 64 + 32 * n:DUMMY + 96 + 32 * n, :], pad_rec[64 + 32 * n:96 + 32 * n, :]).then_inc(x1_out[n], 16)

            def step(i):
                c = i + 2
                if c.exists and (c - 2).exists:
                    sp.wait_ge(xT_done, (c - 2).upto(CC))
                    load_chunk(sp, xin[c.slot], x, c, xin_in[c.slot])
                c = i + 1
                if c.exists:
                    if (i - 1).exists:
                        sp.wait_ge(x1_done, (i - 1).upto(J + 1))
                    load_chunk(sp, xres[c.slot], x, c, xres_in[c.slot])
                c = i - 1
                if c.exists:
                    sp.wait_ge(x1_done, c.upto(J + 1))
                    store_chunk(sp, x1d, c, rec[c.slot][:, :, 0, 0:C].rearrange("p (b h) c -> p b h c", b=B), x1_out[c.slot])

            chunks(sp, step)
            phase_b_may_start(sp)
            sp.wait_ge(weights_ready, 1)
            load_raw(1)
            sp.dma_start(b1_b[:, 0:F], b1[0:1, :].broadcast_to([P, F])).then_inc(bias0_in, 16)
            sp.dma_start(b2_b[:, 0:C], b2[0:1, :].broadcast_to([P, C])).then_inc(bias0_in, 16)
            for e in range(E):
                row = sp.value_load(pad_row[0:1, e:e + 1], min_val=0, max_val=DUMMY - P)
                sp.dma_start(xs[bass.ds(row, P), :], pad_rec[:]).then_inc(pads_out, 16)
            for e in range(2, E):
                sp.wait_ge(weights_ready, e)
                load_raw(e)
            for n in range(2):
                load_chunk(sp, xx[n], x1d, plain(n), yy_in[n])
            for n in range(RING):
                sp.wait_ge(y_out[n], -((n - TILES) // RING) * 16)
            ys_t = ys.rearrange("(b t k) c -> b t (k c)", b=B, k=2)
            for n in range(2):
                load_chunk(sp, yy[n], ys_t, plain(n), yy_in[n])

            def out_step(i):
                sp.wait_ge(c_res, i.upto(J))
                store_chunk(sp, out, i, res[i.slot], res_out[i.slot])
                if not i.fixed or (i + 2).exists:
                    load_chunk(sp, xx[i.slot], x1d, i + 2, yy_in[i.slot])
                    load_chunk(sp, yy[i.slot], ys_t, i + 2, yy_in[i.slot])

            with sp.Fori(0, NCH // 2 - 1) as m:
                out_step(Step(m, 0, 2, NCH))
                out_step(Step(m, 1, 2, NCH))
            for n in range(NCH - 2, NCH):
                out_step(plain(n))
            for n in range(2):
                sp.wait_ge(res_out[n], NCH // 2 * 16 * B)

        @block.gpsimd
        def _(pool):
            pool.memset(ident[:], 0.0).then_inc(made, 1)
            pool.memset(before[:], 1.0).then_inc(made, 1)
            pool.memset(ones[:], 1.0).then_inc(made2, 1)
            pool.memset(half_neg[:], -0.5).then_inc(made2, 1)
            pool.memset(eps_b[:], EPS).then_inc(made2, 1)
            pool.wait_ge(made, 2)
            pool.affine_select(out=ident[:], in_=ident[:], compare_op=ALU.not_equal, fill=1.0, base=0,
                               pattern=[[-1, P]], channel_multiplier=1).then_inc(made2, 1)
            pool.affine_select(out=before[:], in_=before[:], compare_op=ALU.is_gt, fill=0.0, base=0,
                               pattern=[[1, P]], channel_multiplier=-1).then_inc(made2, 1)
            pool.iota(expert_no[:], [[1, E]], base=0, channel_multiplier=0,
                      allow_small_or_imprecise_dtypes=True).then_inc(made2, 1)
            pool.iota(region_no[:], [[REGION, E]], base=0, channel_multiplier=0,
                      allow_small_or_imprecise_dtypes=True).then_inc(made2, 1)
            for i in range(NCH):
                pool.iota(dest_all[:, i * 2 * J:(i + 1) * 2 * J], [[2 * T, B], [2 * P, TH], [1, 2]],
                          base=2 * TC * i, channel_multiplier=2).then_inc(made2, 1)
            pool.memset(xh[0][:, :, :, 0:1].bitcast(F32), 0.0).then_inc(xh_done, 1)
            pool.memset(xl[0][:, :, :, 0:1].bitcast(F32), 0.0).then_inc(xl_done, 1)
            pool.memset(pad_rec[:, 0:C], 0.0).then_inc(padded, 1)
            pool.memset(pad_rec[:, C:REC].bitcast(I32), NOWHERE).then_inc(padded, 1)

            def split(e):
                pool.dma_start(b1_b[:, e % 2 * F:(e % 2 + 1) * F], b1[e:e + 1, :].broadcast_to([P, F])).then_inc(bias_in, 16)
                pool.dma_start(b2_b[:, e % 2 * C:(e % 2 + 1) * C], b2[e:e + 1, :].broadcast_to([P, C])).then_inc(bias_in, 16)
                pool.wait_ge(raw_in, 32 * (e + 1))
                pool.tensor_scalar(wx[:, e % 2, 0, :], raw, 1.0, 0.0, ALU.mult, ALU.add).then_inc(hi_done, 1)
                pool.wait_ge(hi_done, e + 1)
                pool.wait_ge(bias_in, 32 * e)
                pool.tensor_tensor(wx[:, e % 2, 1, :], raw, wx[:, e % 2, 0, :].bitcast(F32),
                                   ALU.subtract).then_inc(weights_ready, 1)

            pool.wait_ge(padded, 2)
            for n in range(2):
                pool.dma_start(xs[DUMMY + 32 * n:DUMMY + 32 * n + 32, :], pad_rec[32 * n:32 * n + 32, :]).then_inc(rec_out[n], 16)
            pool.wait_ge(raw_in, 32)
            pool.tensor_scalar(wx[:, 0, 0, :], raw, 1.0, 0.0, ALU.mult, ALU.add).then_inc(hi_done, 1)
            pool.wait_ge(hi_done, 1)
            pool.tensor_tensor(wx[:, 0, 1, :], raw, wx[:, 0, 0, :].bitcast(F32), ALU.subtract).then_inc(weights_ready, 1)

            def step(i):
                if i.exists:
                    pool.wait_ge(b2_done, i.upto(1))
                    pool.wait_ge(v_out, i.upto(CC))
                    after(pool, p_done, (i - 1).upto(CC * B))
                    pool.tensor_tensor(b2v[:], B2[:], v[i.slot][:], ALU.mult).then_inc(b2v_done, 1)
                    pool.wait_ge(b1_done, i.upto(1))
                    after(pool, num_done, (i - 1).upto(2))
                    pool.tensor_tensor(bv[:], B1[:], v[i.slot][:], ALU.mult).then_inc(bv_done, 1)
                    pool.wait_ge(a1_done, i.upto(1))
                    pool.wait_ge(q_done, i.upto(CC * B))
                    after(pool, mixed_done, (i - 1).upto(1))
                    pool.tensor_tensor(den[:], A1[:], q_all[:, :, :, 0:TC], ALU.mult).then_inc(aq_done, 1)
                    pool.wait_ge(aq_done, i.upto(1))
                    pool.tensor_tensor(den[:], den[:], B1[:], ALU.add).then_inc(den_done, 1)
                c = i - 1
                if c.exists:
                    pool.wait_ge(mv_done, c.upto(J))
                    pool.tensor_tensor(var_e[:], mv[:, :, 1], eps_b[:], ALU.add).then_inc(vare_done, 1)
                    pool.wait_ge(vare_done, c.upto(1))
                    pool.tensor_tensor(rstd[:, c.slot, :], var_e[:], half_neg[:], ALU.pow).then_inc(rstd_done, 1)
                c = i - 2
                if c.exists:
                    pool.wait_ge(slots, c.upto(ROUTE2))
                    pool.wait_ge(rec2_done, c.upto(1))
                    pool.wait_ge(x1_done, c.upto(J + 1))
                    take_wait(pool)
                    for j in range(J):
                        for k in range(2):
                            n = 2 * j + k
                            pool.indirect_dma_start(
                                xs, bass.IndirectOffsetOnAxis(ap=slot_i[c.slot][:, n:n + 1], axis=0),
                                rec[c.slot][:, j, k, :], None, bounds_check=DUMMY - 1,
                                oob_is_err=False).then_inc(rec_out[c.slot], 16)

            chunks(pool, step)

            for n in range(2):
                pool.wait_ge(rec_out[n], NCH // 2 * REC_DMAS + BG)
                pool.wait_ge(x1_out[n], NCH // 2 * B * 16 + BG)
            pool.wait_ge(cnt_done, 1)
            pool.iota(tile_f[:], [[1, TILES], [0, E]], base=0, channel_multiplier=0,
                      allow_small_or_imprecise_dtypes=True).then_inc(made, 1)
            pool.iota(tile_row[:], [[P, TILES]], base=-DUMMY, channel_multiplier=0,
                      allow_small_or_imprecise_dtypes=True).then_inc(made, 1)
            phase_b_may_start(pool)
            split(1)
            end = [pool.value_load(ends[0:1, e:e + 1], min_val=0, max_val=TILES) for e in range(E - 2)]

            def scatter(t):
                for e in range(2, E):
                    with pool.If(end[e - 2] == t.number):
                        split(e)
                pool.wait_ge(y_done, t.upto(1))
                take_wait(pool)
                pool.indirect_dma_start(
                    ys, bass.IndirectOffsetOnAxis(ap=dest[t.slot][:], axis=0), y_sb[t.slot][:], None,
                    bounds_check=2 * TOKENS - 1, oob_is_err=False).then_inc(y_out[t.slot], 16)

            with pool.Fori(0, TILES // RING) as m:
                for n in range(RING):
                    scatter(Step(m, n, RING, TILES))
            for n in range(TILES // RING * RING, TILES):
                scatter(Step(None, n, RING, TILES))

            def norm_step(i):
                pool.wait_ge(c_mv, i.upto(J))
                pool.tensor_tensor(var_e[:], mv[:, :, 1], eps_b[:], ALU.add).then_inc(c_var, 1)
                pool.wait_ge(c_var, i.upto(1))
                pool.tensor_tensor(rstd[:, i.slot, :], var_e[:], half_neg[:], ALU.pow).then_inc(c_rstd, 1)

            with pool.Fori(0, NCH // 2) as m:
                norm_step(Step(m, 0, 2, NCH))
                norm_step(Step(m, 1, 2, NCH))

        @block.tensor
        def _(pe):
            pe.wait_ge(made2, 7 + NCH)

            def transpose_x(c):
                pe.wait_ge(xin_in[c.slot], c.turn(16 * B, 16 * B))
                after(pe, xl_done, (c - 1).upto(CC + 1))
                for cc in range(CC):
                    for j in range(J):
                        ins = pe.transpose(xT_ps[:, cc, j * P:(j + 1) * P],
                                           xin[c.slot][:, j // TH, j % TH, cc * P:(cc + 1) * P], ident[:])
                    ins.then_inc(xT_done, 1)

            def project(c, mat, oc, out_ps):
                terms = [(cc, now, a, b) for cc in range(CC) for now in range(2)
                         for a, b in ((0, xh), (0, xl), (1, xh))]
                for n, (cc, now, part, xpart) in enumerate(terms):
                    ins = pe.matmul(out_ps.rearrange("p (b t) -> p b t", b=B), wq[:, mat, now, part, cc, oc * P:(oc + 1) * P],
                                    xpart[c.slot][:, cc, :, now:now + TC],
                                    start=n == 0, stop=n == len(terms) - 1)
                return ins

            def out_project(c, b):
                for h in range(TH):
                    for cc in range(CC):
                        ins = pe.matmul(wo_ps[:, h, :], mixed[:, cc, b, h * P:(h + 1) * P], wo[:, cc, :],
                                        start=cc == 0, stop=cc == CC - 1)
                ins.then_inc(wo_done, 1)

            def step(i):
                c = i + 1
                if c.exists:
                    if c.fixed and c.number == 0:
                        pe.wait_ge(w_lo, 2)
                    pe.wait_ge(xl_done, c.upto(CC + 1))
                    for mat in range(2):
                        for oc in range(CC):
                            if mat == 0:
                                after(pe, x1T_out, (i - 2).upto(CC, oc + 1))
                            else:
                                pe.wait_ge(v_out, c.upto(CC, oc + 1))
                            project(c, mat, oc, vr_ps[oc][:]).then_inc(vr_done, 1)
                c = i - 1
                if c.exists:
                    if c.fixed and c.number == 0:
                        pe.wait_ge(gate_in, 32)
                    pe.wait_ge(mixed_done, c.upto(1))
                    after(pe, res_done, (c - 1).upto(2))
                    out_project(c, 0)
                c = i + 1
                if c.exists:
                    if c.fixed and c.number == 0:
                        pe.wait_ge(w_lo, 3)
                    after(pe, d2_done, i.upto(1))
                    for oc in range(CC):
                        project(c, 2, oc, k_ps[:, oc, :]).then_inc(k_done, 1)
                c = i - 1
                if c.exists:
                    pe.wait_ge(res_done, c.upto(2, 1))
                    out_project(c, 1)
                c = i - 2
                if c.exists:
                    pe.wait_ge(route, c.upto(ROUTE1))
                    pe.matmul(rank_ps, before[:], picks[:], start=True, stop=False)
                    pe.matmul(rank_ps, ones[:], seen[:, 0:J, :], start=False, stop=True).then_inc(rank_done, 1)
                c = i + 2
                if c.exists:
                    transpose_x(c)
                c = i - 1
                if c.exists:
                    pe.wait_ge(x1_done, c.upto(J + 1, J))
                    for cc in range(CC):
                        if (i + 1).exists:
                            pe.wait_ge(gate_out, (i + 1).upto(CC, cc + 1))
                        else:
                            pe.wait_ge(x1T_out, (c - 1).upto(CC, cc + 1))
                        for j in range(J):
                            ins = pe.transpose(vr_ps[cc][:, j * P:(j + 1) * P],
                                               rec[c.slot][:, j, 0, cc * P:(cc + 1) * P], ident[:])
                        ins.then_inc(x1T_done, 1)
                    pe.wait_ge(x1T_out, c.upto(CC))
                    after(pe, route, (c - 1).upto(ROUTE1, 1))
                    for j in range(J):
                        for cc in range(CC):
                            ins = pe.matmul(lg_ps[:, j, :], x1T[:, cc, j * P:(j + 1) * P], wg[:, cc, :],
                                            start=cc == 0, stop=cc == CC - 1)
                    ins.then_inc(lg_done, 1)

            chunks(pe, step)
            last = Step(None, NCH - 1, 2, NCH)
            pe.wait_ge(route, last.upto(ROUTE1))
            pe.wait_ge(slots, last.upto(ROUTE2, 3))
            pe.matmul(cnt_ps, ones[:], seen[:, J, :], start=True, stop=True).then_inc(cnt_done, 1)

            phase_b_may_start(pe)

            def product1(t, s):
                for n in range(2):
                    terms = [(cc, a, b) for cc in range(CC) for a, b in ((xTh, 0), (xTh, 1), (xTl, 0))]
                    for k, (cc, xpart, part) in enumerate(terms):
                        off = cc * F + n * 512
                        ins = pe.matmul(h_ps[t.slot % 2][:, n * 512:(n + 1) * 512], xpart[t.slot % 2][:, cc, :],
                                        wx[:, s, part, off:off + 512], start=k == 0, stop=k == len(terms) - 1)
                    ins.then_inc(mm1_done, 1)

            def product2(t, s):
                terms = [(fc, a, b) for fc in range(FC) for a, b in ((aTh, 0), (aTh, 1), (aTl, 0))]
                for k, (fc, apart, part) in enumerate(terms):
                    off = W1E + fc * C
                    ins = pe.matmul(y_ps, apart[t.slot % 2][:, fc, :], wx[:, s, part, off:off + C],
                                    start=k == 0, stop=k == len(terms) - 1)
                ins.then_inc(mm2_done, 1)

            def tile(t):
                u = t + 1
                if u.exists:
                    expert = pe.value_load(ex_t[0:1, bass.ds(u.number, 1)], min_val=0, max_val=E - 1)
                    slot = expert % 2
                    pe.wait_ge(txl_done, u.upto(1))
                    after(pe, hid_done, (u - 2).upto(2))
                    pe.wait_ge(weights_ready, expert + 1)
                    with pe.If(slot == 0):
                        product1(u, 0)
                    with pe.Else():
                        product1(u, 1)
                u = t + 2
                if u.exists:
                    pe.wait_ge(rec_in[u.slot % 4], u.turn4(16, 16))
                    after(pe, txl_done, (u - 1).upto(1))
                    for cc in range(CC):
                        ins = pe.transpose(xT2_ps[:, cc, :], recs[u.slot % 4][:, cc * P:(cc + 1) * P], ident[:])
                    ins.then_inc(tx_done, 1)
                u = t - 1
                if u.exists:
                    slot = pe.value_load(par_t[0:1, bass.ds(u.number, 1)], min_val=0, max_val=1)
                    pe.wait_ge(aTl_done, u.upto(2))
                    after(pe, y_done, (u - 1).upto(1))
                    with pe.If(slot == 0):
                        product2(u, 0)
                    with pe.Else():
                        product2(u, 1)
                if t.exists:
                    pe.wait_ge(act_done, t.upto(1))
                    for fc in range(FC):
                        ins = pe.transpose(aT_ps[:, fc, :], hid[t.slot % 2][:, fc * P:(fc + 1) * P], ident[:])
                        if fc % (FC // 2) == FC // 2 - 1:
                            ins.then_inc(aT_done, 1)

            tiles(pe, tile)

        @block.scalar
        def _(act):
            act.wait_ge(consts_in, 6 * 16)
            act.activation(decay_c[:], decay_c[:], ACT.Exp).then_inc(setup_act, 1)
            for n in range(3):
                act.wait_ge(scaled, 4 * (n + 1))
                act.activation(wq[:, n, :, 0, :, :], wscaled[n][:].rearrange("p c b t -> p (c b t)").rearrange(
                    "p (a c d) -> p a c d", a=2, c=CC), ACT.Copy).then_inc(w_hi, 1)

            def step(i):
                c = i + 1
                if c.exists:
                    pe_n = c.upto(2 * CC, 1)
                    act.wait_ge(vr_done, pe_n)
                    after(act, bv_done, (c - 2).upto(1))
                    act.activation(v[c.slot][:, 0], vr_ps[0][:].rearrange("p (b t) -> p b t", b=B), ACT.Copy).then_inc(v_out, 1)
                if i.exists:
                    act.wait_ge(s_done, i.upto(CC))
                    after(act, num_done, (i - 1).upto(2, 1))
                    after(act, den_done, (i - 1).upto(1))
                    act.activation(A1[:], s_buf[:], ACT.Relu).then_inc(relu_done, 1)
                    act.activation(B1[:], s_buf[:], ACT.Relu, scale=-1.0).then_inc(relu_done, 1)
                    act.wait_ge(d3_done, i.upto(1))
                    for cc in range(CC):
                        act.activation(A2[:, cc], A2[:, cc], ACT.Exp, bias=decay_c[:, cc:cc + 1]).then_inc(a2_done, 1)
                    act.wait_ge(d2_done, i.upto(1))
                    act.activation(B2[:], B2[:], ACT.Exp).then_inc(b2_done, 1)
                c = i + 1
                if c.exists:
                    act.wait_ge(vr_done, c.upto(2 * CC, 2))
                    act.activation(v[c.slot][:, 1], vr_ps[1][:].rearrange("p (b t) -> p b t", b=B), ACT.Copy).then_inc(v_out, 1)
                if i.exists:
                    act.wait_ge(relu_done, i.upto(2))
                    act.activation(A1[:], A1[:], ACT.Exp, scale=-1.0).then_inc(a1_done, 1)
                    act.activation(B1[:], B1[:], ACT.Exp, scale=-1.0).then_inc(b1_done, 1)
                c = i + 1
                if c.exists:
                    after(act, mixed_done, (c - 2).upto(1))
                    for cc in range(CC):
                        act.wait_ge(vr_done, c.upto(2 * CC, CC + cc + 1))
                        act.activation(gate[c.slot][:, cc], vr_ps[cc][:].rearrange("p (b t) -> p b t", b=B),
                                       ACT.Sigmoid).then_inc(gate_out, 1)
                c = i + 2
                if c.exists:
                    act.wait_ge(xT_done, c.upto(CC))
                    after(act, k_done, (c - 2).upto(CC))
                    if not c.fixed or c.number > 0:
                        act.wait_ge(xh_done, (c - 1).upto(CC + 1))
                        act.activation(xh[c.slot][:, :, :, 0:1], xh[1 - c.slot][:, :, :, TC:TC + 1].bitcast(F32),
                                       ACT.Copy).then_inc(xh_done, 1)
                    for cc in range(CC):
                        act.activation(xh[c.slot][:, cc, :, 1:TC + 1], xT_ps[:, cc, :].rearrange("p (b t) -> p b t", b=B),
                                       ACT.Copy).then_inc(xh_done, 1)
                if i.exists:
                    act.wait_ge(den_done, i.upto(1))
                    after(act, mixed_done, (i - 1).upto(1))
                    act.activation(r0[:], den[:], ACT.Ln).then_inc(ln_done, 1)
                    act.wait_ge(ln_done, i.upto(1))
                    act.activation(r0[:], r0[:], ACT.Exp, scale=-1.0).then_inc(r0_done, 1)
                c = i - 1
                if c.exists:
                    act.wait_ge(x1_done, c.upto(J + 1, J))
                    act.activation(rec[c.slot][:, :, 1, 0:C], rec[c.slot][:, :, 0, 0:C], ACT.Copy).then_inc(rec2_done, 1)
                    after(act, lg_done, (c - 1).upto(1))
                    for cc in range(CC):
                        act.wait_ge(x1T_done, c.upto(CC, cc + 1))
                        act.activation(x1T[:, cc, :], vr_ps[cc][:], ACT.Copy).then_inc(x1T_out, 1)

            chunks(act, step)

            phase_b_may_start(act)
            act.wait_ge(pads_out, 16 * E)

            def load_records(u):
                row = act.value_load(row_t[0:1, bass.ds(u.number, 1)], min_val=0, max_val=DUMMY)
                act.dma_start(recs[u.slot % 4][:], xs[bass.ds(row, P), :]).then_inc(rec_in[u.slot % 4], 16)

            load_records(Step(None, 0, RING, TILES))
            act.wait_ge(score_done, 1)
            act.activation(score_t[:, :, 0:1], score_t[:, :, 0:1], ACT.Exp).then_inc(exp_done, 1)

            def activate(u, func):
                if u.exists:
                    act.wait_ge(hid_done, u.upto(2))
                    act.activation(hid[u.slot % 2][:], hid[u.slot % 2][:], func).then_inc(act_done, 1)
                w = u - 1
                if w.exists:
                    after(act, mm2_done, (w - 2).upto(1))
                    for n in range(2):
                        act.wait_ge(aT_done, w.upto(2, n + 1))
                        act.activation(aTh[w.slot % 2][:, n * FC // 2:(n + 1) * FC // 2, :],
                                       aT_ps[:, n * FC // 2:(n + 1) * FC // 2, :], ACT.Copy).then_inc(aTh_done, 1)

            def tile(t):
                u = t + 3
                if u.exists:
                    after(act, txl_done, (u - 4).upto(1))
                    load_records(u)
                u = t + 1
                if u.exists:
                    expert = act.value_load(ex_t[0:1, bass.ds(u.number, 1)], min_val=0, max_val=E - 1)
                    with act.If(expert % 2 == 0):
                        activate(u, ACT.Gelu)
                    with act.Else():
                        activate(u, ACT.Silu)
                else:
                    activate(u, None)

            tiles(act, tile)

        @block.vector
        def _(dve):
            dve.wait_ge(consts_in, 6 * 16)
            dve.tensor_scalar(unmix_c[:], mix_c[:], -1.0, 1.0, ALU.mult, ALU.add).then_inc(setup_dve, 1)
            dve.wait_ge(setup_dve, 1)
            dve.wait_ge(weights_in, 3 * 16)
            for n in range(3):
                src = wraw[n][:].rearrange("p c b t -> p (c b t)")
                dst = wscaled[n][:].rearrange("p c b t -> p (c b t)").rearrange("p (a c d) -> p a c d", a=2, c=CC)
                for a, factor in ((0, unmix_c), (1, mix_c)):
                    for cc in range(CC):
                        dve.tensor_scalar(dst[:, a, cc, :], src[:, cc * C:(cc + 1) * C], factor[:, n, cc:cc + 1], None,
                                          ALU.mult).then_inc(scaled, 1)
                dve.wait_ge(scaled, 4 * (n + 1))
                dve.wait_ge(w_hi, n + 1)
                dve.tensor_tensor(wq[:, n, :, 1, :, :], dst, wq[:, n, :, 0, :, :].bitcast(F32), ALU.subtract).then_inc(w_lo, 1)
            dve.wait_ge(setup_act, 1)
            dve.tensor_scalar(decay_c[:], decay_c[:], -1.0, None, ALU.mult).then_inc(setup_dve, 1)
            dve.wait_ge(setup_dve, 2)
            for cc in range(CC):
                dve.tensor_copy(w_row[:, cc, :], decay_c[:, cc:cc + 1].broadcast_to([P, TC])).then_inc(setup_dve, 1)
            dve.memset(seen[:, J, :], 0.0).then_inc(setup_dve, 1)
            dve.wait_ge(setup_dve, 3 + CC)
            dve.wait_ge(made2, 7 + NCH)

            def step(i):
                c = i + 1
                if c.exists:
                    dve.wait_ge(xh_done, c.upto(CC + 1))
                    after(dve, k_done, (c - 2).upto(CC))
                    if not c.fixed or c.number > 0:
                        dve.wait_ge(xl_done, (c - 1).upto(CC + 1))
                        dve.tensor_copy(xl[c.slot][:, :, :, 0:1],
                                        xl[1 - c.slot][:, :, :, TC:TC + 1].bitcast(F32)).then_inc(xl_done, 1)
                    for cc in range(CC):
                        dve.tensor_tensor(xl[c.slot][:, cc, :, 1:TC + 1], xT_ps[:, cc, :].rearrange("p (b t) -> p b t", b=B),
                                          xh[c.slot][:, cc, :, 1:TC + 1].bitcast(F32), ALU.subtract).then_inc(xl_done, 1)
                if i.exists:
                    if i.fixed and i.number == 0:
                        dve.memset(o_all[:, :, :, 0:1], LOWEST).then_inc(o_carry, 1)
                    else:
                        dve.wait_ge(o_done, (i - 1).upto(CC * B))
                        dve.tensor_copy(o_all[:, :, :, 0:1], o_all[:, :, :, TC:TC + 1]).then_inc(o_carry, 1)
                    dve.wait_ge(o_carry, i.upto(1))
                    dve.wait_ge(k_done, i.upto(CC))
                    for cc in range(CC):
                        for b in range(B):
                            dve.tensor_tensor_scan(o_all[:, cc, b, 1:TC + 1], w_row[:, cc, :],
                                                   k_ps[:, cc, b * TC:(b + 1) * TC], o_all[:, cc, b, 0:1],
                                                   ALU.add, ALU.max).then_inc(o_done, 1)
                    dve.wait_ge(o_done, i.upto(CC * B))
                    after(dve, relu_done, (i - 1).upto(2))
                    for cc in range(CC):
                        dve.scalar_tensor_tensor(out=s_buf[:, cc], in0=k_ps[:, cc, :].rearrange("p (b t) -> p b t", b=B),
                                                 scalar=first_c[:, cc:cc + 1], in1=o_all[:, cc, :, 0:TC],
                                                 op0=ALU.add, op1=ALU.subtract).then_inc(s_done, 1)
                    dve.tensor_tensor(A2[:], o_all[:, :, :, 0:TC], o_all[:, :, :, 1:TC + 1], ALU.subtract).then_inc(d3_done, 1)
                    after(dve, b2v_done, (i - 1).upto(1))
                    dve.tensor_tensor(B2[:], k_ps[:].rearrange("p c (b t) -> p c b t", b=B), o_all[:, :, :, 1:TC + 1],
                                      ALU.subtract).then_inc(d2_done, 1)
                c = i - 1
                if c.exists:
                    dve.wait_ge(r0_done, c.upto(1))
                    after(dve, wo_done, (c - 1).upto(2))
                    dve.tensor_tensor(newton[:], den[:], r0[:], ALU.mult).then_inc(div_done, 1)
                    dve.wait_ge(div_done, c.upto(3, 1))
                    dve.scalar_tensor_tensor(out=newton[:], in0=newton[:], scalar=2.0, in1=r0[:],
                                             op0=ALU.subtract, op1=ALU.mult).then_inc(div_done, 1)
                    dve.wait_ge(div_done, c.upto(3, 2))
                    dve.wait_ge(num_done, c.upto(2))
                    dve.tensor_tensor(newton[:], num[:], newton[:], ALU.mult).then_inc(div_done, 1)
                    dve.wait_ge(div_done, c.upto(3))
                    dve.wait_ge(gate_out, c.upto(CC))
                    dve.scalar_tensor_tensor(out=mixed[:], in0=newton[:], scalar=-1.0, in1=gate[c.slot][:],
                                             op0=ALU.mult, op1=ALU.mult).then_inc(mixed_done, 1)
                c = i - 2
                if c.exists:
                    dve.wait_ge(lg_done, c.upto(1))
                    dve.tensor_tensor(lg[:], lg_ps, bg_b[:].unsqueeze(1).broadcast_to([P, J, E]), ALU.add).then_inc(route, 1)
                    dve.wait_ge(route, c.upto(ROUTE1, 1))
                    take_wait(dve)
                    for j in range(J):
                        dve.max(m8[:, j, :], lg[:, j, :]).then_inc(route, 1)
                    dve.wait_ge(route, c.upto(ROUTE1, 1 + J))
                    take_wait(dve)
                    for j in range(J):
                        dve.max_index(i8[:, j, :], m8[:, j, :], lg[:, j, :]).then_inc(route, 1)
                    dve.tensor_copy(top2[:].rearrange("p i j k -> p (i j k)")[:, bass.ds(c.number * (2 * J), 2 * J)].rearrange(
                        "p (j k) -> p j k", j=J), m8[:, :, 0:2]).then_inc(slots, 1)
                    dve.wait_ge(route, c.upto(ROUTE1, 1 + 2 * J))
                    dve.tensor_copy(idxf[:], i8[:, :, 0:2]).then_inc(route, 1)
                    dve.wait_ge(route, c.upto(ROUTE1, 2 + 2 * J))
                    dve.tensor_tensor(hot[:], expert_no[:].unsqueeze(1).unsqueeze(1).broadcast_to([P, J, 2, E]),
                                      idxf[:].unsqueeze(3).broadcast_to([P, J, 2, E]), ALU.is_equal).then_inc(route, 1)
                    dve.wait_ge(route, c.upto(ROUTE1, 3 + 2 * J))
                    dve.tensor_copy(seen[:, 0, :], seen[:, J, :]).then_inc(route, 1)
                    dve.tensor_tensor(picks[:], hot[:, :, 0, :], hot[:, :, 1, :], ALU.add).then_inc(slots, 1)
                    for j in range(J):
                        dve.wait_ge(route, c.upto(ROUTE1, 4 + 2 * J + j))
                        if j == 0:
                            dve.wait_ge(slots, c.upto(ROUTE2, 2))
                        dve.tensor_tensor(seen[:, j + 1, :], seen[:, j, :], picks[:, j, :], ALU.add).then_inc(route, 1)
                if i.exists:
                    dve.wait_ge(a2_done, i.upto(CC))
                    dve.wait_ge(b2_done, i.upto(1))
                    if i.fixed and i.number == 0:
                        dve.memset(q_all[:, :, :, 0:1], 0.0).then_inc(qp_carry, 1)
                        dve.memset(p_all[:, :, :, 0:1], 0.0).then_inc(qp_carry, 1)
                    else:
                        dve.wait_ge(aq_done, (i - 1).upto(1))
                        dve.tensor_copy(q_all[:, :, :, 0:1], q_all[:, :, :, TC:TC + 1]).then_inc(qp_carry, 1)
                        dve.tensor_copy(p_all[:, :, :, 0:1], p_all[:, :, :, TC:TC + 1]).then_inc(qp_carry, 1)
                    dve.wait_ge(qp_carry, i.upto(2))
                    for all_, add, done in ((q_all, B2, q_done), (p_all, b2v, p_done)):
                        if all_ is p_all:
                            dve.wait_ge(b2v_done, i.upto(1))
                        for cc in range(CC):
                            for b in range(B):
                                dve.tensor_tensor_scan(all_[:, cc, b, 1:TC + 1], A2[:, cc, b, :], add[:, cc, b, :],
                                                       all_[:, cc, b, 0:1], ALU.mult, ALU.add).then_inc(done, 1)
                c = i - 1
                if c.exists:
                    add_residual(c, 0)
                if i.exists:
                    dve.wait_ge(a1_done, i.upto(1))
                    dve.wait_ge(p_done, i.upto(CC * B))
                    dve.tensor_tensor(num[:], A1[:], p_all[:, :, :, 0:TC], ALU.mult).then_inc(num_done, 1)
                    dve.wait_ge(num_done, i.upto(2, 1))
                    dve.wait_ge(bv_done, i.upto(1))
                    dve.tensor_tensor(num[:], num[:], bv[:], ALU.add).then_inc(num_done, 1)
                c = i - 1
                if c.exists:
                    add_residual(c, 1)
                    dve.wait_ge(res_done, c.upto(2))
                    for j in range(J):
                        dve.bn_stats(stats[:, j, :], xres[c.slot][:, j // TH, j % TH, :]).then_inc(bn_done, 1)
                    dve.wait_ge(bn_done, c.upto(J))
                    take_wait(dve)
                    for j in range(J):
                        dve.bn_aggr(mv[:, j, :], stats[:, j, :]).then_inc(mv_done, 1)
                c = i - 2
                if c.exists:
                    dve.wait_ge(rank_done, c.upto(1))
                    dve.tensor_tensor(rank[:], rank_ps, region_no[:].unsqueeze(1).broadcast_to([P, J, E]), ALU.add).then_inc(slots, 1)
                    dve.wait_ge(slots, c.upto(ROUTE2, 3))
                    dve.tensor_tensor(spread[:], hot[:], rank[:].unsqueeze(2).broadcast_to([P, J, 2, E]), ALU.mult).then_inc(slots, 1)
                    dve.wait_ge(slots, c.upto(ROUTE2, 4))
                    dve.tensor_reduce(slot_f[:], spread[:], AX.X, ALU.add).then_inc(slots, 1)
                    dve.wait_ge(slots, c.upto(ROUTE2, 5))
                    dve.tensor_copy(slot_i[c.slot][:].rearrange("p (j k) -> p j k", j=J), slot_f[:]).then_inc(slots, 1)
                c = i - 1
                if c.exists:
                    dve.wait_ge(rstd_done, c.upto(1))
                    dve.wait_ge(rec_out[c.slot], c.turn(REC_DMAS, BG))
                    dve.wait_ge(x1_out[c.slot], c.turn(B * 16, BG))
                    for j in range(J):
                        dve.tensor_scalar(rec[c.slot][:, j, 0, 0:C], xres[c.slot][:, j // TH, j % TH, :], mv[:, j, 0:1], rstd[:, c.slot, j:j + 1],
                                          ALU.subtract, ALU.mult).then_inc(x1_done, 1)
                    dve.tensor_copy(rec[c.slot][:, :, :, C:REC].bitcast(I32),
                                    dest_all[:, bass.ds(c.number * (2 * J), 2 * J)].rearrange("p (j k a) -> p j k a", j=J, a=1)
                                    ).then_inc(x1_done, 1)

            def add_residual(c, b):
                dve.wait_ge(wo_done, c.upto(2, b + 1))
                if b == 0:
                    dve.wait_ge(xres_in[c.slot], c.turn(16 * B, 16 * B))
                dve.tensor_tensor(xres[c.slot][:, b], wo_ps[:], xres[c.slot][:, b], ALU.add).then_inc(res_done, 1)

            chunks(dve, step)

            step_no = [0]

            def link(ins):
                step_no[0] += 1
                ins.then_inc(table, 1)
                dve.wait_ge(table, step_no[0])

            dve.wait_ge(cnt_done, 1)
            dve.wait_ge(made, 4)
            link(dve.tensor_copy(cnt_f[:], cnt_ps[0:1, :]))
            link(dve.tensor_tensor(pad_row[:], cnt_f[:], region_no[0:1, :], ALU.add))
            link(dve.tensor_scalar(cnt_i[:], cnt_f[:], float(P - 1), None, ALU.add))
            link(dve.tensor_scalar(tiles_i[:], cnt_i[:], 7, None, ALU.logical_shift_right))
            link(dve.tensor_copy(tiles_f[:], tiles_i[:]))
            link(dve.tensor_tensor_scan(ends_f[:], ones[0:1, 0:E], tiles_f[:], 0.0, ALU.mult, ALU.add))
            link(dve.tensor_tensor(starts_f[:], ends_f[:], tiles_f[:], ALU.subtract))
            link(dve.tensor_copy(ends[:], ends_f[:]))
            link(dve.scalar_tensor_tensor(out=rowbase[:], in0=starts_f[:], scalar=-float(P), in1=region_no[0:1, :],
                                          op0=ALU.mult, op1=ALU.add))
            over = lambda a: a[:].unsqueeze(1).broadcast_to([1, TILES, E])
            link(dve.tensor_tensor(past_s[:], tile_f[:], over(starts_f), ALU.is_ge))
            link(dve.tensor_tensor(past_e[:], tile_f[:], over(ends_f), ALU.is_ge))
            link(dve.tensor_tensor(past_s[:], past_s[:], past_e[:], ALU.subtract))
            link(dve.tensor_tensor(past_s[:], past_s[:], over(rowbase), ALU.mult))
            link(dve.tensor_reduce(row_f[:], past_s[:], AX.X, ALU.add))
            link(dve.tensor_reduce(ex_f[:], past_e[:], AX.X, ALU.add))
            link(dve.tensor_scalar(real_f[:], ex_f[:], float(E), None, ALU.is_lt))
            link(dve.tensor_tensor(real_f[:], real_f[:], tile_row[:], ALU.mult))
            link(dve.scalar_tensor_tensor(out=row_t[:], in0=row_f[:], scalar=float(DUMMY), in1=real_f[:],
                                          op0=ALU.add, op1=ALU.add))
            link(dve.tensor_scalar(ex_t[:], ex_f[:], float(E - 1), None, ALU.min))
            link(dve.tensor_scalar(par_t[:], ex_t[:], 1, None, ALU.bitwise_and))
            dve.tensor_tensor(score_t[:, :, 0:1], top2[:].rearrange("p i j k -> p (i j) k")[:, :, 1:2],
                              top2[:].rearrange("p i j k -> p (i j) k")[:, :, 0:1], ALU.subtract).then_inc(score_done, 1)
            dve.tensor_copy(cnt_f[:], cnt_f[:]).then_inc(table_done, 1)
            phase_b_may_start(dve)
            dve.wait_ge(bias0_in, 32)

            def tile(t):
                u = t + 2
                if u.exists:
                    dve.wait_ge(tx_done, u.upto(1))
                    after(dve, mm1_done, (u - 2).upto(2))
                    dve.tensor_copy(xTh[u.slot % 2][:], xT2_ps).then_inc(txh_done, 1)
                    after(dve, y_out[u.slot], u.turn(16))
                    dve.tensor_copy(dest[u.slot][:], recs[u.slot % 4][:, C:REC].bitcast(I32)).then_inc(table, 1)
                    dve.wait_ge(txh_done, u.upto(1))
                    dve.tensor_tensor(xTl[u.slot % 2][:], xT2_ps, xTh[u.slot % 2][:].bitcast(F32),
                                      ALU.subtract).then_inc(txl_done, 1)
                u = t + 1
                if u.exists:
                    slot = dve.value_load(par_t[0:1, bass.ds(u.number, 1)], min_val=0, max_val=1)
                    after(dve, aT_done, (u - 2).upto(2))
                    for n in range(2):
                        dve.wait_ge(mm1_done, u.upto(2, n + 1))
                        dve.tensor_tensor(hid[u.slot % 2][:, n * 512:(n + 1) * 512], h_ps[u.slot % 2][:, n * 512:(n + 1) * 512],
                                          b1_b[:, bass.ds(slot * F + n * 512, 512)], ALU.add).then_inc(hid_done, 1)
                u = t - 1
                if u.exists:
                    slot = dve.value_load(par_t[0:1, bass.ds(u.number, 1)], min_val=0, max_val=1)
                    dve.wait_ge(mm2_done, u.upto(1))
                    after(dve, y_out[u.slot], u.turn(16))
                    dve.tensor_tensor(y_sb[u.slot][:], y_ps, b2_b[:, bass.ds(slot * C, C)],
                                      ALU.add).then_inc(y_done, 1)
                if t.exists:
                    for n in range(2):
                        dve.wait_ge(aTh_done, t.upto(2, n + 1))
                        dve.tensor_tensor(aTl[t.slot % 2][:, n * FC // 2:(n + 1) * FC // 2, :],
                                          aT_ps[:, n * FC // 2:(n + 1) * FC // 2, :],
                                          aTh[t.slot % 2][:, n * FC // 2:(n + 1) * FC // 2, :].bitcast(F32),
                                          ALU.subtract).then_inc(aTl_done, 1)

            tiles(dve, tile)

            dve.wait_ge(exp_done, 1)
            base = step_no[0] + TILES
            dve.tensor_scalar(score[:, :, 1:2], score_t[:, :, 0:1], 1.0, None, ALU.add).then_inc(table, 1)
            dve.wait_ge(table, base + 1)
            dve.reciprocal(score[:, :, 0:1], score[:, :, 1:2]).then_inc(table, 1)
            dve.wait_ge(table, base + 2)
            dve.tensor_tensor(score[:, :, 1:2], score_t[:, :, 0:1], score[:, :, 0:1], ALU.mult).then_inc(table, 1)
            dve.wait_ge(table, base + 3)

            def out_step(i):
                dve.wait_ge(yy_in[i.slot], i.turn(32 * B, 32 * B))
                after(dve, c_res, (i - 1).upto(J))
                flat = score[:].rearrange("p n k -> p (n k)")
                for k in range(2):
                    for j in range(J):
                        b, h = j // TH, j % TH
                        dve.scalar_tensor_tensor(
                            out=zz[:, j, :], in0=yy[i.slot][:, b, h, k * C:(k + 1) * C],
                            scalar=flat[:, bass.ds(i.number * (2 * J) + (2 * j + k), 1)],
                            in1=xx[i.slot][:, b, h, :] if k == 0 else zz[:, j, :], op0=ALU.mult, op1=ALU.add).then_inc(c_sum, 1)
                    dve.wait_ge(c_sum, i.upto(2 * J, (k + 1) * J))
                for j in range(J):
                    dve.bn_stats(stats[:, j, :], zz[:, j, :]).then_inc(c_bn, 1)
                dve.wait_ge(c_bn, i.upto(J))
                take_wait(dve)
                for j in range(J):
                    dve.bn_aggr(mv[:, j, :], stats[:, j, :]).then_inc(c_mv, 1)
                dve.wait_ge(c_rstd, i.upto(1))
                if (i - 2).exists:
                    dve.wait_ge(res_out[i.slot], i.turn(16 * B))
                for j in range(J):
                    dve.tensor_scalar(res[i.slot][:, j // TH, j % TH, :], zz[:, j, :], mv[:, j, 0:1],
                                      rstd[:, i.slot, j:j + 1], ALU.subtract, ALU.mult).then_inc(c_res, 1)

            for n in range(2):
                out_step(Step(None, n, 2, NCH))
            with dve.Fori(1, NCH // 2) as m:
                out_step(Step(m, 0, 2, NCH))
                out_step(Step(m, 1, 2, NCH))


INPUTS = ["L0_attn_x", "L0_attn_time_decay", "L0_attn_time_first", "L0_attn_time_mix_k", "L0_attn_time_mix_v",
          "L0_attn_time_mix_r", "L0_attn_Wk", "L0_attn_Wv", "L0_attn_Wr", "L0_attn_Wo", "L0_ffn_W1", "L0_ffn_b1",
          "L0_ffn_W2", "L0_ffn_b2", "L0_ffn_Wg", "L0_ffn_bg"]
TRANSPOSED = {"L0_attn_Wk", "L0_attn_Wv", "L0_attn_Wr", "L0_attn_Wo"}


def kernel(**inputs):
    import concourse.bacc as bacc
    from concourse.bass_utils import run_bass_kernel_spmd

    nc = bacc.Bacc("TRN2", target_bir_lowering=False, num_devices=1)
    arrays, aps = {}, []
    for name in INPUTS:
        a = np.asarray(inputs[name])
        a = np.ascontiguousarray(a.T if name in TRANSPOSED else a)
        arrays[f"in_{name}"] = a
        aps.append(nc.dram_tensor(f"in_{name}", a.shape, mybir.dt.from_np(a.dtype), kind="ExternalInput").ap())
    shape = arrays["in_L0_attn_x"].shape
    aps.append(nc.dram_tensor("out", shape, F32, kind="ExternalOutput").ap())
    build(nc, *aps)
    return run_bass_kernel_spmd(nc, [arrays], core_ids=[0]).results[0]["out"]
```

```python
from contextlib import ExitStack

import numpy as np

import concourse.bass as bass
from concourse import mybir

ALU = mybir.AluOpType
ACT = mybir.ActivationFunctionType
AX = mybir.AxisListType
F32 = mybir.dt.float32
F32R = mybir.dt.float32r
I32 = mybir.dt.int32
U32 = mybir.dt.uint32

P = 128


class Step:

    def __init__(self, m, off, every, count):
        self.m, self.off, self.every, self.count = m, off, every, count

    def __add__(self, k):
        return Step(self.m, self.off + k, self.every, self.count)

    def __sub__(self, k):
        return self + -k

    @property
    def fixed(self):
        return self.m is None

    @property
    def number(self):
        return self.off if self.fixed else self.m * self.every + self.off

    @property
    def exists(self):
        return not self.fixed or 0 <= self.off < self.count

    @property
    def slot(self):
        return self.off % self.every

    def turn(self, n=1, more=0):
        if self.fixed:
            return self.off // self.every * n + more
        return self.m * n + (self.off // self.every * n + more)

    def upto(self, each, n=None):
        n = each if n is None else n
        if self.fixed:
            return self.off * each + n
        return self.m * (self.every * each) + (self.off * each + n)


def build(nc, x, decay, first, mix_k, mix_v, mix_r, wkT, wvT, wrT, woT, w1, b1, w2, b2, wgT, bg, out):
    B, T, C = x.shape
    E, _, F = w1.shape
    CC = C // P
    TC = 256
    NCH = T // TC
    TH = TC // P
    J = B * TH
    N = B * TC
    W = CC * N
    TOKENS = B * T
    BLK = 256
    BH = BLK // P
    BLOCKS = (2 * TOKENS + E * (BLK - 1)) // BLK
    REGION = TOKENS + BLK
    DUMMY = E * REGION
    REC = C + 1
    NOWHERE = 1 << 20
    FC = F // P
    PIECES = T // P
    RING = 4
    W1E, W2E = CC * F, FC * C
    WE = W1E + W2E
    LOWEST = -1e38
    EPS = 1e-5

    xs = nc.dram_tensor("records_dram", (DUMMY + BLK, REC), F32, kind="Internal").ap()
    ys = nc.dram_tensor("expert_out_dram", (2 * TOKENS, C), F32, kind="Internal").ap()
    x1d = nc.dram_tensor("x1_dram", (B, T, C), F32, kind="Internal").ap()

    with ExitStack() as ctx:
        def sb(name, shape, dt=F32, where=ctx):
            return where.enter_context(nc.sbuf_tensor(name, shape, dt))

        def sem(name):
            return ctx.enter_context(nc.semaphore(name))

        ident = sb("ident", [P, P])
        before = sb("before", [P, P])
        ones = sb("ones", [P, P])
        decay_c = sb("decay_c", [P, CC])
        first_c = sb("first_c", [P, CC])
        mix_c = sb("mix_c", [P, 3, CC])
        b1_c = sb("b1_c", [P, E * FC])
        unmix_c = sb("unmix_c", [P, 3, CC])
        bg_b = sb("bg_b", [P, E])
        expert_no = sb("expert_no", [P, E])
        region_no = sb("region_no", [P, E])
        dest_all = sb("dest_all", [P, NCH * J * 2], I32)
        half_neg = sb("half_neg", [P, J])
        eps_b = sb("eps_b", [P, J])
        top2 = sb("top2", [P, NCH, J, 2])
        score = sb("score", [P, NCH * J, 2])
        score_t = sb("score_t", [P, NCH * J, 2])
        pad_rec = sb("pad_rec", [P, REC])
        cnt_f = sb("cnt_f", [1, E])
        cnt_i = sb("cnt_i", [1, E], I32)
        tiles_i = sb("tiles_i", [1, E], I32)
        tiles_f = sb("tiles_f", [1, E])
        ends_f = sb("ends_f", [1, E])
        starts_f = sb("starts_f", [1, E])
        rowbase = sb("rowbase", [1, E])
        pad_row = sb("pad_row", [1, E], I32)
        ends = sb("ends", [1, E], I32)
        RECS = J * 2 * REC
        staging = sb("staging", [P, max(WE, 2 * RECS)])
        raw = staging[:, 0:WE]
        rec = [staging[:, n * RECS:(n + 1) * RECS].rearrange("p (j k c) -> p j k c", j=J, k=2) for n in range(2)]
        tile_f = sb("tile_f", [1, BLOCKS, E])
        past_s = sb("past_s", [1, BLOCKS, E])
        past_e = sb("past_e", [1, BLOCKS, E])
        tile_row = sb("tile_row", [1, BLOCKS])
        row_f = sb("row_f", [1, BLOCKS])
        ex_f = sb("ex_f", [1, BLOCKS])
        real_f = sb("real_f", [1, BLOCKS])
        row_t = sb("row_t", [1, BLOCKS], I32)
        ex_t = sb("ex_t", [1, BLOCKS], I32)
        par_t = sb("par_t", [1, BLOCKS], I32)
        var_e = sb("var_e", [P, J])
        rstd = sb("rstd", [P, 2, J])
        shift = sb("shift", [P, 2, J])
        neg_mean = sb("neg_mean", [P, J])
        stats = sb("stats", [P, J, 6])
        mv = sb("mv", [P, J, 2])

        phase_a = ExitStack()
        sb("w_slot0_place", [P, 2 * WE], F32, phase_a)
        xin = [sb(f"xin{n}", [P, B, TH, C], F32, phase_a) for n in range(2)]
        xres = [sb(f"xres{n}", [P, B, TH, C], F32, phase_a) for n in range(2)]
        xh = [sb(f"xh{n}", [P, CC, B, TC + 2], F32R, phase_a) for n in range(2)]
        xl = [sb(f"xl{n}", [P, CC, B, TC + 2], F32R, phase_a) for n in range(2)]
        wq = sb("wq", [P, 3, 2, 2, CC, C], F32R, phase_a)
        wo = sb("wo", [P, CC, C], F32, phase_a)
        wg = sb("wg", [P, CC, E], F32, phase_a)
        w_row = sb("w_row", [P, CC, TC], F32, phase_a)
        o_all = sb("o_all", [P, CC, B, TC + 1], F32, phase_a)
        p_all = sb("p_all", [P, CC, B, TC + 1], F32, phase_a)
        q_all = sb("q_all", [P, CC, B, TC + 1], F32, phase_a)
        s_buf = sb("s_buf", [P, CC, B, TC], F32, phase_a)
        A1 = sb("A1", [P, CC, B, TC], F32, phase_a)
        B1 = sb("B1", [P, CC, B, TC], F32, phase_a)
        A2 = sb("A2", [P, CC, B, TC], F32, phase_a)
        B2 = sb("B2", [P, CC, B, TC], F32, phase_a)
        v = [sb(f"v{n}", [P, CC, B, TC], F32, phase_a) for n in range(2)]
        gate = [sb(f"gate{n}", [P, CC, B, TC], F32, phase_a) for n in range(2)]
        b2v = sb("b2v", [P, CC, B, TC], F32, phase_a)
        bv = sb("bv", [P, CC, B, TC], F32, phase_a)
        num = sb("num", [P, CC, B, TC], F32, phase_a)
        den = sb("den", [P, CC, B, TC], F32, phase_a)
        r0 = sb("r0", [P, CC, B, TC], F32, phase_a)
        newton = sb("newton", [P, CC, B, TC], F32, phase_a)
        mixed = newton
        wraw = [s_buf, A1, B1]
        wscaled = [num, den, r0]
        b1_rows = sb("b1_rows", [E * FC, P], F32, phase_a)
        x1T = sb("x1T", [P, CC, N], F32, phase_a)
        lg = sb("lg", [P, J, E], F32, phase_a)
        m8 = sb("m8", [P, J, 8], F32, phase_a)
        i8 = sb("i8", [P, J, 8], U32, phase_a)
        idxf = sb("idxf", [P, J, 2], F32, phase_a)
        hot = sb("hot", [P, J, 2, E], F32, phase_a)
        seen = sb("seen", [P, E], F32, phase_a)
        newly = sb("newly", [P, E], F32, phase_a)
        picks = sb("picks", [P, J, E], F32, phase_a)
        rank = sb("rank", [P, J, E], F32, phase_a)
        spread = sb("spread", [P, J, 2, E], F32, phase_a)
        slot_f = sb("slot_f", [P, J, 2], F32, phase_a)
        slot_i = [sb(f"slot_i{n}", [P, J * 2], I32, phase_a) for n in range(2)]

        def ps(name, shape, where):
            return where.enter_context(nc.psum_tensor(name, shape, F32))

        xT_ps = ps("xT_ps", [P, CC, N], phase_a)
        k_ps = ps("k_ps", [P, CC, N], phase_a)
        vr_ps = [ps(f"vr_ps{n}", [P, N], phase_a) for n in range(2)]
        wo_ps = ps("wo_ps", [P, TH, C], phase_a)
        small_ps = ps("small_ps", [P, 512], phase_a)
        lg_ps = small_ps[:, 0:J * E].rearrange("p (j e) -> p j e", j=J)
        rank_ps = small_ps[:, 64:64 + J * E].rearrange("p (j e) -> p j e", j=J)
        cnt_ps = small_ps[:, 128:128 + E]
        phase_a.close()

        wx = sb("wx", [P, 2, 2, WE], F32R)
        xx = sb("xx", [P, PIECES, B, C])
        phase_b = ExitStack()
        b2_b = sb("b2_b", [P, E * C], F32, phase_b)
        recs = [sb(f"recs{n}", [P, BH, REC], F32, phase_b) for n in range(RING)]
        dest = [sb(f"dest{n}", [P, BH], I32, phase_b) for n in range(RING)]
        xTh = [sb(f"xTh{n}", [P, CC, BLK], F32R, phase_b) for n in range(2)]
        xTl = [sb(f"xTl{n}", [P, CC, BLK], F32R, phase_b) for n in range(2)]
        act_T = [sb(f"act_T{n}", [P, FC, BLK], F32, phase_b) for n in range(1)]
        aTh = [sb(f"aTh{n}", [P, FC, BLK], F32R, phase_b) for n in range(2)]
        aTl = [sb(f"aTl{n}", [P, FC, BLK], F32R, phase_b) for n in range(2)]
        y_sb = [sb(f"y_sb{n}", [P, BH, C], F32, phase_b) for n in range(RING)]
        hT_ps = [ps(f"hT_ps{n}", [P, 2, BLK], phase_b) for n in range(FC // 2)]
        xT2_ps = ps("xT2_ps", [P, CC, BLK], phase_b)
        y_ps = [ps(f"y_ps{n}", [P, 512], phase_b)[:, 0:C] for n in range(BH)]
        phase_b.close()
        yy = [sb(f"yy{n}", [P, B, 2 * C]) for n in range(RING)]
        zz = [sb(f"zz{n}", [P, B, C]) for n in range(2)]
        res = [sb(f"res{n}", [P, B, C]) for n in range(RING)]
        mv_c = [sb(f"mv_c{n}", [P, B, 2]) for n in range(2)]

        carried = sem("carried")
        consts_in, weights_in, gate_in, raw_in = sem("consts_in"), sem("weights_in"), sem("gate_in"), sem("raw_in")
        made, made2, padded = sem("made"), sem("made2"), sem("padded")
        setup_act, setup_dve = sem("setup_act"), sem("setup_dve")
        scaled, w_hi, w_lo = sem("scaled"), sem("w_hi"), sem("w_lo")
        xin_in = [sem(f"xin_in{n}") for n in range(2)]
        xres_in = [sem(f"xres_in{n}") for n in range(2)]
        xT_done, xh_done, xl_done = sem("xT_done"), sem("xh_done"), sem("xl_done")
        vr_done, k_done, v_out, gate_out = sem("vr_done"), sem("k_done"), sem("v_out"), sem("gate_out")
        o_carry, o_done, s_done, d3_done, d2_done = (sem(n) for n in ("o_carry", "o_done", "s_done", "d3_done", "d2_done"))
        relu_done, a1_done, b1_done, a2_done, b2_done = (sem(n) for n in ("relu_done", "a1_done", "b1_done", "a2_done", "b2_done"))
        qp_carry, q_done, p_done = sem("qp_carry"), sem("q_done"), sem("p_done")
        b2v_done, bv_done, aq_done, den_done, num_done = (sem(n) for n in ("b2v_done", "bv_done", "aq_done", "den_done", "num_done"))
        ln_done, r0_done, div_done, mixed_done = sem("ln_done"), sem("r0_done"), sem("div_done"), sem("mixed_done")
        wo_done, res_done, bn_done, mv_done = sem("wo_done"), sem("res_done"), sem("bn_done"), sem("mv_done")
        vare_done, rstd_done, x1_done, rec2_done = sem("vare_done"), sem("rstd_done"), sem("x1_done"), sem("rec2_done")
        dest_done, top2_done, cnt_done = sem("dest_done"), sem("top2_done"), sem("cnt_done")
        x1T_done, x1T_out, lg_done = sem("x1T_done"), sem("x1T_out"), sem("lg_done")
        route, rank_done, slots = sem("route"), sem("rank_done"), sem("slots")
        rec_out = [sem(f"rec_out{n}") for n in range(2)]
        x1_out = [sem(f"x1_out{n}") for n in range(2)]
        table, table_done, pads_out = sem("table"), sem("table_done"), sem("pads_out")
        bias_in, hi_done, weights_ready = sem("bias_in"), sem("hi_done"), sem("weights_ready")
        bias1_in, bias1_turned, bias1_done = sem("bias1_in"), sem("bias1_turned"), sem("bias1_done")
        rec_in = [sem(f"rec_in{n}") for n in range(RING)]
        y_out = [sem(f"y_out{n}") for n in range(RING)]
        tx_done, txh_done, txl_done = sem("tx_done"), sem("txh_done"), sem("txl_done")
        mm1_done, act_done = sem("mm1_done"), sem("act_done")
        aTh_done, aTl_done = sem("aTh_done"), sem("aTl_done")
        mm2_done, y_done = sem("mm2_done"), sem("y_done")
        exp_done, score_done = sem("exp_done"), sem("score_done")
        yy_in = [sem(f"yy_in{n}") for n in range(RING)]
        res_out = [sem(f"res_out{n}") for n in range(RING)]
        xx_in = sem("xx_in")
        c_sum, c_bn, c_mv, c_var, c_rstd, c_res = (sem(n) for n in ("c_sum", "c_bn", "c_mv", "c_var", "c_rstd", "c_res"))

        BG = 16
        REC_DMAS = 2 * J * 16
        ROUTE1, ROUTE2 = 2 * J + 4, 6

        def chunks(eng, body):
            plain = lambda n: Step(None, n, 2, NCH)
            for n in range(-2, 2):
                body(plain(n))
            with eng.Fori(1, NCH // 2 - 1) as m:
                body(Step(m, 0, 2, NCH))
                body(Step(m, 1, 2, NCH))
            for n in range(NCH - 2, NCH + 2):
                body(plain(n))

        LAST = (BLOCKS + 1) // RING * RING - RING

        def blocks(eng, body):
            plain = lambda n: Step(None, n, RING, BLOCKS)
            for n in range(-2, RING):
                body(plain(n))
            with eng.Fori(1, LAST // RING) as m:
                for n in range(RING):
                    body(Step(m, n, RING, BLOCKS))
            for n in range(LAST, BLOCKS + 1):
                body(plain(n))

        def pieces(eng, body):
            for n in range(RING):
                body(Step(None, n, RING, PIECES))
            with eng.Fori(1, PIECES // RING) as m:
                for n in range(RING):
                    body(Step(m, n, RING, PIECES))

        def after(eng, semaphore, value):
            if not isinstance(value, int) or value > 0:
                eng.wait_ge(semaphore, value)

        def take_wait(eng):
            eng.sem_inc(carried, 1)

        def load_chunk(sp, to, ap, i, done):
            for b in range(B):
                sp.dma_start(to[:, b], ap[b, bass.ds(i.number * TC, TC), :].rearrange("(h p) c -> p h c", p=P)).then_inc(done, 16)

        def store_chunk(sp, ap, i, rows, done):
            for b in range(B):
                sp.dma_start(ap[b, bass.ds(i.number * TC, TC), :].rearrange("(h p) c -> p h c", p=P), rows[:, b]).then_inc(done, 16)

        def phase_b_may_start(eng):
            eng.wait_ge(table_done, 1)
            for n in range(2):
                eng.wait_ge(rec_out[n], NCH // 2 * REC_DMAS + BG)
                eng.wait_ge(x1_out[n], NCH // 2 * B * 16 + BG)

        block = ctx.enter_context(nc.Block())

        @block.sync
        def _(sp):
            plain = lambda n: Step(None, n, 2, NCH)
            load_chunk(sp, xin[0], x, plain(0), xin_in[0])
            for n, w in enumerate((wvT, wrT, wkT)):
                sp.dma_start(wraw[n][:].rearrange("p c b t -> p (c b t)")[:, 0:CC * C].rearrange("p (c d) -> p c d", c=CC),
                             w.rearrange("(c p) d -> p c d", p=P)).then_inc(weights_in, 16)
            for n, m in enumerate((mix_v, mix_r, mix_k)):
                sp.dma_start(mix_c[:, n, :], m.rearrange("a b (c p) -> p (a b c)", p=P),
                             allow_slow_non_contiguous=True).then_inc(consts_in, 16)
            sp.dma_start(decay_c[:], decay.rearrange("(c p) -> p c", p=P),
                             allow_slow_non_contiguous=True).then_inc(consts_in, 16)
            sp.dma_start(first_c[:], first.rearrange("(c p) -> p c", p=P),
                             allow_slow_non_contiguous=True).then_inc(consts_in, 16)
            sp.dma_start(bg_b[:], bg.rearrange("(a e) -> a e", a=1).broadcast_to([P, E])).then_inc(consts_in, 16)
            sp.dma_start(b1_rows[:], b1.rearrange("e (c p) -> (e c) p", p=P)).then_inc(bias1_in, 16)
            load_chunk(sp, xin[1], x, plain(1), xin_in[1])
            sp.dma_start(wo[:], woT.rearrange("(c p) d -> p c d", p=P)).then_inc(gate_in, 16)
            sp.dma_start(wg[:], wgT.rearrange("(c p) e -> p c e", p=P)).then_inc(gate_in, 16)

            def load_raw(e):
                sp.dma_start(raw[:, 0:W1E].rearrange("p (c f) -> p c f", c=CC),
                             w1[e].rearrange("(c p) f -> p c f", p=P)).then_inc(raw_in, 16)
                sp.dma_start(raw[:, W1E:WE].rearrange("p (c d) -> p c d", c=FC),
                             w2[e].rearrange("(c p) d -> p c d", p=P)).then_inc(raw_in, 16)

            load_raw(0)
            sp.wait_ge(padded, 2)
            for n in range(2):
                sp.dma_start(xs[DUMMY + 128 + 64 * n:DUMMY + 192 + 64 * n, :], pad_rec[64 * n:64 * n + 64, :]).then_inc(x1_out[n], 16)

            def step(i):
                c = i + 2
                if c.exists and (c - 2).exists:
                    sp.wait_ge(xT_done, (c - 2).upto(CC))
                    load_chunk(sp, xin[c.slot], x, c, xin_in[c.slot])
                if (i - 2).exists:
                    sp.wait_ge(x1_done, (i - 2).upto(J))
                if i.exists:
                    load_chunk(sp, xres[i.slot], x, i, xres_in[i.slot])
                c = i - 2
                if c.exists:
                    store_chunk(sp, x1d, c, rec[c.slot][:, :, 0, 0:C].rearrange("p (b h) c -> p b h c", b=B), x1_out[c.slot])

            chunks(sp, step)
            sp.wait_ge(table, 2)
            for e in range(E):
                row = sp.value_load(pad_row[0:1, e:e + 1], min_val=0, max_val=DUMMY - BLK)
                sp.dma_start(xs[bass.ds(row, BLK), :].rearrange("(h p) c -> p h c", p=P),
                             pad_rec[:].unsqueeze(1).broadcast_to([P, BH, REC])).then_inc(pads_out, 16)
            phase_b_may_start(sp)
            sp.wait_ge(weights_ready, 1)
            sp.wait_ge(rec_in[0], 16)
            load_raw(1)
            sp.dma_start(b2_b[:], b2.rearrange("(a e) c -> a (e c)", a=1).broadcast_to([P, E * C])).then_inc(bias_in, 16)
            for e in range(2, E):
                sp.wait_ge(weights_ready, e)
                load_raw(e)
                if e == 2:
                    for b in range(B):
                        sp.dma_start(xx[:, :, b, :], x1d[b].rearrange("(q p) c -> p q c", p=P)).then_inc(xx_in, 16)
            for n in range(RING):
                sp.wait_ge(y_out[n], -((n - BLOCKS) // RING) * 16 * BH)
            ys_t = ys.rearrange("(b t k) c -> b t (k c)", b=B, k=2)

            def load_outputs(i):
                sp.dma_start(yy[i.slot][:], ys_t[:, bass.ds(i.number * P, P), :].rearrange("b p c -> p b c")).then_inc(yy_in[i.slot], 16)

            for n in range(RING):
                load_outputs(Step(None, n, RING, PIECES))
            for n in range(RING, PIECES):
                sp.wait_ge(c_sum, (n - RING + 1) * 2 * B)
                load_outputs(Step(None, n, RING, PIECES))
            for n in range(RING):
                sp.wait_ge(res_out[n], PIECES // RING * 16)

        @block.gpsimd
        def _(pool):
            pool.memset(ident[:], 0.0).then_inc(made, 1)
            pool.memset(before[:], 1.0).then_inc(made, 1)
            pool.memset(ones[:], 1.0).then_inc(made2, 1)
            pool.memset(half_neg[:], -0.5).then_inc(made2, 1)
            pool.memset(eps_b[:], EPS).then_inc(made2, 1)
            pool.wait_ge(made, 2)
            pool.affine_select(out=ident[:], in_=ident[:], compare_op=ALU.not_equal, fill=1.0, base=0,
                               pattern=[[-1, P]], channel_multiplier=1).then_inc(made2, 1)
            pool.affine_select(out=before[:], in_=before[:], compare_op=ALU.is_gt, fill=0.0, base=0,
                               pattern=[[1, P]], channel_multiplier=-1).then_inc(made2, 1)
            pool.iota(expert_no[:], [[1, E]], base=0, channel_multiplier=0,
                      allow_small_or_imprecise_dtypes=True).then_inc(made2, 1)
            pool.iota(region_no[:], [[REGION, E]], base=0, channel_multiplier=0,
                      allow_small_or_imprecise_dtypes=True).then_inc(made2, 1)
            for i in range(NCH):
                pool.iota(dest_all[:, i * 2 * J:(i + 1) * 2 * J], [[2 * T, B], [2 * P, TH], [1, 2]],
                          base=2 * TC * i, channel_multiplier=2).then_inc(made2, 1)
            pool.memset(xh[0][:, :, :, 0:1].bitcast(F32), 0.0).then_inc(xh_done, 1)
            pool.memset(xl[0][:, :, :, 0:1].bitcast(F32), 0.0).then_inc(xl_done, 1)
            pool.memset(pad_rec[:, 0:C], 0.0).then_inc(padded, 1)
            pool.memset(pad_rec[:, C:REC].bitcast(I32), NOWHERE).then_inc(padded, 1)

            def split(e):
                pool.wait_ge(raw_in, 32 * (e + 1))
                pool.tensor_scalar(wx[:, e % 2, 0, :], raw, 1.0, 0.0, ALU.mult, ALU.add).then_inc(hi_done, 1)
                pool.wait_ge(hi_done, e + 1)
                pool.tensor_tensor(wx[:, e % 2, 1, :], raw, wx[:, e % 2, 0, :].bitcast(F32),
                                   ALU.subtract).then_inc(weights_ready, 1)

            pool.iota(tile_f[:], [[1, BLOCKS], [0, E]], base=0, channel_multiplier=0,
                      allow_small_or_imprecise_dtypes=True).then_inc(made, 1)
            pool.iota(tile_row[:], [[BLK, BLOCKS]], base=-DUMMY, channel_multiplier=0,
                      allow_small_or_imprecise_dtypes=True).then_inc(made, 1)
            pool.wait_ge(padded, 2)
            for n in range(2):
                pool.dma_start(xs[DUMMY + 64 * n:DUMMY + 64 * n + 64, :], pad_rec[64 * n:64 * n + 64, :]).then_inc(rec_out[n], 16)
            pool.wait_ge(raw_in, 32)
            pool.tensor_scalar(wx[:, 0, 0, :], raw, 1.0, 0.0, ALU.mult, ALU.add).then_inc(hi_done, 1)
            pool.wait_ge(hi_done, 1)
            pool.tensor_tensor(wx[:, 0, 1, :], raw, wx[:, 0, 0, :].bitcast(F32), ALU.subtract).then_inc(weights_ready, 1)

            def step(i):
                if i.exists:
                    pool.wait_ge(b2_done, i.upto(1))
                    pool.wait_ge(v_out, i.upto(CC))
                    after(pool, p_done, (i - 1).upto(CC * B))
                    pool.tensor_tensor(b2v[:], B2[:], v[i.slot][:], ALU.mult).then_inc(b2v_done, 1)
                    pool.wait_ge(b1_done, i.upto(1))
                    after(pool, num_done, (i - 1).upto(2))
                    pool.tensor_tensor(bv[:], B1[:], v[i.slot][:], ALU.mult).then_inc(bv_done, 1)
                    pool.wait_ge(a1_done, i.upto(1))
                    pool.wait_ge(q_done, i.upto(CC * B))
                    after(pool, mixed_done, (i - 1).upto(1))
                    pool.tensor_tensor(den[:], A1[:], q_all[:, :, :, 0:TC], ALU.mult).then_inc(aq_done, 1)
                    pool.wait_ge(aq_done, i.upto(1))
                    pool.tensor_tensor(den[:], den[:], B1[:], ALU.add).then_inc(den_done, 1)
                c = i - 1
                if c.exists:
                    pool.wait_ge(mv_done, c.upto(J))
                    pool.tensor_tensor(var_e[:], mv[:, :, 1], eps_b[:], ALU.add).then_inc(vare_done, 1)
                    pool.tensor_scalar(neg_mean[:], mv[:, :, 0], -1.0, 0.0, ALU.mult, ALU.add).then_inc(vare_done, 1)
                    pool.wait_ge(vare_done, c.upto(3, 2))
                    pool.tensor_tensor(rstd[:, c.slot, :], var_e[:], half_neg[:], ALU.pow).then_inc(vare_done, 1)
                    pool.wait_ge(vare_done, c.upto(3))
                    pool.tensor_tensor(shift[:, c.slot, :], neg_mean[:], rstd[:, c.slot, :], ALU.mult).then_inc(rstd_done, 1)
                c = i - 2
                if c.exists:
                    pool.wait_ge(slots, c.upto(ROUTE2))
                    pool.wait_ge(rec2_done, c.upto(1))
                    pool.wait_ge(dest_done, c.upto(1))
                    take_wait(pool)
                    for j in range(J):
                        for k in range(2):
                            n = 2 * j + k
                            pool.indirect_dma_start(
                                xs, bass.IndirectOffsetOnAxis(ap=slot_i[c.slot][:, n:n + 1], axis=0),
                                rec[c.slot][:, j, k, :], None, bounds_check=DUMMY - 1,
                                oob_is_err=False).then_inc(rec_out[c.slot], 16)

            chunks(pool, step)

            phase_b_may_start(pool)
            split(1)
            end = [pool.value_load(ends[0:1, e:e + 1], min_val=0, max_val=BLOCKS) for e in range(E - 2)]

            def scatter(t):
                for e in range(2, E):
                    with pool.If(end[e - 2] == t.number):
                        split(e)
                for h in range(BH):
                    pool.wait_ge(y_done, t.upto(BH, h + 1))
                    take_wait(pool)
                    pool.indirect_dma_start(
                        ys, bass.IndirectOffsetOnAxis(ap=dest[t.slot][:, h:h + 1], axis=0), y_sb[t.slot][:, h, :], None,
                        bounds_check=2 * TOKENS - 1, oob_is_err=False).then_inc(y_out[t.slot], 16)

            with pool.Fori(0, BLOCKS // RING) as m:
                for n in range(RING):
                    scatter(Step(m, n, RING, BLOCKS))
            for n in range(BLOCKS // RING * RING, BLOCKS):
                scatter(Step(None, n, RING, BLOCKS))

            def norm_step(i):
                n = i.slot % 2
                pool.wait_ge(c_mv, i.upto(B))
                after(pool, c_res, (i - 2).upto(B))
                after(pool, c_rstd, (i - 1).upto(1))
                pool.tensor_tensor(var_e[:, 0:B], mv_c[n][:, :, 1], eps_b[:, 0:B], ALU.add).then_inc(c_var, 1)
                pool.tensor_scalar(neg_mean[:, 0:B], mv_c[n][:, :, 0], -1.0, 0.0, ALU.mult, ALU.add).then_inc(c_var, 1)
                pool.wait_ge(c_var, i.upto(3, 2))
                pool.tensor_tensor(rstd[:, n, 0:B], var_e[:, 0:B], half_neg[:, 0:B], ALU.pow).then_inc(c_var, 1)
                pool.wait_ge(c_var, i.upto(3))
                pool.tensor_tensor(shift[:, n, 0:B], neg_mean[:, 0:B], rstd[:, n, 0:B], ALU.mult).then_inc(c_rstd, 1)

            pieces(pool, norm_step)

        @block.tensor
        def _(pe):
            pe.wait_ge(made2, 7 + NCH)
            pe.wait_ge(bias1_in, 16)
            pe.transpose(small_ps[:, 256:256 + E * FC], b1_rows[:], ident[0:E * FC, 0:E * FC]).then_inc(bias1_turned, 1)

            def transpose_x(c):
                pe.wait_ge(xin_in[c.slot], c.turn(16 * B, 16 * B))
                after(pe, xl_done, (c - 1).upto(CC + 1))
                if (c - 4).exists:
                    pe.wait_ge(x1T_out, (c - 4).upto(CC))
                for cc in range(CC):
                    for j in range(J):
                        ins = pe.transpose(xT_ps[:, cc, j * P:(j + 1) * P],
                                           xin[c.slot][:, j // TH, j % TH, cc * P:(cc + 1) * P], ident[:])
                    ins.then_inc(xT_done, 1)

            def project(c, mat, oc, out_ps):
                terms = [(cc, now, a, b) for cc in range(CC) for now in range(2)
                         for a, b in ((0, xh), (0, xl), (1, xh))]
                for n, (cc, now, part, xpart) in enumerate(terms):
                    ins = pe.matmul(out_ps.rearrange("p (b t) -> p b t", b=B), wq[:, mat, now, part, cc, oc * P:(oc + 1) * P],
                                    xpart[c.slot][:, cc, :, now:now + TC],
                                    start=n == 0, stop=n == len(terms) - 1)
                return ins

            def out_project(c, b):
                for h in range(TH):
                    for cc in range(CC):
                        ins = pe.matmul(wo_ps[:, h, :], mixed[:, cc, b, h * P:(h + 1) * P], wo[:, cc, :],
                                        start=cc == 0, stop=cc == CC - 1)
                ins.then_inc(wo_done, 1)

            def score_rows(c):
                if c.exists:
                    pe.wait_ge(x1T_out, c.upto(CC))
                    pe.wait_ge(dest_done, c.upto(1))
                    pe.matmul(lg_ps, ones[0:1, :], bg_b[0:1, :].unsqueeze(1).broadcast_to([1, J, E]), start=True, stop=False)
                    for j in range(J):
                        for cc in range(CC):
                            ins = pe.matmul(lg_ps[:, j, :], x1T[:, cc, j * P:(j + 1) * P], wg[:, cc, :],
                                            start=False, stop=j == J - 1 and cc == CC - 1)
                    ins.then_inc(lg_done, 1)

            def step(i):
                for n in range(CC):
                    c = i + 1
                    if c.exists:
                        if n == 0:
                            if c.fixed and c.number == 0:
                                pe.wait_ge(w_lo, 2)
                            pe.wait_ge(xl_done, c.upto(CC + 1))
                        after(pe, gate_out, i.upto(CC, n + 1))
                        project(c, 0, n, vr_ps[n][:]).then_inc(vr_done, 1)
                    c = i - 2
                    if c.exists and n == CC - 1:
                        pe.wait_ge(x1_done, c.upto(J))
                        for cc in range(CC):
                            for j in range(J):
                                ins = pe.transpose(xT_ps[:, cc, j * P:(j + 1) * P],
                                                   rec[c.slot][:, j, 0, cc * P:(cc + 1) * P], ident[:])
                            ins.then_inc(x1T_done, 1)
                for n in range(CC):
                    c = i + 1
                    if c.exists:
                        pe.wait_ge(v_out, c.upto(CC, n + 1))
                        project(c, 1, n, vr_ps[n][:]).then_inc(vr_done, 1)
                    if n == 0:
                        if not i.fixed or i.number < NCH:
                            score_rows(i - 2)
                        if (i + 2).exists:
                            transpose_x(i + 2)
                    c = i - 1
                    if c.exists:
                        if n == 0:
                            if c.fixed and c.number == 0:
                                pe.wait_ge(gate_in, 32)
                            pe.wait_ge(mixed_done, c.upto(1))
                            after(pe, res_done, (c - 1).upto(2))
                        else:
                            pe.wait_ge(res_done, c.upto(2, 1))
                        out_project(c, n)
                if i.fixed and i.number >= NCH:
                    score_rows(i - 2)
                c = i - 2
                if c.exists:
                    pe.wait_ge(route, c.upto(ROUTE1))
                    pe.matmul(rank_ps, before[:], picks[:], start=True, stop=False)
                    for j in range(J - 1):
                        pe.matmul(rank_ps[:, j + 1:J, :], ones[:], picks[:, j:j + 1, :].broadcast_to([P, J - 1 - j, E]),
                                  start=False, stop=False)
                    pe.matmul(rank_ps, ones[:], seen[:].unsqueeze(1).broadcast_to([P, J, E]), start=False, stop=True).then_inc(rank_done, 1)
                    if c.fixed and c.number == NCH - 1:
                        pe.wait_ge(slots, c.upto(ROUTE2, 4))
                        pe.matmul(cnt_ps, ones[:], seen[:], start=True, stop=True).then_inc(cnt_done, 1)
                c = i + 1
                if c.exists:
                    if c.fixed and c.number == 0:
                        pe.wait_ge(w_lo, 3)
                    after(pe, d2_done, i.upto(1))
                    for oc in range(CC):
                        project(c, 2, oc, k_ps[:, oc, :]).then_inc(k_done, 1)
            chunks(pe, step)

            phase_b_may_start(pe)

            def product1(t, s):
                for b in range(FC // 2):
                    after(pe, act_done, (t - 1).upto(FC, 2 * b + 2))
                    for f in range(2):
                        terms = [(cc, part, a) for cc in range(CC) for part, a in ((0, xTh), (0, xTl), (1, xTh))]
                        for k, (cc, part, xpart) in enumerate(terms):
                            off = cc * F + (2 * b + f) * P
                            ins = pe.matmul(hT_ps[b][:, f, :], wx[:, s, part, off:off + P], xpart[t.slot % 2][:, cc, :],
                                            start=k == 0, stop=k == len(terms) - 1)
                    ins.then_inc(mm1_done, 1)

            def product2(t, s):
                for h in range(BH):
                    after(pe, y_done, (t - 1).upto(BH, h + 1))
                    terms = [(fc, a, b) for fc in range(FC) for a, b in ((aTh, 0), (aTh, 1), (aTl, 0))]
                    for k, (fc, apart, part) in enumerate(terms):
                        off = W1E + fc * C
                        ins = pe.matmul(y_ps[h], apart[t.slot % 2][:, fc, h * P:(h + 1) * P], wx[:, s, part, off:off + C],
                                        start=k == 0, stop=k == len(terms) - 1)
                    ins.then_inc(mm2_done, 1)

            def block_step(t):
                u = t + 1
                if u.exists:
                    expert = pe.value_load(ex_t[0:1, bass.ds(u.number, 1)], min_val=0, max_val=E - 1)
                    slot = expert % 2
                    pe.wait_ge(txl_done, u.upto(1))
                    pe.wait_ge(weights_ready, expert + 1)
                    with pe.If(slot == 0):
                        product1(u, 0)
                    with pe.Else():
                        product1(u, 1)
                u = t + 2
                if u.exists:
                    pe.wait_ge(rec_in[u.slot], u.turn(16, 16))
                    after(pe, txl_done, (u - 1).upto(1))
                    for cc in range(CC):
                        for h in range(BH):
                            ins = pe.transpose(xT2_ps[:, cc, h * P:(h + 1) * P], recs[u.slot][:, h, cc * P:(cc + 1) * P], ident[:])
                    ins.then_inc(tx_done, 1)
                if t.exists:
                    slot = pe.value_load(par_t[0:1, bass.ds(t.number, 1)], min_val=0, max_val=1)
                    pe.wait_ge(aTl_done, t.upto(FC // 2))
                    with pe.If(slot == 0):
                        product2(t, 0)
                    with pe.Else():
                        product2(t, 1)

            blocks(pe, block_step)

        @block.scalar
        def _(act):
            act.wait_ge(consts_in, 6 * 16)
            act.activation(decay_c[:], decay_c[:], ACT.Exp).then_inc(setup_act, 1)
            for n in range(3):
                act.wait_ge(scaled, 4 * (n + 1))
                act.activation(wq[:, n, :, 0, :, :], wscaled[n][:].rearrange("p c b t -> p (c b t)").rearrange(
                    "p (a c d) -> p a c d", a=2, c=CC), ACT.Copy).then_inc(w_hi, 1)

            def copy_v(c, cc):
                act.wait_ge(vr_done, c.upto(2 * CC, cc + 1))
                if cc == 0:
                    after(act, bv_done, (c - 2).upto(1))
                act.activation(v[c.slot][:, cc], vr_ps[cc][:].rearrange("p (b t) -> p b t", b=B), ACT.Copy).then_inc(v_out, 1)

            def step(i):
                c = i + 1
                if c.exists:
                    copy_v(c, 0)
                if i.exists:
                    act.wait_ge(s_done, i.upto(CC))
                    after(act, num_done, (i - 1).upto(2, 1))
                    after(act, den_done, (i - 1).upto(1))
                    act.activation(A1[:], s_buf[:], ACT.Relu).then_inc(relu_done, 1)
                    act.activation(B1[:], s_buf[:], ACT.Relu, scale=-1.0).then_inc(relu_done, 1)
                c = i - 2
                if c.exists:
                    for cc in range(CC):
                        act.wait_ge(x1T_done, c.upto(CC, cc + 1))
                        act.activation(x1T[:, cc, :], xT_ps[:, cc, :], ACT.Copy).then_inc(x1T_out, 1)
                if i.exists:
                    act.wait_ge(d3_done, i.upto(1))
                    for cc in range(CC):
                        act.activation(A2[:, cc], A2[:, cc], ACT.Exp, bias=decay_c[:, cc:cc + 1]).then_inc(a2_done, 1)
                    act.wait_ge(d2_done, i.upto(1))
                    act.activation(B2[:], B2[:], ACT.Exp).then_inc(b2_done, 1)
                c = i + 1
                if c.exists:
                    copy_v(c, 1)
                if i.exists:
                    act.wait_ge(relu_done, i.upto(2))
                    act.activation(B1[:], B1[:], ACT.Exp, scale=-1.0).then_inc(b1_done, 1)
                    act.activation(A1[:], A1[:], ACT.Exp, scale=-1.0).then_inc(a1_done, 1)
                c = i + 2
                if c.exists:
                    act.wait_ge(xT_done, c.upto(CC))
                    after(act, k_done, (c - 2).upto(CC))
                    if not c.fixed or c.number > 0:
                        act.wait_ge(xh_done, (c - 1).upto(CC + 1))
                        act.activation(xh[c.slot][:, :, :, 0:1], xh[1 - c.slot][:, :, :, TC:TC + 1].bitcast(F32),
                                       ACT.Copy).then_inc(xh_done, 1)
                    for cc in range(CC):
                        act.activation(xh[c.slot][:, cc, :, 1:TC + 1], xT_ps[:, cc, :].rearrange("p (b t) -> p b t", b=B),
                                       ACT.Copy).then_inc(xh_done, 1)
                c = i - 2
                if c.exists:
                    act.wait_ge(x1_done, c.upto(J))
                    act.activation(rec[c.slot][:, :, 1, 0:C], rec[c.slot][:, :, 0, 0:C], ACT.Copy).then_inc(rec2_done, 1)
                c = i + 1
                if c.exists:
                    after(act, mixed_done, (c - 2).upto(1))
                    for cc in range(CC):
                        act.wait_ge(vr_done, c.upto(2 * CC, CC + cc + 1))
                        act.activation(gate[c.slot][:, cc], vr_ps[cc][:].rearrange("p (b t) -> p b t", b=B),
                                       ACT.Sigmoid).then_inc(gate_out, 1)
                if i.exists:
                    act.wait_ge(den_done, i.upto(1))
                    after(act, mixed_done, (i - 1).upto(1))
                    act.activation(r0[:], den[:], ACT.Ln).then_inc(ln_done, 1)
                    act.wait_ge(ln_done, i.upto(1))
                    act.activation(r0[:], r0[:], ACT.Exp, scale=-1.0).then_inc(r0_done, 1)
                c = i - 1
                if c.exists:
                    act.wait_ge(rstd_done, c.upto(1))
                    act.wait_ge(rec_out[c.slot], c.turn(REC_DMAS, BG))
                    act.wait_ge(x1_out[c.slot], c.turn(B * 16, BG))
                    for j in range(J):
                        act.activation(rec[c.slot][:, j, 0, 0:C], xres[c.slot][:, j // TH, j % TH, :], ACT.Identity,
                                       bias=shift[:, c.slot, j:j + 1], scale=rstd[:, c.slot, j:j + 1]).then_inc(x1_done, 1)
                c = i - 2
                if c.exists:
                    act.wait_ge(lg_done, c.upto(1))

            chunks(act, step)

            phase_b_may_start(act)
            act.wait_ge(pads_out, 16 * E)

            def load_records(u):
                row = act.value_load(row_t[0:1, bass.ds(u.number, 1)], min_val=0, max_val=DUMMY)
                act.dma_start(recs[u.slot][:], xs[bass.ds(row, BLK), :].rearrange("(h p) c -> p h c", p=P)).then_inc(rec_in[u.slot], 16)

            load_records(Step(None, 0, RING, BLOCKS))
            act.wait_ge(score_done, 1)
            act.activation(score_t[:, :, 0:1], score_t[:, :, 0:1], ACT.Exp).then_inc(exp_done, 1)

            def activate(u, expert, func):
                for b in range(FC // 2 + 1):
                    if b < FC // 2:
                        act.wait_ge(mm1_done, u.upto(FC // 2, b + 1))
                        after(act, aTl_done, (u - 1).upto(FC // 2, b + 1))
                        for f in range(2):
                            act.activation(act_T[0][:, 2 * b + f, :], hT_ps[b][:, f, :], func,
                                           bias=b1_c[:, bass.ds(expert * FC + (2 * b + f), 1)]).then_inc(act_done, 1)
                    if b > 0:
                        act.wait_ge(act_done, u.upto(FC, 2 * b))
                        after(act, mm2_done, (u - 2).upto(BH))
                        act.activation(aTh[u.slot % 2][:, 2 * b - 2:2 * b, :], act_T[0][:, 2 * b - 2:2 * b, :], ACT.Copy).then_inc(aTh_done, 1)

            def block_step(t):
                u = t + 3
                if u.exists:
                    after(act, txl_done, (u - RING).upto(1))
                    load_records(u)
                u = t + 1
                if u.exists:
                    expert = act.value_load(ex_t[0:1, bass.ds(u.number, 1)], min_val=0, max_val=E - 1)
                    with act.If(expert % 2 == 0):
                        activate(u, expert, ACT.Gelu)
                    with act.Else():
                        activate(u, expert, ACT.Silu)

            blocks(act, block_step)

            def out_step(i):
                act.wait_ge(c_rstd, i.upto(1))
                if (i - RING).exists:
                    act.wait_ge(res_out[i.slot], i.turn(16))
                for b in range(B):
                    act.activation(res[i.slot][:, b, :], zz[i.slot % 2][:, b, :], ACT.Identity,
                                   bias=shift[:, i.slot % 2, b:b + 1], scale=rstd[:, i.slot % 2, b:b + 1]).then_inc(c_res, 1)
                act.wait_ge(c_res, i.upto(B))
                act.dma_start(out[:, bass.ds(i.number * P, P), :].rearrange("b p c -> p b c"), res[i.slot][:]).then_inc(res_out[i.slot], 16)

            pieces(act, out_step)

        @block.vector
        def _(dve):
            dve.wait_ge(consts_in, 6 * 16)
            dve.tensor_scalar(unmix_c[:], mix_c[:], -1.0, 1.0, ALU.mult, ALU.add).then_inc(setup_dve, 1)
            dve.wait_ge(setup_dve, 1)
            dve.wait_ge(weights_in, 3 * 16)
            for n in range(3):
                src = wraw[n][:].rearrange("p c b t -> p (c b t)")
                dst = wscaled[n][:].rearrange("p c b t -> p (c b t)").rearrange("p (a c d) -> p a c d", a=2, c=CC)
                for a, factor in ((0, unmix_c), (1, mix_c)):
                    for cc in range(CC):
                        dve.tensor_scalar(dst[:, a, cc, :], src[:, cc * C:(cc + 1) * C], factor[:, n, cc:cc + 1], None,
                                          ALU.mult).then_inc(scaled, 1)
                dve.wait_ge(scaled, 4 * (n + 1))
                dve.wait_ge(w_hi, n + 1)
                dve.tensor_tensor(wq[:, n, :, 1, :, :], dst, wq[:, n, :, 0, :, :].bitcast(F32), ALU.subtract).then_inc(w_lo, 1)
            dve.wait_ge(setup_act, 1)
            dve.tensor_scalar(decay_c[:], decay_c[:], -1.0, None, ALU.mult).then_inc(setup_dve, 1)
            dve.wait_ge(setup_dve, 2)
            for cc in range(CC):
                dve.tensor_copy(w_row[:, cc, :], decay_c[:, cc:cc + 1].broadcast_to([P, TC])).then_inc(setup_dve, 1)
            dve.memset(seen[:], 0.0).then_inc(setup_dve, 1)
            dve.wait_ge(setup_dve, 3 + CC)
            dve.wait_ge(made2, 7 + NCH)
            dve.wait_ge(bias1_turned, 1)
            dve.tensor_copy(b1_c[:], small_ps[:, 256:256 + E * FC]).then_inc(bias1_done, 1)

            def stabilise(i):
                if i.fixed and i.number == 0:
                    dve.memset(o_all[:, :, :, 0:1], LOWEST).then_inc(o_carry, 1)
                else:
                    dve.wait_ge(o_done, (i - 1).upto(CC * B))
                    dve.tensor_copy(o_all[:, :, :, 0:1], o_all[:, :, :, TC:TC + 1]).then_inc(o_carry, 1)
                dve.wait_ge(o_carry, i.upto(1))
                dve.wait_ge(k_done, i.upto(CC))
                for cc in range(CC):
                    for b in range(B):
                        dve.tensor_tensor_scan(o_all[:, cc, b, 1:TC + 1], w_row[:, cc, :],
                                               k_ps[:, cc, b * TC:(b + 1) * TC], o_all[:, cc, b, 0:1],
                                               ALU.add, ALU.max).then_inc(o_done, 1)
                dve.wait_ge(o_done, i.upto(CC * B))
                after(dve, relu_done, (i - 1).upto(2))
                for cc in range(CC):
                    dve.scalar_tensor_tensor(out=s_buf[:, cc], in0=k_ps[:, cc, :].rearrange("p (b t) -> p b t", b=B),
                                             scalar=first_c[:, cc:cc + 1], in1=o_all[:, cc, :, 0:TC],
                                             op0=ALU.add, op1=ALU.subtract).then_inc(s_done, 1)
                dve.tensor_tensor(A2[:], o_all[:, :, :, 0:TC], o_all[:, :, :, 1:TC + 1], ALU.subtract).then_inc(d3_done, 1)
                after(dve, b2v_done, (i - 1).upto(1))
                dve.tensor_tensor(B2[:], k_ps[:].rearrange("p c (b t) -> p c b t", b=B), o_all[:, :, :, 1:TC + 1],
                                  ALU.subtract).then_inc(d2_done, 1)

            def divide(c):
                dve.wait_ge(r0_done, c.upto(1))
                after(dve, wo_done, (c - 1).upto(2))
                dve.tensor_tensor(newton[:], den[:], r0[:], ALU.mult).then_inc(div_done, 1)
                dve.wait_ge(div_done, c.upto(3, 1))
                dve.scalar_tensor_tensor(out=newton[:], in0=newton[:], scalar=2.0, in1=r0[:],
                                         op0=ALU.subtract, op1=ALU.mult).then_inc(div_done, 1)
                dve.wait_ge(div_done, c.upto(3, 2))
                dve.wait_ge(num_done, c.upto(2))
                dve.tensor_tensor(newton[:], num[:], newton[:], ALU.mult).then_inc(div_done, 1)
                dve.wait_ge(div_done, c.upto(3))
                dve.wait_ge(gate_out, c.upto(CC))
                dve.scalar_tensor_tensor(out=mixed[:], in0=newton[:], scalar=-1.0, in1=gate[c.slot][:],
                                         op0=ALU.mult, op1=ALU.mult).then_inc(mixed_done, 1)

            def choose(c):
                dve.wait_ge(lg_done, c.upto(1))
                dve.tensor_copy(lg[:], lg_ps).then_inc(route, 1)
                dve.wait_ge(route, c.upto(ROUTE1, 1))
                take_wait(dve)
                for j in range(J):
                    dve.max(m8[:, j, :], lg[:, j, :]).then_inc(route, 1)
                dve.wait_ge(route, c.upto(ROUTE1, 1 + J))
                take_wait(dve)
                for j in range(J):
                    dve.max_index(i8[:, j, :], m8[:, j, :], lg[:, j, :]).then_inc(route, 1)
                dve.tensor_copy(top2[:].rearrange("p i j k -> p (i j k)")[:, bass.ds(c.number * (2 * J), 2 * J)].rearrange(
                    "p (j k) -> p j k", j=J), m8[:, :, 0:2]).then_inc(top2_done, 1)
                dve.wait_ge(route, c.upto(ROUTE1, 1 + 2 * J))
                dve.tensor_copy(idxf[:], i8[:, :, 0:2]).then_inc(route, 1)
                dve.wait_ge(route, c.upto(ROUTE1, 2 + 2 * J))
                dve.tensor_tensor(hot[:], expert_no[:].unsqueeze(1).unsqueeze(1).broadcast_to([P, J, 2, E]),
                                  idxf[:].unsqueeze(3).broadcast_to([P, J, 2, E]), ALU.is_equal).then_inc(route, 1)
                dve.wait_ge(route, c.upto(ROUTE1, 3 + 2 * J))
                dve.tensor_tensor(picks[:], hot[:, :, 0, :], hot[:, :, 1, :], ALU.add).then_inc(route, 1)

            def accumulate(i):
                dve.wait_ge(a2_done, i.upto(CC))
                dve.wait_ge(b2_done, i.upto(1))
                if i.fixed and i.number == 0:
                    dve.memset(q_all[:, :, :, 0:1], 0.0).then_inc(qp_carry, 1)
                    dve.memset(p_all[:, :, :, 0:1], 0.0).then_inc(qp_carry, 1)
                else:
                    dve.wait_ge(aq_done, (i - 1).upto(1))
                    dve.tensor_copy(q_all[:, :, :, 0:1], q_all[:, :, :, TC:TC + 1]).then_inc(qp_carry, 1)
                    dve.tensor_copy(p_all[:, :, :, 0:1], p_all[:, :, :, TC:TC + 1]).then_inc(qp_carry, 1)
                dve.wait_ge(qp_carry, i.upto(2))
                for all_, add, done in ((q_all, B2, q_done), (p_all, b2v, p_done)):
                    if all_ is p_all:
                        dve.wait_ge(b2v_done, i.upto(1))
                    for cc in range(CC):
                        for b in range(B):
                            dve.tensor_tensor_scan(all_[:, cc, b, 1:TC + 1], A2[:, cc, b, :], add[:, cc, b, :],
                                                   all_[:, cc, b, 0:1], ALU.mult, ALU.add).then_inc(done, 1)

            def lower_halves(c):
                dve.wait_ge(xh_done, c.upto(CC + 1))
                after(dve, k_done, (c - 2).upto(CC))
                if not c.fixed or c.number > 0:
                    dve.wait_ge(xl_done, (c - 1).upto(CC + 1))
                    dve.tensor_copy(xl[c.slot][:, :, :, 0:1],
                                    xl[1 - c.slot][:, :, :, TC:TC + 1].bitcast(F32)).then_inc(xl_done, 1)
                for cc in range(CC):
                    dve.tensor_tensor(xl[c.slot][:, cc, :, 1:TC + 1], xT_ps[:, cc, :].rearrange("p (b t) -> p b t", b=B),
                                      xh[c.slot][:, cc, :, 1:TC + 1].bitcast(F32), ALU.subtract).then_inc(xl_done, 1)

            def numerator(i):
                dve.wait_ge(a1_done, i.upto(1))
                dve.wait_ge(p_done, i.upto(CC * B))
                dve.tensor_tensor(num[:], A1[:], p_all[:, :, :, 0:TC], ALU.mult).then_inc(num_done, 1)
                dve.wait_ge(num_done, i.upto(2, 1))
                dve.wait_ge(bv_done, i.upto(1))
                dve.tensor_tensor(num[:], num[:], bv[:], ALU.add).then_inc(num_done, 1)

            def statistics(c):
                dve.wait_ge(res_done, c.upto(2))
                for j in range(J):
                    dve.bn_stats(stats[:, j, :], xres[c.slot][:, j // TH, j % TH, :]).then_inc(bn_done, 1)
                dve.wait_ge(bn_done, c.upto(J))
                take_wait(dve)
                for j in range(J):
                    dve.bn_aggr(mv[:, j, :], stats[:, j, :]).then_inc(mv_done, 1)

            def place(c):
                dve.wait_ge(rank_done, c.upto(1))
                dve.tensor_tensor(rank[:], rank_ps, region_no[:].unsqueeze(1).broadcast_to([P, J, E]), ALU.add).then_inc(slots, 1)
                dve.tensor_reduce(newly[:], picks[:].rearrange("p j e -> p e j"), AX.X, ALU.add).then_inc(slots, 1)
                dve.wait_ge(slots, c.upto(ROUTE2, 2))
                dve.tensor_tensor(spread[:], hot[:], rank[:].unsqueeze(2).broadcast_to([P, J, 2, E]), ALU.mult).then_inc(slots, 1)
                dve.wait_ge(slots, c.upto(ROUTE2, 3))
                dve.tensor_tensor(seen[:], seen[:], newly[:], ALU.add).then_inc(slots, 1)
                dve.wait_ge(slots, c.upto(ROUTE2, 4))
                dve.tensor_reduce(slot_f[:], spread[:], AX.X, ALU.add).then_inc(slots, 1)
                dve.wait_ge(slots, c.upto(ROUTE2, 5))
                dve.tensor_copy(slot_i[c.slot][:].rearrange("p (j k) -> p j k", j=J), slot_f[:]).then_inc(slots, 1)

            def label(c):
                dve.wait_ge(rec_out[c.slot], c.turn(REC_DMAS, BG))
                dve.tensor_copy(rec[c.slot][:, :, :, C:REC].bitcast(I32),
                                dest_all[:, bass.ds(c.number * (2 * J), 2 * J)].rearrange("p (j k a) -> p j k a", j=J, a=1)
                                ).then_inc(dest_done, 1)

            def residual_0(c):
                add_residual(c, 0)

            def residual_1(c):
                add_residual(c, 1)

            def add_residual(c, b):
                dve.wait_ge(wo_done, c.upto(2, b + 1))
                if b == 0:
                    dve.wait_ge(xres_in[c.slot], c.turn(16 * B, 16 * B))
                dve.tensor_tensor(xres[c.slot][:, b], wo_ps[:], xres[c.slot][:, b], ALU.add).then_inc(res_done, 1)

            def step(i):
                stages = [(stabilise, i), (divide, i - 1)]
                if i.fixed and i.number >= NCH - 1:
                    stages += [(accumulate, i), (residual_0, i - 1), (numerator, i), (residual_1, i - 1), (statistics, i - 1),
                               (choose, i - 2), (place, i - 2), (label, i - 1)]
                else:
                    stages += [(choose, i - 2), (residual_0, i - 1), (accumulate, i), (lower_halves, i + 2), (numerator, i),
                               (residual_1, i - 1), (statistics, i - 1), (place, i - 2), (label, i - 1)]
                for stage, c in stages:
                    if c.exists:
                        stage(c)

            chunks(dve, step)

            step_no = [0]

            def link(ins):
                step_no[0] += 1
                ins.then_inc(table, 1)
                dve.wait_ge(table, step_no[0])

            dve.wait_ge(made, 4)
            dve.wait_ge(cnt_done, 1)
            link(dve.tensor_copy(cnt_f[:], cnt_ps[0:1, :]))
            link(dve.tensor_tensor(pad_row[:], cnt_f[:], region_no[0:1, :], ALU.add))
            link(dve.tensor_scalar(cnt_i[:], cnt_f[:], float(BLK - 1), None, ALU.add))
            link(dve.tensor_scalar(tiles_i[:], cnt_i[:], BLK.bit_length() - 1, None, ALU.logical_shift_right))
            link(dve.tensor_copy(tiles_f[:], tiles_i[:]))
            link(dve.tensor_tensor_scan(ends_f[:], ones[0:1, 0:E], tiles_f[:], 0.0, ALU.mult, ALU.add))
            link(dve.tensor_tensor(starts_f[:], ends_f[:], tiles_f[:], ALU.subtract))
            link(dve.tensor_copy(ends[:], ends_f[:]))
            link(dve.scalar_tensor_tensor(out=rowbase[:], in0=starts_f[:], scalar=-float(BLK), in1=region_no[0:1, :],
                                          op0=ALU.mult, op1=ALU.add))
            over = lambda a: a[:].unsqueeze(1).broadcast_to([1, BLOCKS, E])
            link(dve.tensor_tensor(past_s[:], tile_f[:], over(starts_f), ALU.is_ge))
            link(dve.tensor_tensor(past_e[:], tile_f[:], over(ends_f), ALU.is_ge))
            link(dve.tensor_tensor(past_s[:], past_s[:], past_e[:], ALU.subtract))
            link(dve.tensor_tensor(past_s[:], past_s[:], over(rowbase), ALU.mult))
            link(dve.tensor_reduce(row_f[:], past_s[:], AX.X, ALU.add))
            link(dve.tensor_reduce(ex_f[:], past_e[:], AX.X, ALU.add))
            link(dve.tensor_scalar(real_f[:], ex_f[:], float(E), None, ALU.is_lt))
            link(dve.tensor_tensor(real_f[:], real_f[:], tile_row[:], ALU.mult))
            link(dve.scalar_tensor_tensor(out=row_t[:], in0=row_f[:], scalar=float(DUMMY), in1=real_f[:],
                                          op0=ALU.add, op1=ALU.add))
            link(dve.tensor_scalar(ex_t[:], ex_f[:], float(E - 1), None, ALU.min))
            link(dve.tensor_scalar(par_t[:], ex_t[:], 1, None, ALU.bitwise_and))
            dve.tensor_tensor(score_t[:, :, 0:1], top2[:].rearrange("p i j k -> p (i j) k")[:, :, 1:2],
                              top2[:].rearrange("p i j k -> p (i j) k")[:, :, 0:1], ALU.subtract).then_inc(score_done, 1)
            dve.tensor_copy(cnt_f[:], cnt_f[:]).then_inc(table_done, 1)
            phase_b_may_start(dve)

            def block_step(t):
                u = t - 1
                if u.exists:
                    expert = dve.value_load(ex_t[0:1, bass.ds(u.number, 1)], min_val=0, max_val=E - 1)
                    after(dve, y_out[u.slot], u.turn(16 * BH))
                    for h in range(BH):
                        dve.wait_ge(mm2_done, u.upto(BH, h + 1))
                        dve.tensor_tensor(y_sb[u.slot][:, h, :], y_ps[h], b2_b[:, bass.ds(expert * C, C)],
                                          ALU.add).then_inc(y_done, 1)
                u = t + 1
                if u.exists:
                    after(dve, mm2_done, (u - 2).upto(BH))
                    for b in range(FC // 2):
                        dve.wait_ge(aTh_done, u.upto(FC // 2, b + 1))
                        dve.tensor_tensor(aTl[u.slot % 2][:, 2 * b:2 * b + 2, :], act_T[0][:, 2 * b:2 * b + 2, :],
                                          aTh[u.slot % 2][:, 2 * b:2 * b + 2, :].bitcast(F32),
                                          ALU.subtract).then_inc(aTl_done, 1)
                u = t + 2
                if u.exists:
                    dve.wait_ge(tx_done, u.upto(1))
                    after(dve, mm1_done, (u - 2).upto(FC // 2))
                    dve.tensor_copy(xTh[u.slot % 2][:], xT2_ps[:]).then_inc(txh_done, 1)
                    after(dve, y_out[u.slot], u.turn(16 * BH))
                    dve.tensor_copy(dest[u.slot][:], recs[u.slot][:, :, C:REC].rearrange("p h a -> p (h a)").bitcast(I32)).then_inc(table, 1)
                    dve.wait_ge(txh_done, u.upto(1))
                    dve.tensor_tensor(xTl[u.slot % 2][:], xT2_ps[:], xTh[u.slot % 2][:].bitcast(F32),
                                      ALU.subtract).then_inc(txl_done, 1)

            dve.wait_ge(exp_done, 1)
            link(dve.tensor_scalar(score[:, :, 1:2], score_t[:, :, 0:1], 1.0, None, ALU.add))
            link(dve.reciprocal(score[:, :, 0:1], score[:, :, 1:2]))
            link(dve.tensor_tensor(score[:, :, 1:2], score_t[:, :, 0:1], score[:, :, 0:1], ALU.mult))
            dve.wait_ge(bias_in, 16)

            blocks(dve, block_step)

            dve.wait_ge(xx_in, 16 * B)

            def out_step(i):
                n = i.slot % 2
                dve.wait_ge(yy_in[i.slot], i.turn(16, 16))
                after(dve, c_res, (i - 2).upto(B))
                flat = score[:].rearrange("p n k -> p (n k)")
                for k in range(2):
                    for b in range(B):
                        if i.fixed:
                            column = (i.off // TH * J + b * TH + i.off % TH) * 2 + k
                        else:
                            column = i.m * (i.every // TH * J * 2) + ((i.off // TH * J + b * TH + i.off % TH) * 2 + k)
                        dve.scalar_tensor_tensor(
                            out=zz[n][:, b, :], in0=yy[i.slot][:, b, k * C:(k + 1) * C], scalar=flat[:, bass.ds(column, 1)],
                            in1=xx[:, bass.ds(i.number, 1), b, :].rearrange("p a c -> p (a c)") if k == 0 else zz[n][:, b, :],
                            op0=ALU.mult, op1=ALU.add).then_inc(c_sum, 1)
                    dve.wait_ge(c_sum, i.upto(2 * B, (k + 1) * B))
                for b in range(B):
                    dve.bn_stats(stats[:, b, :], zz[n][:, b, :]).then_inc(c_bn, 1)
                dve.wait_ge(c_bn, i.upto(B))
                after(dve, c_rstd, (i - 2).upto(1))
                take_wait(dve)
                for b in range(B):
                    dve.bn_aggr(mv_c[n][:, b, :], stats[:, b, :]).then_inc(c_mv, 1)

            pieces(dve, out_step)


INPUTS = ["L0_attn_x", "L0_attn_time_decay", "L0_attn_time_first", "L0_attn_time_mix_k", "L0_attn_time_mix_v",
          "L0_attn_time_mix_r", "L0_attn_Wk", "L0_attn_Wv", "L0_attn_Wr", "L0_attn_Wo", "L0_ffn_W1", "L0_ffn_b1",
          "L0_ffn_W2", "L0_ffn_b2", "L0_ffn_Wg", "L0_ffn_bg"]
TRANSPOSED = {"L0_attn_Wk", "L0_attn_Wv", "L0_attn_Wr", "L0_attn_Wo"}


def kernel(**inputs):
    import concourse.bacc as bacc
    from concourse.bass_utils import run_bass_kernel_spmd

    nc = bacc.Bacc("TRN2", target_bir_lowering=False, num_devices=1)
    arrays, aps = {}, []
    for name in INPUTS:
        a = np.asarray(inputs[name])
        a = np.ascontiguousarray(a.T if name in TRANSPOSED else a)
        arrays[f"in_{name}"] = a
        aps.append(nc.dram_tensor(f"in_{name}", a.shape, mybir.dt.from_np(a.dtype), kind="ExternalInput").ap())
    shape = arrays["in_L0_attn_x"].shape
    aps.append(nc.dram_tensor("out", shape, F32, kind="ExternalOutput").ap())
    build(nc, *aps)
    return run_bass_kernel_spmd(nc, [arrays], core_ids=[0]).results[0]["out"]
```

```python
from contextlib import ExitStack, nullcontext

import numpy as np

import concourse.bass as bass
from concourse import mybir

ALU = mybir.AluOpType
ACT = mybir.ActivationFunctionType
AX = mybir.AxisListType
F32 = mybir.dt.float32
F32R = mybir.dt.float32r
I32 = mybir.dt.int32
U32 = mybir.dt.uint32

P = 128


class Step:

    def __init__(self, m, off, every, count, stop=0):
        self.m, self.off, self.every, self.count, self.stop = m, off, every, count, stop

    def __add__(self, k):
        return Step(self.m, self.off + k, self.every, self.count, self.stop)

    def __sub__(self, k):
        return self + -k

    @property
    def fixed(self):
        return self.m is None

    @property
    def number(self):
        return self.off if self.fixed else self.m * self.every + self.off

    @property
    def exists(self):
        return not self.fixed or 0 <= self.off < self.count

    @property
    def largest(self):
        return self.off if self.fixed else (self.stop - 1) * self.every + self.off

    @property
    def slot(self):
        return self.off % self.every

    def turn(self, n=1, more=0):
        if self.fixed:
            return self.off // self.every * n + more
        return self.m * n + (self.off // self.every * n + more)

    def upto(self, each, n=None):
        n = each if n is None else n
        if self.fixed:
            return self.off * each + n
        return self.m * (self.every * each) + (self.off * each + n)


def build(nc, x, decay, first, mix_k, mix_v, mix_r, wkT, wvT, wrT, woT, w1, b1, w2, b2, wgT, bg, out):
    B, T, C = x.shape
    E, _, F = w1.shape
    CC = C // P
    TC = 256
    NCH = T // TC
    TH = TC // P
    J = B * TH
    N = B * TC
    W = CC * N
    TOKENS = B * T
    BLK = 256
    BH = BLK // P
    BLOCKS = (2 * TOKENS + E * (BLK - 1)) // BLK
    ALWAYS = 2 * TOKENS // BLK
    REGION = TOKENS + BLK
    DUMMY = E * REGION
    REC = C + 1
    NOWHERE = 1 << 20
    FC = F // P
    PIECES = T // P
    RING = 4
    W1E, W2E = CC * F, FC * C
    WE = W1E + W2E
    LOWEST = -1e38
    EPS = 1e-5

    xs = nc.dram_tensor("records_dram", (DUMMY + BLK, REC), F32, kind="Internal").ap()
    ys = nc.dram_tensor("expert_out_dram", (2 * TOKENS, C), F32, kind="Internal").ap()
    x1d = nc.dram_tensor("x1_dram", (B, T, C), F32, kind="Internal").ap()

    with ExitStack() as ctx:
        def sb(name, shape, dt=F32, where=ctx):
            return where.enter_context(nc.sbuf_tensor(name, shape, dt))

        def sem(name):
            return ctx.enter_context(nc.semaphore(name))

        ident = sb("ident", [P, P])
        before = sb("before", [P, P])
        ones = sb("ones", [P, P])
        consts_c = sb("consts_c", [P, 5 * CC])
        mix_c = consts_c[:, 0:3 * CC].rearrange("p (n c) -> p n c", n=3)
        decay_c = consts_c[:, 3 * CC:4 * CC]
        first_c = consts_c[:, 4 * CC:5 * CC]
        b1_c = sb("b1_c", [P, E * FC])
        unmix_c = sb("unmix_c", [P, 3, CC])
        bg_b = sb("bg_b", [P, E])
        expert_no = sb("expert_no", [P, E])
        region_no = sb("region_no", [P, E])
        dest_all = sb("dest_all", [P, NCH * J * 2], I32)
        half_neg = sb("half_neg", [P, J])
        eps_b = sb("eps_b", [P, J])
        top2 = sb("top2", [P, NCH, J, 2])
        score = sb("score", [P, NCH * J, 2])
        score_t = sb("score_t", [P, NCH * J, 2])
        pad_rec = sb("pad_rec", [P, REC])
        cnt_f = sb("cnt_f", [1, E])
        cnt_i = sb("cnt_i", [1, E], I32)
        blocks_i = sb("blocks_i", [1, E], I32)
        blocks_f = sb("blocks_f", [1, E])
        ends_f = sb("ends_f", [1, E])
        starts_f = sb("starts_f", [1, E])
        rowbase = sb("rowbase", [1, E])
        pad_row = sb("pad_row", [1, E], I32)
        ends = sb("ends", [1, E], I32)
        RECS = J * 2 * REC
        staging = sb("staging", [P, max(WE, 2 * RECS)])
        raw = staging[:, 0:WE]
        rec = [staging[:, n * RECS:(n + 1) * RECS].rearrange("p (j k c) -> p j k c", j=J, k=2) for n in range(2)]
        block_f = sb("block_f", [1, BLOCKS, E])
        past_s = sb("past_s", [1, BLOCKS, E])
        past_e = sb("past_e", [1, BLOCKS, E])
        block_row = sb("block_row", [1, BLOCKS])
        row_f = sb("row_f", [1, BLOCKS])
        ex_f = sb("ex_f", [1, BLOCKS])
        real_f = sb("real_f", [1, BLOCKS])
        row_t = sb("row_t", [1, BLOCKS], I32)
        ex_t = sb("ex_t", [1, BLOCKS], I32)
        par_t = sb("par_t", [1, BLOCKS], I32)
        rest_f = sb("rest_f", [1, BLOCKS])
        restbase = sb("restbase", [1, E])
        full_t = sb("full_t", [1, BLOCKS], I32)
        var_e = sb("var_e", [P, J])
        rstd = sb("rstd", [P, 2, J])
        shift = sb("shift", [P, 2, J])
        neg_mean = sb("neg_mean", [P, J])
        stats = sb("stats", [P, J, 6])
        mv = sb("mv", [P, J, 2])

        phase_a = ExitStack()
        sb("w_slot0_place", [P, 2 * WE], F32, phase_a)
        xin = [sb(f"xin{n}", [P, B, TH, C], F32, phase_a) for n in range(2)]
        xres = [sb(f"xres{n}", [P, B, TH, C], F32, phase_a) for n in range(2)]
        xh = [sb(f"xh{n}", [P, CC, B, TC + 2], F32R, phase_a) for n in range(2)]
        xl = [sb(f"xl{n}", [P, CC, B, TC + 2], F32R, phase_a) for n in range(2)]
        wq = sb("wq", [P, 3, 2, 2, CC, C], F32R, phase_a)
        wo = sb("wo", [P, CC, C], F32, phase_a)
        wg = sb("wg", [P, CC, E], F32, phase_a)
        w_row = sb("w_row", [P, CC, TC], F32, phase_a)
        o_all = sb("o_all", [P, CC, B, TC + 1], F32, phase_a)
        p_all = sb("p_all", [P, CC, B, TC + 1], F32, phase_a)
        q_all = sb("q_all", [P, CC, B, TC + 1], F32, phase_a)
        s_buf = sb("s_buf", [P, CC, B, TC], F32, phase_a)
        A1 = sb("A1", [P, CC, B, TC], F32, phase_a)
        B1 = sb("B1", [P, CC, B, TC], F32, phase_a)
        A2 = sb("A2", [P, CC, B, TC], F32, phase_a)
        B2 = sb("B2", [P, CC, B, TC], F32, phase_a)
        v = [sb(f"v{n}", [P, CC, B, TC], F32, phase_a) for n in range(2)]
        gate = [sb(f"gate{n}", [P, CC, B, TC], F32, phase_a) for n in range(2)]
        b2v = sb("b2v", [P, CC, B, TC], F32, phase_a)
        bv = sb("bv", [P, CC, B, TC], F32, phase_a)
        num = sb("num", [P, CC, B, TC], F32, phase_a)
        den = sb("den", [P, CC, B, TC], F32, phase_a)
        r0 = sb("r0", [P, CC, B, TC], F32, phase_a)
        newton = sb("newton", [P, CC, B, TC], F32, phase_a)
        mixed = newton
        wraw = [s_buf, A1, B1]
        wscaled = [num, den, r0]
        const_rows = sb("const_rows", [5 * CC, P], F32, phase_a)
        b1_rows = sb("b1_rows", [E * FC, P], F32, phase_a)
        x1T = sb("x1T", [P, CC, N], F32, phase_a)
        m8 = sb("m8", [P, J, 8], F32, phase_a)
        i8 = sb("i8", [P, J, 8], U32, phase_a)
        idxf = sb("idxf", [P, J, 2], F32, phase_a)
        hot = sb("hot", [P, J, 2, E], F32, phase_a)
        seen = sb("seen", [P, E], F32, phase_a)
        newly = sb("newly", [P, E], F32, phase_a)
        picks = sb("picks", [P, J, E], F32, phase_a)
        rank = sb("rank", [P, J, E], F32, phase_a)
        spread = sb("spread", [P, J, 2, E], F32, phase_a)
        slot_f = sb("slot_f", [P, J, 2], F32, phase_a)
        slot_i = [sb(f"slot_i{n}", [P, J * 2], I32, phase_a) for n in range(2)]

        def ps(name, shape, where):
            return where.enter_context(nc.psum_tensor(name, shape, F32))

        xT_ps = ps("xT_ps", [P, CC, N], phase_a)
        k_ps = ps("k_ps", [P, CC, N], phase_a)
        vr_ps = [ps(f"vr_ps{n}", [P, N], phase_a) for n in range(2)]
        wo_ps = ps("wo_ps", [P, TH, C], phase_a)
        small_ps = ps("small_ps", [P, 512], phase_a)
        lg_ps = small_ps[:, 0:J * E].rearrange("p (j e) -> p j e", j=J)
        rank_ps = small_ps[:, 64:64 + J * E].rearrange("p (j e) -> p j e", j=J)
        cnt_ps = small_ps[:, 128:128 + E]
        phase_a.close()

        wx = sb("wx", [P, 2, 2, WE], F32R)
        xx = sb("xx", [P, PIECES, B, C])
        phase_b = ExitStack()
        b2_b = sb("b2_b", [P, E * C], F32, phase_b)
        recs = [sb(f"recs{n}", [P, BH, REC], F32, phase_b) for n in range(RING)]
        dest = [sb(f"dest{n}", [P, BH], I32, phase_b) for n in range(RING)]
        xTh = [sb(f"xTh{n}", [P, CC, BLK], F32R, phase_b) for n in range(2)]
        xTl = [sb(f"xTl{n}", [P, CC, BLK], F32R, phase_b) for n in range(2)]
        act_T = sb("act_T", [P, FC, BLK], F32, phase_b)
        aTh = [sb(f"aTh{n}", [P, FC, BLK], F32R, phase_b) for n in range(2)]
        aTl = [sb(f"aTl{n}", [P, FC, BLK], F32R, phase_b) for n in range(2)]
        y_sb = [sb(f"y_sb{n}", [P, BH, C], F32, phase_b) for n in range(RING)]
        hT_ps = [ps(f"hT_ps{n}", [P, 2, BLK], phase_b) for n in range(FC // 2)]
        xT2_ps = ps("xT2_ps", [P, CC, BLK], phase_b)
        y_ps = [ps(f"y_ps{n}", [P, 512], phase_b)[:, 0:C] for n in range(BH)]
        phase_b.close()
        yy = [sb(f"yy{n}", [P, B, 2 * C]) for n in range(RING)]
        zz = [sb(f"zz{n}", [P, B, C]) for n in range(RING)]
        res = [sb(f"res{n}", [P, B, C]) for n in range(RING)]
        y2 = [sb(f"y2_{n}", [P, B, C]) for n in range(RING)]
        stats_c = [sb(f"stats_c{n}", [P, B, 6]) for n in range(RING)]
        mv_c = [sb(f"mv_c{n}", [P, B, 2]) for n in range(RING)]
        rstd_c = [sb(f"rstd_c{n}", [P, B]) for n in range(RING)]
        shift_c = [sb(f"shift_c{n}", [P, B]) for n in range(RING)]

        carried = sem("carried")
        bias1_done, top2_done = sem("bias1_done"), sem("top2_done")
        consts_in, gate_in, raw_in = sem("consts_in"), sem("gate_in"), sem("raw_in")
        weights_in = [sem(f"weights_in{n}") for n in range(3)]
        consts_turned = sem("consts_turned")
        made, made2, padded = sem("made"), sem("made2"), sem("padded")
        setup_act, setup_dve = sem("setup_act"), sem("setup_dve")
        scaled = [sem(f"scaled{n}") for n in range(3)]
        w_hi, w_lo = sem("w_hi"), sem("w_lo")
        xin_in = [sem(f"xin_in{n}") for n in range(2)]
        xres_in = [sem(f"xres_in{n}") for n in range(2)]
        xT_done, xh_done, xl_done = sem("xT_done"), sem("xh_done"), sem("xl_done")
        vr_done, k_done, v_out, gate_out = sem("vr_done"), sem("k_done"), sem("v_out"), sem("gate_out")
        o_carry, o_done, s_done, d3_done, d2_done = (sem(n) for n in ("o_carry", "o_done", "s_done", "d3_done", "d2_done"))
        relu_done, a1_done, b1_done, a2_done, b2_done = (sem(n) for n in ("relu_done", "a1_done", "b1_done", "a2_done", "b2_done"))
        qp_carry, q_done, p_done = sem("qp_carry"), sem("q_done"), sem("p_done")
        b2v_done, bv_done, aq_done, den_done, num_done = (sem(n) for n in ("b2v_done", "bv_done", "aq_done", "den_done", "num_done"))
        ln_done, r0_done, div_done, mixed_done = sem("ln_done"), sem("r0_done"), sem("div_done"), sem("mixed_done")
        wo_done, res_done, bn_done, mv_done = sem("wo_done"), sem("res_done"), sem("bn_done"), sem("mv_done")
        vare_done, rstd_done, x1_done, rec2_done = sem("vare_done"), sem("rstd_done"), sem("x1_done"), sem("rec2_done")
        dest_done, cnt_done = sem("dest_done"), sem("cnt_done")
        x1T_done, x1T_out, lg_done = sem("x1T_done"), sem("x1T_out"), sem("lg_done")
        route, rank_done, slots = sem("route"), sem("rank_done"), sem("slots")
        rec_out = [sem(f"rec_out{n}") for n in range(2)]
        x1_out = [sem(f"x1_out{n}") for n in range(2)]
        table, table_done, pads_out = sem("table"), sem("table_done"), sem("pads_out")
        bias_in, hi_done, weights_ready = sem("bias_in"), sem("hi_done"), sem("weights_ready")
        bias1_in, bias1_turned = sem("bias1_in"), sem("bias1_turned")
        rec_in = [sem(f"rec_in{n}") for n in range(RING)]
        y_out = [sem(f"y_out{n}") for n in range(RING)]
        tx_done, txh_done, txl_done = sem("tx_done"), sem("txh_done"), sem("txl_done")
        mm1_done, act_done = sem("mm1_done"), sem("act_done")
        aTh_done, aTl_done = sem("aTh_done"), sem("aTl_done")
        mm2_done, y_done = [sem(f"mm2_done{n}") for n in range(BH)], sem("y_done")
        exp_done, score_done = sem("exp_done"), sem("score_done")
        yy_in = [sem(f"yy_in{n}") for n in range(RING)]
        res_out = [sem(f"res_out{n}") for n in range(RING)]
        xx_in, y2_done, c_sum2 = sem("xx_in"), sem("y2_done"), sem("c_sum2")
        c_sum, c_bn, c_mv, c_var, c_rstd, c_res = (sem(n) for n in ("c_sum", "c_bn", "c_mv", "c_var", "c_rstd", "c_res"))

        BG = 16
        REC_DMAS = 2 * J * 16
        ROUTE1, ROUTE2 = 2 * J + 3, 6

        def chunks(eng, body):
            plain = lambda n: Step(None, n, 2, NCH)
            for n in range(-2, 2):
                body(plain(n))
            with eng.Fori(1, NCH // 2 - 1) as m:
                body(Step(m, 0, 2, NCH))
                body(Step(m, 1, 2, NCH))
            for n in range(NCH - 2, NCH + 2):
                body(plain(n))

        LAST = ALWAYS // RING * RING

        def blocks(eng, body):
            plain = lambda n: Step(None, n, RING, BLOCKS)
            for n in range(-2, RING):
                body(plain(n))
            with eng.Fori(1, LAST // RING) as m:
                for n in range(RING):
                    body(Step(m, n, RING, BLOCKS, LAST // RING))
            for n in range(LAST, BLOCKS + 1):
                body(plain(n))

        def blocks_in_use(eng):
            return eng.value_load(ends[0:1, E - 1:E], min_val=ALWAYS, max_val=BLOCKS)

        def if_used(eng, used, u):
            return eng.If(used > u.number) if u.largest >= ALWAYS else nullcontext()

        def pieces(eng, body):
            for n in range(RING):
                body(Step(None, n, RING, PIECES))
            with eng.Fori(1, PIECES // RING) as m:
                for n in range(RING):
                    body(Step(m, n, RING, PIECES))

        def column(i, b, k):
            at = (i.off // TH * J + b * TH + i.off % TH) * 2 + k
            return at if i.fixed else i.m * (i.every // TH * J * 2) + at

        def after(eng, semaphore, value):
            if not isinstance(value, int) or value > 0:
                eng.wait_ge(semaphore, value)

        def take_wait(eng):
            eng.sem_inc(carried, 1)

        def load_chunk(sp, to, ap, i, done):
            for b in range(B):
                sp.dma_start(to[:, b], ap[b, bass.ds(i.number * TC, TC), :].rearrange("(h p) c -> p h c", p=P)).then_inc(done, 16)

        def store_chunk(sp, ap, i, rows, done):
            for b in range(B):
                sp.dma_start(ap[b, bass.ds(i.number * TC, TC), :].rearrange("(h p) c -> p h c", p=P), rows[:, b]).then_inc(done, 16)

        def phase_b_may_start(eng):
            eng.wait_ge(table_done, 1)
            for n in range(2):
                eng.wait_ge(rec_out[n], NCH // 2 * REC_DMAS + BG)
                eng.wait_ge(x1_out[n], NCH // 2 * B * 16 + BG)

        def wscaled_of(n):
            return wscaled[n][:].rearrange("p c b t -> p (c b t)").rearrange("p (a c d) -> p a c d", a=2, c=CC)

        def scale_matrix(eng, n):
            eng.wait_ge(weights_in[n], 16)
            src = wraw[n][:].rearrange("p c b t -> p (c b t)")
            for a, factor in ((0, unmix_c), (1, mix_c)):
                for cc in range(CC):
                    eng.tensor_scalar(wscaled_of(n)[:, a, cc, :], src[:, cc * C:(cc + 1) * C], factor[:, n, cc:cc + 1], 0.0,
                                      ALU.mult, ALU.add).then_inc(scaled[n], 1)

        block = ctx.enter_context(nc.Block())

        @block.sync
        def _(sp):
            plain = lambda n: Step(None, n, 2, NCH)
            for n, row in enumerate([m.rearrange("a b (c p) -> (a b c) p", p=P) for m in (mix_v, mix_r, mix_k)] +
                                    [v.rearrange("(c p) -> c p", p=P) for v in (decay, first)]):
                sp.dma_start(const_rows[n * CC:(n + 1) * CC, :], row).then_inc(consts_in, 16)

            def load_matrix(n, w):
                sp.dma_start(wraw[n][:].rearrange("p c b t -> p (c b t)")[:, 0:CC * C].rearrange("p (c d) -> p c d", c=CC),
                             w.rearrange("(c p) d -> p c d", p=P)).then_inc(weights_in[n], 16)

            load_matrix(0, wvT)
            load_chunk(sp, xin[0], x, plain(0), xin_in[0])
            load_matrix(1, wrT)
            load_matrix(2, wkT)
            sp.dma_start(bg_b[:], bg.rearrange("(a e) -> a e", a=1).broadcast_to([P, E])).then_inc(gate_in, 16)
            sp.dma_start(b1_rows[:], b1.rearrange("e (c p) -> (e c) p", p=P)).then_inc(bias1_in, 16)
            load_chunk(sp, xin[1], x, plain(1), xin_in[1])
            sp.dma_start(wo[:], woT.rearrange("(c p) d -> p c d", p=P)).then_inc(gate_in, 16)
            sp.dma_start(wg[:], wgT.rearrange("(c p) e -> p c e", p=P)).then_inc(gate_in, 16)

            def load_raw(e):
                sp.dma_start(raw[:, 0:W1E].rearrange("p (c f) -> p c f", c=CC),
                             w1[e].rearrange("(c p) f -> p c f", p=P)).then_inc(raw_in, 16)
                sp.dma_start(raw[:, W1E:WE].rearrange("p (c d) -> p c d", c=FC),
                             w2[e].rearrange("(c p) d -> p c d", p=P)).then_inc(raw_in, 16)

            load_raw(0)
            sp.wait_ge(padded, 2)
            for n in range(2):
                sp.dma_start(xs[DUMMY + 128 + 64 * n:DUMMY + 192 + 64 * n, :], pad_rec[64 * n:64 * n + 64, :]).then_inc(x1_out[n], 16)

            def step(i):
                c = i + 2
                if c.exists and (c - 2).exists:
                    sp.wait_ge(xT_done, (c - 2).upto(CC))
                    load_chunk(sp, xin[c.slot], x, c, xin_in[c.slot])
                if (i - 2).exists:
                    sp.wait_ge(x1_done, (i - 2).upto(J))
                if i.exists:
                    load_chunk(sp, xres[i.slot], x, i, xres_in[i.slot])
                c = i - 2
                if c.exists:
                    store_chunk(sp, x1d, c, rec[c.slot][:, :, 0, 0:C].rearrange("p (b h) c -> p b h c", b=B), x1_out[c.slot])

            chunks(sp, step)
            sp.wait_ge(table, 2)
            for e in range(E):
                row = sp.value_load(pad_row[0:1, e:e + 1], min_val=0, max_val=DUMMY - BLK)
                sp.dma_start(xs[bass.ds(row, BLK), :].rearrange("(h p) c -> p h c", p=P),
                             pad_rec[:].unsqueeze(1).broadcast_to([P, BH, REC])).then_inc(pads_out, 16)
            phase_b_may_start(sp)
            sp.wait_ge(weights_ready, 1)
            sp.wait_ge(rec_in[0], 16)
            load_raw(1)
            sp.dma_start(b2_b[:], b2.rearrange("(a e) c -> a (e c)", a=1).broadcast_to([P, E * C])).then_inc(bias_in, 16)
            for e in range(2, E):
                sp.wait_ge(weights_ready, e)
                load_raw(e)
                if e == 2:
                    for b in range(B):
                        sp.dma_start(xx[:, :, b, :], x1d[b].rearrange("(q p) c -> p q c", p=P)).then_inc(xx_in, 16)
            used = blocks_in_use(sp)
            for n in range(RING):
                sp.wait_ge(y_out[n], -((n - ALWAYS) // RING) * 16 * BH)
            for n in range(ALWAYS, BLOCKS):
                with sp.If(used > n):
                    sp.wait_ge(y_out[n % RING], (n // RING + 1) * 16 * BH)
            ys_t = ys.rearrange("(b t k) c -> b t (k c)", b=B, k=2)

            def load_outputs(i):
                sp.dma_start(yy[i.slot][:], ys_t[:, bass.ds(i.number * P, P), :].rearrange("b p c -> p b c")).then_inc(yy_in[i.slot], 16)

            def store_results(i):
                sp.wait_ge(c_res, i.upto(B))
                sp.dma_start(out[:, bass.ds(i.number * P, P), :].rearrange("b p c -> p b c"), res[i.slot][:]).then_inc(res_out[i.slot], 16)

            for n in range(RING):
                load_outputs(Step(None, n, RING, PIECES))

            def turn_over(i):
                sp.wait_ge(c_sum, i.upto(B))
                sp.wait_ge(y2_done, i.upto(B))
                load_outputs(i + RING)
                if (i - 2).exists:
                    store_results(i - 2)

            for n in range(RING):
                turn_over(Step(None, n, RING, PIECES))
            with sp.Fori(1, PIECES // RING - 1) as m:
                for n in range(RING):
                    turn_over(Step(m, n, RING, PIECES))
            for n in range(PIECES - RING - 2, PIECES):
                store_results(Step(None, n, RING, PIECES))
            for n in range(RING):
                sp.wait_ge(res_out[n], PIECES // RING * 16)

        @block.gpsimd
        def _(pool):
            pool.memset(ident[:], 0.0).then_inc(made, 1)
            pool.memset(before[:], 1.0).then_inc(made, 1)
            pool.memset(ones[:], 1.0).then_inc(made2, 1)
            pool.memset(half_neg[:], -0.5).then_inc(made2, 1)
            pool.memset(eps_b[:], EPS).then_inc(made2, 1)
            pool.wait_ge(made, 2)
            pool.affine_select(out=ident[:], in_=ident[:], compare_op=ALU.not_equal, fill=1.0, base=0,
                               pattern=[[-1, P]], channel_multiplier=1).then_inc(made2, 1)
            pool.affine_select(out=before[:], in_=before[:], compare_op=ALU.is_gt, fill=0.0, base=0,
                               pattern=[[1, P]], channel_multiplier=-1).then_inc(made2, 1)
            pool.iota(expert_no[:], [[1, E]], base=0, channel_multiplier=0,
                      allow_small_or_imprecise_dtypes=True).then_inc(made2, 1)
            pool.iota(region_no[:], [[REGION, E]], base=0, channel_multiplier=0,
                      allow_small_or_imprecise_dtypes=True).then_inc(made2, 1)
            for i in range(NCH):
                pool.iota(dest_all[:, i * 2 * J:(i + 1) * 2 * J], [[2 * T, B], [2 * P, TH], [1, 2]],
                          base=2 * TC * i, channel_multiplier=2).then_inc(made2, 1)
            pool.memset(xh[0][:, :, :, 0:1].bitcast(F32), 0.0).then_inc(xh_done, 1)
            pool.memset(xl[0][:, :, :, 0:1].bitcast(F32), 0.0).then_inc(xl_done, 1)
            pool.memset(pad_rec[:, 0:C], 0.0).then_inc(padded, 1)
            pool.memset(pad_rec[:, C:REC].bitcast(I32), NOWHERE).then_inc(padded, 1)

            def split(e):
                pool.wait_ge(raw_in, 32 * (e + 1))
                pool.tensor_scalar(wx[:, e % 2, 0, :], raw, 1.0, 0.0, ALU.mult, ALU.add).then_inc(hi_done, 1)
                pool.wait_ge(hi_done, e + 1)
                pool.tensor_tensor(wx[:, e % 2, 1, :], raw, wx[:, e % 2, 0, :].bitcast(F32),
                                   ALU.subtract).then_inc(weights_ready, 1)

            pool.wait_ge(setup_dve, 2)
            scale_matrix(pool, 1)
            scale_matrix(pool, 2)
            pool.iota(block_f[:], [[1, BLOCKS], [0, E]], base=0, channel_multiplier=0,
                      allow_small_or_imprecise_dtypes=True).then_inc(made, 1)
            pool.iota(block_row[:], [[BLK, BLOCKS]], base=-DUMMY, channel_multiplier=0,
                      allow_small_or_imprecise_dtypes=True).then_inc(made, 1)
            pool.wait_ge(padded, 2)
            for n in range(2):
                pool.dma_start(xs[DUMMY + 64 * n:DUMMY + 64 * n + 64, :], pad_rec[64 * n:64 * n + 64, :]).then_inc(rec_out[n], 16)
            pool.wait_ge(raw_in, 32)
            pool.tensor_scalar(wx[:, 0, 0, :], raw, 1.0, 0.0, ALU.mult, ALU.add).then_inc(hi_done, 1)
            pool.wait_ge(hi_done, 1)
            pool.tensor_tensor(wx[:, 0, 1, :], raw, wx[:, 0, 0, :].bitcast(F32), ALU.subtract).then_inc(weights_ready, 1)

            def step(i):
                if i.exists:
                    pool.wait_ge(b2_done, i.upto(1))
                    pool.wait_ge(v_out, i.upto(CC))
                    after(pool, p_done, (i - 1).upto(CC * B))
                    pool.tensor_tensor(b2v[:], B2[:], v[i.slot][:], ALU.mult).then_inc(b2v_done, 1)
                    pool.wait_ge(b1_done, i.upto(1))
                    after(pool, num_done, (i - 1).upto(2))
                    pool.tensor_tensor(bv[:], B1[:], v[i.slot][:], ALU.mult).then_inc(bv_done, 1)
                    pool.wait_ge(a1_done, i.upto(1))
                    pool.wait_ge(q_done, i.upto(CC * B))
                    after(pool, mixed_done, (i - 1).upto(B))
                    pool.tensor_tensor(den[:], A1[:], q_all[:, :, :, 0:TC], ALU.mult).then_inc(aq_done, 1)
                    pool.wait_ge(aq_done, i.upto(1))
                    pool.tensor_tensor(den[:], den[:], B1[:], ALU.add).then_inc(den_done, 1)
                c = i - 1
                if c.exists:
                    pool.wait_ge(mv_done, c.upto(J))
                    pool.tensor_tensor(var_e[:], mv[:, :, 1], eps_b[:], ALU.add).then_inc(vare_done, 1)
                    pool.tensor_scalar(neg_mean[:], mv[:, :, 0], -1.0, 0.0, ALU.mult, ALU.add).then_inc(vare_done, 1)
                    pool.wait_ge(vare_done, c.upto(3, 2))
                    pool.tensor_tensor(rstd[:, c.slot, :], var_e[:], half_neg[:], ALU.pow).then_inc(vare_done, 1)
                    pool.wait_ge(vare_done, c.upto(3))
                    pool.tensor_tensor(shift[:, c.slot, :], neg_mean[:], rstd[:, c.slot, :], ALU.mult).then_inc(rstd_done, 1)
                c = i - 2
                if c.exists:
                    pool.wait_ge(slots, c.upto(ROUTE2))
                    pool.wait_ge(rec2_done, c.upto(1))
                    pool.wait_ge(dest_done, c.upto(1))
                    take_wait(pool)
                    for j in range(J):
                        for k in range(2):
                            n = 2 * j + k
                            pool.indirect_dma_start(
                                xs, bass.IndirectOffsetOnAxis(ap=slot_i[c.slot][:, n:n + 1], axis=0),
                                rec[c.slot][:, j, k, :], None, bounds_check=DUMMY - 1,
                                oob_is_err=False).then_inc(rec_out[c.slot], 16)

            chunks(pool, step)

            phase_b_may_start(pool)
            split(1)
            used = blocks_in_use(pool)
            end = [pool.value_load(ends[0:1, e:e + 1], min_val=0, max_val=BLOCKS) for e in range(E - 2)]

            def scatter(t):
                for e in range(2, E):
                    with pool.If(end[e - 2] == t.number):
                        split(e)
                with if_used(pool, used, t):
                    for h in range(BH):
                        pool.wait_ge(y_done, t.upto(BH, h + 1))
                        take_wait(pool)
                        pool.indirect_dma_start(
                            ys, bass.IndirectOffsetOnAxis(ap=dest[t.slot][:, h:h + 1], axis=0), y_sb[t.slot][:, h, :], None,
                            bounds_check=2 * TOKENS - 1, oob_is_err=False).then_inc(y_out[t.slot], 16)

            with pool.Fori(0, ALWAYS // RING) as m:
                for n in range(RING):
                    scatter(Step(m, n, RING, BLOCKS, ALWAYS // RING))
            for n in range(ALWAYS // RING * RING, BLOCKS):
                scatter(Step(None, n, RING, BLOCKS))

            def norm_step(i):
                n = i.slot
                pool.wait_ge(c_mv, i.upto(B))
                after(pool, c_res, (i - RING).upto(B))
                after(pool, c_rstd, (i - 1).upto(1))
                pool.tensor_tensor(var_e[:, 0:B], mv_c[n][:, :, 1], eps_b[:, 0:B], ALU.add).then_inc(c_var, 1)
                pool.tensor_scalar(neg_mean[:, 0:B], mv_c[n][:, :, 0], -1.0, 0.0, ALU.mult, ALU.add).then_inc(c_var, 1)
                pool.wait_ge(c_var, i.upto(3, 2))
                pool.tensor_tensor(rstd_c[n][:], var_e[:, 0:B], half_neg[:, 0:B], ALU.pow).then_inc(c_var, 1)
                pool.wait_ge(c_var, i.upto(3))
                pool.tensor_tensor(shift_c[n][:], neg_mean[:, 0:B], rstd_c[n][:], ALU.mult).then_inc(c_rstd, 1)

            pieces(pool, norm_step)

        @block.tensor
        def _(pe):
            pe.wait_ge(made2, 7 + NCH)
            pe.wait_ge(consts_in, 5 * 16)
            pe.transpose(small_ps[:, 256:256 + 5 * CC], const_rows[:], ident[0:5 * CC, 0:5 * CC]).then_inc(consts_turned, 1)

            def turn_biases():
                pe.wait_ge(bias1_in, 16)
                pe.wait_ge(setup_dve, 1)
                pe.transpose(small_ps[:, 256:256 + E * FC], b1_rows[:], ident[0:E * FC, 0:E * FC]).then_inc(bias1_turned, 1)

            def transpose_x(c):
                pe.wait_ge(xin_in[c.slot], c.turn(16 * B, 16 * B))
                after(pe, xl_done, (c - 1).upto(CC + 1))
                if (c - 4).exists:
                    pe.wait_ge(x1T_out, (c - 4).upto(CC))
                for cc in range(CC):
                    for j in range(J):
                        ins = pe.transpose(xT_ps[:, cc, j * P:(j + 1) * P],
                                           xin[c.slot][:, j // TH, j % TH, cc * P:(cc + 1) * P], ident[:])
                    ins.then_inc(xT_done, 1)

            def project(c, mat, oc, out_ps):
                terms = [(cc, now, a, b) for cc in range(CC) for now in range(2)
                         for a, b in ((0, xh), (0, xl), (1, xh))]
                for n, (cc, now, part, xpart) in enumerate(terms):
                    ins = pe.matmul(out_ps.rearrange("p (b t) -> p b t", b=B), wq[:, mat, now, part, cc, oc * P:(oc + 1) * P],
                                    xpart[c.slot][:, cc, :, now:now + TC],
                                    start=n == 0, stop=n == len(terms) - 1)
                return ins

            def out_project(c, b):
                for h in range(TH):
                    for cc in range(CC):
                        ins = pe.matmul(wo_ps[:, h, :], mixed[:, cc, b, h * P:(h + 1) * P], wo[:, cc, :],
                                        start=cc == 0, stop=cc == CC - 1)
                ins.then_inc(wo_done, 1)

            def score_rows(c):
                if c.exists:
                    pe.wait_ge(x1T_out, c.upto(CC))
                    pe.wait_ge(dest_done, c.upto(1))
                    pe.matmul(lg_ps, ones[0:1, :], bg_b[0:1, :].unsqueeze(1).broadcast_to([1, J, E]), start=True, stop=False)
                    for j in range(J):
                        for cc in range(CC):
                            ins = pe.matmul(lg_ps[:, j, :], x1T[:, cc, j * P:(j + 1) * P], wg[:, cc, :],
                                            start=False, stop=j == J - 1 and cc == CC - 1)
                    ins.then_inc(lg_done, 1)

            def step(i):
                for n in range(CC):
                    c = i + 1
                    if c.exists:
                        if n == 0:
                            if c.fixed and c.number == 0:
                                pe.wait_ge(w_lo, 1)
                            pe.wait_ge(xl_done, c.upto(CC + 1))
                        after(pe, gate_out, i.upto(CC, n + 1))
                        project(c, 0, n, vr_ps[n][:]).then_inc(vr_done, 1)
                    c = i - 2
                    if c.exists and n == CC - 1:
                        pe.wait_ge(x1_done, c.upto(J))
                        for cc in range(CC):
                            for j in range(J):
                                ins = pe.transpose(xT_ps[:, cc, j * P:(j + 1) * P],
                                                   rec[c.slot][:, j, 0, cc * P:(cc + 1) * P], ident[:])
                            ins.then_inc(x1T_done, 1)
                for n in range(CC):
                    c = i + 1
                    if c.exists:
                        if c.fixed and c.number == 0:
                            pe.wait_ge(w_lo, 2)
                        pe.wait_ge(v_out, c.upto(CC, n + 1))
                        project(c, 1, n, vr_ps[n][:]).then_inc(vr_done, 1)
                    if n == 0:
                        if not i.fixed or i.number < NCH:
                            score_rows(i - 2)
                        if (i + 2).exists:
                            transpose_x(i + 2)
                    c = i - 1
                    if c.exists:
                        if n == 0:
                            if c.fixed and c.number == 0:
                                pe.wait_ge(gate_in, 48)
                            after(pe, res_done, (c - 1).upto(2))
                        else:
                            pe.wait_ge(res_done, c.upto(2, 1))
                        pe.wait_ge(mixed_done, c.upto(B, n + 1))
                        out_project(c, n)
                if i.fixed and i.number == -2:
                    turn_biases()
                if i.fixed and i.number >= NCH:
                    score_rows(i - 2)
                c = i - 2
                if c.exists:
                    pe.wait_ge(route, c.upto(ROUTE1))
                    pe.matmul(rank_ps, before[:], picks[:], start=True, stop=False)
                    for j in range(J - 1):
                        pe.matmul(rank_ps[:, j + 1:J, :], ones[:], picks[:, j:j + 1, :].broadcast_to([P, J - 1 - j, E]),
                                  start=False, stop=False)
                    pe.matmul(rank_ps, ones[:], seen[:].unsqueeze(1).broadcast_to([P, J, E]), start=False, stop=True).then_inc(rank_done, 1)
                    if c.fixed and c.number == NCH - 1:
                        pe.wait_ge(slots, c.upto(ROUTE2, 4))
                        pe.matmul(cnt_ps, ones[:], seen[:], start=True, stop=True).then_inc(cnt_done, 1)
                c = i + 1
                if c.exists:
                    if c.fixed and c.number == 0:
                        pe.wait_ge(w_lo, 3)
                    after(pe, d2_done, i.upto(1))
                    for oc in range(CC):
                        project(c, 2, oc, k_ps[:, oc, :]).then_inc(k_done, 1)
            chunks(pe, step)

            phase_b_may_start(pe)

            def product1(t, s):
                for b in range(FC // 2):
                    after(pe, act_done, (t - 1).upto(FC, 2 * b + 2))
                    for f in range(2):
                        terms = [(cc, part, a) for cc in range(CC) for part, a in ((0, xTh), (0, xTl), (1, xTh))]
                        for k, (cc, part, xpart) in enumerate(terms):
                            off = cc * F + (2 * b + f) * P
                            ins = pe.matmul(hT_ps[b][:, f, :], wx[:, s, part, off:off + P], xpart[t.slot % 2][:, cc, :],
                                            start=k == 0, stop=k == len(terms) - 1)
                    ins.then_inc(mm1_done, 1)

            def product2(t, s, h):
                terms = [(fc, a, b) for fc in range(FC) for a, b in ((aTh, 0), (aTh, 1), (aTl, 0))]
                for k, (fc, apart, part) in enumerate(terms):
                    off = W1E + fc * C
                    ins = pe.matmul(y_ps[h], apart[t.slot % 2][:, fc, h * P:(h + 1) * P], wx[:, s, part, off:off + C],
                                    start=k == 0, stop=k == len(terms) - 1)
                ins.then_inc(mm2_done[h], 1)

            used = blocks_in_use(pe)

            def block_step(t):
                u = t + 2
                if u.exists:
                    with if_used(pe, used, u):
                        pe.wait_ge(rec_in[u.slot], u.turn(16, 16))
                        after(pe, txl_done, (u - 1).upto(1))
                        for cc in range(CC):
                            for h in range(BH):
                                ins = pe.transpose(xT2_ps[:, cc, h * P:(h + 1) * P], recs[u.slot][:, h, cc * P:(cc + 1) * P], ident[:])
                        ins.then_inc(tx_done, 1)
                u = t + 1
                if u.exists:
                    with if_used(pe, used, u):
                        expert = pe.value_load(ex_t[0:1, bass.ds(u.number, 1)], min_val=0, max_val=E - 1)
                        slot = expert % 2
                        pe.wait_ge(txl_done, u.upto(1))
                        pe.wait_ge(weights_ready, expert + 1)
                        with pe.If(slot == 0):
                            product1(u, 0)
                        with pe.Else():
                            product1(u, 1)
                if t.exists:
                    with if_used(pe, used, t):
                        slot = pe.value_load(par_t[0:1, bass.ds(t.number, 1)], min_val=0, max_val=1)
                        pe.wait_ge(aTl_done, t.upto(FC // 2))
                        after(pe, y_done, (t - 1).upto(BH))
                        with pe.If(slot == 0):
                            product2(t, 0, 0)
                        with pe.Else():
                            product2(t, 1, 0)
                        if t.fixed and t.number == 0:
                            with pe.If(slot == 0):
                                product2(t, 0, 1)
                            with pe.Else():
                                product2(t, 1, 1)
                        else:
                            full = pe.value_load(full_t[0:1, bass.ds(t.number, 1)], min_val=0, max_val=1)
                            with pe.If(full == 0):
                                pe.sem_inc(mm2_done[1], 1)
                            with pe.Else():
                                with pe.If(slot == 0):
                                    product2(t, 0, 1)
                                with pe.Else():
                                    product2(t, 1, 1)

            blocks(pe, block_step)

        @block.scalar
        def _(act):
            act.wait_ge(setup_dve, 1)
            act.activation(decay_c, decay_c, ACT.Exp).then_inc(setup_act, 1)

            def upper_weights(n):
                act.wait_ge(scaled[n], 2 * CC)
                act.activation(wq[:, n, :, 0, :, :], wscaled_of(n), ACT.Copy).then_inc(w_hi, 1)

            upper_weights(0)

            def copy_v(c, cc):
                act.wait_ge(vr_done, c.upto(2 * CC, cc + 1))
                if cc == 0:
                    after(act, bv_done, (c - 2).upto(1))
                act.activation(v[c.slot][:, cc], vr_ps[cc][:].rearrange("p (b t) -> p b t", b=B), ACT.Copy).then_inc(v_out, 1)

            def step(i):
                c = i + 1
                if c.exists:
                    copy_v(c, 0)
                if i.exists:
                    act.wait_ge(s_done, i.upto(CC))
                    after(act, num_done, (i - 1).upto(2, 1))
                    after(act, den_done, (i - 1).upto(1))
                    act.activation(A1[:], s_buf[:], ACT.Relu).then_inc(relu_done, 1)
                    act.activation(B1[:], s_buf[:], ACT.Relu, scale=-1.0).then_inc(relu_done, 1)
                c = i - 2
                if c.exists:
                    for cc in range(CC):
                        act.wait_ge(x1T_done, c.upto(CC, cc + 1))
                        act.activation(x1T[:, cc, :], xT_ps[:, cc, :], ACT.Copy).then_inc(x1T_out, 1)
                if i.exists:
                    act.wait_ge(d3_done, i.upto(1))
                    for cc in range(CC):
                        act.activation(A2[:, cc], A2[:, cc], ACT.Exp, bias=decay_c[:, cc:cc + 1]).then_inc(a2_done, 1)
                    act.wait_ge(d2_done, i.upto(1))
                    act.activation(B2[:], B2[:], ACT.Exp).then_inc(b2_done, 1)
                c = i + 1
                if c.exists:
                    copy_v(c, 1)
                if i.exists:
                    act.wait_ge(relu_done, i.upto(2))
                    act.activation(B1[:], B1[:], ACT.Exp, scale=-1.0).then_inc(b1_done, 1)
                    act.activation(A1[:], A1[:], ACT.Exp, scale=-1.0).then_inc(a1_done, 1)
                c = i + 2
                if c.exists:
                    act.wait_ge(xT_done, c.upto(CC))
                    after(act, k_done, (c - 2).upto(CC))
                    if not c.fixed or c.number > 0:
                        act.wait_ge(xh_done, (c - 1).upto(CC + 1))
                        act.activation(xh[c.slot][:, :, :, 0:1], xh[1 - c.slot][:, :, :, TC:TC + 1].bitcast(F32),
                                       ACT.Copy).then_inc(xh_done, 1)
                    for cc in range(CC):
                        act.activation(xh[c.slot][:, cc, :, 1:TC + 1], xT_ps[:, cc, :].rearrange("p (b t) -> p b t", b=B),
                                       ACT.Copy).then_inc(xh_done, 1)
                c = i - 2
                if c.exists:
                    act.wait_ge(x1_done, c.upto(J))
                    act.activation(rec[c.slot][:, :, 1, 0:C], rec[c.slot][:, :, 0, 0:C], ACT.Copy).then_inc(rec2_done, 1)
                c = i + 1
                if c.exists:
                    after(act, mixed_done, (c - 2).upto(B))
                    for cc in range(CC):
                        act.wait_ge(vr_done, c.upto(2 * CC, CC + cc + 1))
                        act.activation(gate[c.slot][:, cc], vr_ps[cc][:].rearrange("p (b t) -> p b t", b=B),
                                       ACT.Sigmoid).then_inc(gate_out, 1)
                if i.exists:
                    act.wait_ge(den_done, i.upto(1))
                    after(act, mixed_done, (i - 1).upto(B))
                    act.activation(r0[:], den[:], ACT.Ln).then_inc(ln_done, 1)
                    act.wait_ge(ln_done, i.upto(1))
                    act.activation(r0[:], r0[:], ACT.Exp, scale=-1.0).then_inc(r0_done, 1)
                c = i - 1
                if c.exists:
                    act.wait_ge(rstd_done, c.upto(1))
                    act.wait_ge(rec_out[c.slot], c.turn(REC_DMAS, BG))
                    act.wait_ge(x1_out[c.slot], c.turn(B * 16, BG))
                    for j in range(J):
                        act.activation(rec[c.slot][:, j, 0, 0:C], xres[c.slot][:, j // TH, j % TH, :], ACT.Identity,
                                       bias=shift[:, c.slot, j:j + 1], scale=rstd[:, c.slot, j:j + 1]).then_inc(x1_done, 1)
                c = i - 2
                if c.exists:
                    act.wait_ge(lg_done, c.upto(1))
                if i.fixed and i.number == -2:
                    upper_weights(1)
                    upper_weights(2)

            chunks(act, step)

            phase_b_may_start(act)
            act.wait_ge(pads_out, 16 * E)

            def load_records(u):
                row = act.value_load(row_t[0:1, bass.ds(u.number, 1)], min_val=0, max_val=DUMMY)
                act.dma_start(recs[u.slot][:], xs[bass.ds(row, BLK), :].rearrange("(h p) c -> p h c", p=P)).then_inc(rec_in[u.slot], 16)

            load_records(Step(None, 0, RING, BLOCKS))
            act.wait_ge(score_done, 1)
            act.activation(score_t[:, :, 0:1], score_t[:, :, 0:1], ACT.Exp).then_inc(exp_done, 1)

            def activate(u, expert, func):
                for b in range(FC // 2 + 1):
                    if b < FC // 2:
                        act.wait_ge(mm1_done, u.upto(FC // 2, b + 1))
                        after(act, aTl_done, (u - 1).upto(FC // 2, b + 1))
                        for f in range(2):
                            act.activation(act_T[:, 2 * b + f, :], hT_ps[b][:, f, :], func,
                                           bias=b1_c[:, bass.ds(expert * FC + (2 * b + f), 1)]).then_inc(act_done, 1)
                    if b > 0:
                        act.wait_ge(act_done, u.upto(FC, 2 * b))
                        for h in range(BH):
                            after(act, mm2_done[h], (u - 2).upto(1))
                        act.activation(aTh[u.slot % 2][:, 2 * b - 2:2 * b, :], act_T[:, 2 * b - 2:2 * b, :], ACT.Copy).then_inc(aTh_done, 1)

            used = blocks_in_use(act)

            def block_step(t):
                u = t + 3
                if u.exists:
                    with if_used(act, used, u):
                        after(act, txl_done, (u - RING).upto(1))
                        load_records(u)
                u = t + 1
                if u.exists:
                    with if_used(act, used, u):
                        expert = act.value_load(ex_t[0:1, bass.ds(u.number, 1)], min_val=0, max_val=E - 1)
                        with act.If(expert % 2 == 0):
                            activate(u, expert, ACT.Gelu)
                        with act.Else():
                            activate(u, expert, ACT.Silu)

            blocks(act, block_step)

            def second_outputs(i):
                act.wait_ge(yy_in[i.slot], i.turn(16, 16))
                after(act, c_sum2, (i - RING).upto(1))
                flat = score[:].rearrange("p n k -> p (n k)")
                for b in range(B):
                    act.activation(y2[i.slot][:, b, :], yy[i.slot][:, b, C:2 * C], ACT.Copy,
                                   scale=flat[:, bass.ds(column(i, b, 1), 1)]).then_inc(y2_done, 1)

            def out_step(i):
                second_outputs(i)
                if (i - 2).exists:
                    normalise(i - 2)

            def normalise(i):
                act.wait_ge(c_rstd, i.upto(1))
                if (i - RING).exists:
                    act.wait_ge(res_out[i.slot], i.turn(16))
                for b in range(B):
                    act.activation(res[i.slot][:, b, :], zz[i.slot][:, b, :], ACT.Identity,
                                   bias=shift_c[i.slot][:, b:b + 1], scale=rstd_c[i.slot][:, b:b + 1]).then_inc(c_res, 1)

            pieces(act, out_step)
            for n in range(PIECES - 2, PIECES):
                normalise(Step(None, n, RING, PIECES))

        @block.vector
        def _(dve):
            dve.wait_ge(consts_turned, 1)
            dve.tensor_copy(consts_c[:], small_ps[:, 256:256 + 5 * CC]).then_inc(setup_dve, 1)
            dve.wait_ge(setup_dve, 1)
            dve.tensor_scalar(unmix_c[:], mix_c, -1.0, 1.0, ALU.mult, ALU.add).then_inc(setup_dve, 1)
            dve.wait_ge(setup_dve, 2)
            scale_matrix(dve, 0)

            def lower_weights(n):
                dve.wait_ge(w_hi, n + 1)
                dve.tensor_tensor(wq[:, n, :, 1, :, :], wscaled_of(n), wq[:, n, :, 0, :, :].bitcast(F32), ALU.subtract).then_inc(w_lo, 1)

            lower_weights(0)

            def finish_setup():
                lower_weights(1)
                lower_weights(2)
                dve.wait_ge(setup_act, 1)
                dve.tensor_scalar(decay_c, decay_c, -1.0, None, ALU.mult).then_inc(setup_dve, 1)
                dve.wait_ge(setup_dve, 3)
                for cc in range(CC):
                    dve.tensor_copy(w_row[:, cc, :], decay_c[:, cc:cc + 1].broadcast_to([P, TC])).then_inc(setup_dve, 1)
                dve.memset(seen[:], 0.0).then_inc(setup_dve, 1)
                dve.wait_ge(setup_dve, 4 + CC)
                dve.wait_ge(made2, 7 + NCH)
                dve.wait_ge(bias1_turned, 1)
                dve.tensor_copy(b1_c[:], small_ps[:, 256:256 + E * FC]).then_inc(bias1_done, 1)

            def stabilise(i):
                if i.fixed and i.number == 0:
                    dve.memset(o_all[:, :, :, 0:1], LOWEST).then_inc(o_carry, 1)
                else:
                    dve.wait_ge(o_done, (i - 1).upto(CC * B))
                    dve.tensor_copy(o_all[:, :, :, 0:1], o_all[:, :, :, TC:TC + 1]).then_inc(o_carry, 1)
                dve.wait_ge(o_carry, i.upto(1))
                dve.wait_ge(k_done, i.upto(CC))
                for cc in range(CC):
                    for b in range(B):
                        dve.tensor_tensor_scan(o_all[:, cc, b, 1:TC + 1], w_row[:, cc, :],
                                               k_ps[:, cc, b * TC:(b + 1) * TC], o_all[:, cc, b, 0:1],
                                               ALU.add, ALU.max).then_inc(o_done, 1)
                dve.wait_ge(o_done, i.upto(CC * B))
                after(dve, relu_done, (i - 1).upto(2))
                for cc in range(CC):
                    dve.scalar_tensor_tensor(out=s_buf[:, cc], in0=k_ps[:, cc, :].rearrange("p (b t) -> p b t", b=B),
                                             scalar=first_c[:, cc:cc + 1], in1=o_all[:, cc, :, 0:TC],
                                             op0=ALU.add, op1=ALU.subtract).then_inc(s_done, 1)
                dve.tensor_tensor(A2[:], o_all[:, :, :, 0:TC], o_all[:, :, :, 1:TC + 1], ALU.subtract).then_inc(d3_done, 1)
                after(dve, b2v_done, (i - 1).upto(1))
                dve.tensor_tensor(B2[:], k_ps[:].rearrange("p c (b t) -> p c b t", b=B), o_all[:, :, :, 1:TC + 1],
                                  ALU.subtract).then_inc(d2_done, 1)

            def divide(c):
                dve.wait_ge(r0_done, c.upto(1))
                after(dve, wo_done, (c - 1).upto(2))
                dve.tensor_tensor(newton[:], den[:], r0[:], ALU.mult).then_inc(div_done, 1)
                dve.wait_ge(div_done, c.upto(3, 1))
                dve.scalar_tensor_tensor(out=newton[:], in0=newton[:], scalar=2.0, in1=r0[:],
                                         op0=ALU.subtract, op1=ALU.mult).then_inc(div_done, 1)
                dve.wait_ge(div_done, c.upto(3, 2))
                dve.wait_ge(num_done, c.upto(2))
                dve.tensor_tensor(newton[:], num[:], newton[:], ALU.mult).then_inc(div_done, 1)
                dve.wait_ge(div_done, c.upto(3))
                dve.wait_ge(gate_out, c.upto(CC))
                for b in range(B):
                    dve.scalar_tensor_tensor(out=mixed[:, :, b, :], in0=newton[:, :, b, :], scalar=-1.0, in1=gate[c.slot][:, :, b, :],
                                             op0=ALU.mult, op1=ALU.mult).then_inc(mixed_done, 1)

            def choose(c):
                dve.wait_ge(lg_done, c.upto(1))
                take_wait(dve)
                for j in range(J):
                    dve.max(m8[:, j, :], lg_ps[:, j, :]).then_inc(route, 1)
                dve.wait_ge(route, c.upto(ROUTE1, J))
                take_wait(dve)
                for j in range(J):
                    dve.max_index(i8[:, j, :], m8[:, j, :], lg_ps[:, j, :]).then_inc(route, 1)
                dve.tensor_copy(top2[:].rearrange("p i j k -> p (i j k)")[:, bass.ds(c.number * (2 * J), 2 * J)].rearrange(
                    "p (j k) -> p j k", j=J), m8[:, :, 0:2]).then_inc(top2_done, 1)
                dve.wait_ge(route, c.upto(ROUTE1, 2 * J))
                dve.tensor_copy(idxf[:], i8[:, :, 0:2]).then_inc(route, 1)
                dve.wait_ge(route, c.upto(ROUTE1, 1 + 2 * J))
                dve.tensor_tensor(hot[:], expert_no[:].unsqueeze(1).unsqueeze(1).broadcast_to([P, J, 2, E]),
                                  idxf[:].unsqueeze(3).broadcast_to([P, J, 2, E]), ALU.is_equal).then_inc(route, 1)
                dve.wait_ge(route, c.upto(ROUTE1, 2 + 2 * J))
                dve.tensor_tensor(picks[:], hot[:, :, 0, :], hot[:, :, 1, :], ALU.add).then_inc(route, 1)

            def accumulate(i):
                dve.wait_ge(a2_done, i.upto(CC))
                dve.wait_ge(b2_done, i.upto(1))
                if i.fixed and i.number == 0:
                    dve.memset(q_all[:, :, :, 0:1], 0.0).then_inc(qp_carry, 1)
                    dve.memset(p_all[:, :, :, 0:1], 0.0).then_inc(qp_carry, 1)
                else:
                    dve.wait_ge(aq_done, (i - 1).upto(1))
                    dve.tensor_copy(q_all[:, :, :, 0:1], q_all[:, :, :, TC:TC + 1]).then_inc(qp_carry, 1)
                    dve.tensor_copy(p_all[:, :, :, 0:1], p_all[:, :, :, TC:TC + 1]).then_inc(qp_carry, 1)
                dve.wait_ge(qp_carry, i.upto(2))
                for all_, add, done in ((q_all, B2, q_done), (p_all, b2v, p_done)):
                    if all_ is p_all:
                        dve.wait_ge(b2v_done, i.upto(1))
                    for cc in range(CC):
                        for b in range(B):
                            dve.tensor_tensor_scan(all_[:, cc, b, 1:TC + 1], A2[:, cc, b, :], add[:, cc, b, :],
                                                   all_[:, cc, b, 0:1], ALU.mult, ALU.add).then_inc(done, 1)

            def lower_halves(c):
                dve.wait_ge(xh_done, c.upto(CC + 1))
                after(dve, k_done, (c - 2).upto(CC))
                if not c.fixed or c.number > 0:
                    dve.wait_ge(xl_done, (c - 1).upto(CC + 1))
                    dve.tensor_copy(xl[c.slot][:, :, :, 0:1],
                                    xl[1 - c.slot][:, :, :, TC:TC + 1].bitcast(F32)).then_inc(xl_done, 1)
                for cc in range(CC):
                    dve.tensor_tensor(xl[c.slot][:, cc, :, 1:TC + 1], xT_ps[:, cc, :].rearrange("p (b t) -> p b t", b=B),
                                      xh[c.slot][:, cc, :, 1:TC + 1].bitcast(F32), ALU.subtract).then_inc(xl_done, 1)

            def numerator(i):
                dve.wait_ge(a1_done, i.upto(1))
                dve.wait_ge(p_done, i.upto(CC * B))
                dve.tensor_tensor(num[:], A1[:], p_all[:, :, :, 0:TC], ALU.mult).then_inc(num_done, 1)
                dve.wait_ge(num_done, i.upto(2, 1))
                dve.wait_ge(bv_done, i.upto(1))
                dve.tensor_tensor(num[:], num[:], bv[:], ALU.add).then_inc(num_done, 1)

            def statistics(c):
                dve.wait_ge(res_done, c.upto(2))
                for j in range(J):
                    dve.bn_stats(stats[:, j, :], xres[c.slot][:, j // TH, j % TH, :]).then_inc(bn_done, 1)
                dve.wait_ge(bn_done, c.upto(J))
                take_wait(dve)
                for j in range(J):
                    dve.bn_aggr(mv[:, j, :], stats[:, j, :]).then_inc(mv_done, 1)

            def place(c):
                dve.wait_ge(rank_done, c.upto(1))
                dve.tensor_tensor(rank[:], rank_ps, region_no[:].unsqueeze(1).broadcast_to([P, J, E]), ALU.add).then_inc(slots, 1)
                dve.tensor_reduce(newly[:], picks[:].rearrange("p j e -> p e j"), AX.X, ALU.add).then_inc(slots, 1)
                dve.wait_ge(slots, c.upto(ROUTE2, 2))
                dve.tensor_tensor(spread[:], hot[:], rank[:].unsqueeze(2).broadcast_to([P, J, 2, E]), ALU.mult).then_inc(slots, 1)
                dve.wait_ge(slots, c.upto(ROUTE2, 3))
                dve.tensor_tensor(seen[:], seen[:], newly[:], ALU.add).then_inc(slots, 1)
                dve.wait_ge(slots, c.upto(ROUTE2, 4))
                dve.tensor_reduce(slot_f[:], spread[:], AX.X, ALU.add).then_inc(slots, 1)
                dve.wait_ge(slots, c.upto(ROUTE2, 5))
                dve.tensor_copy(slot_i[c.slot][:].rearrange("p (j k) -> p j k", j=J), slot_f[:]).then_inc(slots, 1)

            def label(c):
                dve.wait_ge(rec_out[c.slot], c.turn(REC_DMAS, BG))
                dve.tensor_copy(rec[c.slot][:, :, :, C:REC].bitcast(I32),
                                dest_all[:, bass.ds(c.number * (2 * J), 2 * J)].rearrange("p (j k a) -> p j k a", j=J, a=1)
                                ).then_inc(dest_done, 1)

            def residual_0(c):
                add_residual(c, 0)

            def residual_1(c):
                add_residual(c, 1)

            def add_residual(c, b):
                dve.wait_ge(wo_done, c.upto(2, b + 1))
                if b == 0:
                    dve.wait_ge(xres_in[c.slot], c.turn(16 * B, 16 * B))
                dve.tensor_tensor(xres[c.slot][:, b], wo_ps[:], xres[c.slot][:, b], ALU.add).then_inc(res_done, 1)

            def step(i):
                stages = [(stabilise, i), (divide, i - 1)]
                if i.fixed and i.number >= NCH - 1:
                    stages += [(accumulate, i), (residual_0, i - 1), (numerator, i), (residual_1, i - 1), (statistics, i - 1),
                               (choose, i - 2), (place, i - 2), (label, i - 1)]
                else:
                    stages += [(choose, i - 2), (residual_0, i - 1), (accumulate, i), (lower_halves, i + 2), (numerator, i),
                               (residual_1, i - 1), (statistics, i - 1), (place, i - 2), (label, i - 1)]
                for stage, c in stages:
                    if c.exists:
                        stage(c)
                if i.fixed and i.number == -2:
                    finish_setup()

            chunks(dve, step)

            step_no = [0]

            def link(ins):
                step_no[0] += 1
                ins.then_inc(table, 1)
                dve.wait_ge(table, step_no[0])

            dve.wait_ge(made, 4)
            dve.wait_ge(cnt_done, 1)
            link(dve.tensor_copy(cnt_f[:], cnt_ps[0:1, :]))
            link(dve.tensor_tensor(pad_row[:], cnt_f[:], region_no[0:1, :], ALU.add))
            link(dve.tensor_scalar(cnt_i[:], cnt_f[:], 1.0, float(BLK - 1), ALU.max, ALU.add))
            link(dve.tensor_scalar(blocks_i[:], cnt_i[:], BLK.bit_length() - 1, None, ALU.logical_shift_right))
            link(dve.tensor_copy(blocks_f[:], blocks_i[:]))
            link(dve.tensor_tensor_scan(ends_f[:], ones[0:1, 0:E], blocks_f[:], 0.0, ALU.mult, ALU.add))
            link(dve.tensor_tensor(starts_f[:], ends_f[:], blocks_f[:], ALU.subtract))
            link(dve.tensor_copy(ends[:], ends_f[:]))
            link(dve.scalar_tensor_tensor(out=rowbase[:], in0=starts_f[:], scalar=-float(BLK), in1=region_no[0:1, :],
                                          op0=ALU.mult, op1=ALU.add))
            link(dve.scalar_tensor_tensor(out=restbase[:], in0=starts_f[:], scalar=float(BLK), in1=cnt_f[:],
                                          op0=ALU.mult, op1=ALU.add))
            over = lambda a: a[:].unsqueeze(1).broadcast_to([1, BLOCKS, E])
            link(dve.tensor_tensor(past_s[:], block_f[:], over(starts_f), ALU.is_ge))
            link(dve.tensor_tensor(past_e[:], block_f[:], over(ends_f), ALU.is_ge))
            link(dve.tensor_tensor(past_s[:], past_s[:], past_e[:], ALU.subtract))
            link(dve.tensor_reduce(ex_f[:], past_e[:], AX.X, ALU.add))
            link(dve.tensor_tensor(past_e[:], past_s[:], over(restbase), ALU.mult))
            link(dve.tensor_tensor(past_s[:], past_s[:], over(rowbase), ALU.mult))
            link(dve.tensor_reduce(row_f[:], past_s[:], AX.X, ALU.add))
            link(dve.tensor_reduce(rest_f[:], past_e[:], AX.X, ALU.add))
            link(dve.tensor_tensor(rest_f[:], rest_f[:], block_row[:], ALU.subtract))
            link(dve.tensor_scalar(full_t[:], rest_f[:], float(P + DUMMY), None, ALU.is_gt))
            link(dve.tensor_scalar(real_f[:], ex_f[:], float(E), None, ALU.is_lt))
            link(dve.tensor_tensor(real_f[:], real_f[:], block_row[:], ALU.mult))
            link(dve.scalar_tensor_tensor(out=row_t[:], in0=row_f[:], scalar=float(DUMMY), in1=real_f[:],
                                          op0=ALU.add, op1=ALU.add))
            link(dve.tensor_scalar(ex_t[:], ex_f[:], float(E - 1), None, ALU.min))
            link(dve.tensor_scalar(par_t[:], ex_t[:], 1, None, ALU.bitwise_and))
            dve.tensor_tensor(score_t[:, :, 0:1], top2[:].rearrange("p i j k -> p (i j) k")[:, :, 1:2],
                              top2[:].rearrange("p i j k -> p (i j) k")[:, :, 0:1], ALU.subtract).then_inc(score_done, 1)
            dve.tensor_copy(cnt_f[:], cnt_f[:]).then_inc(table_done, 1)
            phase_b_may_start(dve)

            used = blocks_in_use(dve)

            def block_step(t):
                u = t - 1
                if u.exists:
                    with if_used(dve, used, u):
                        expert = dve.value_load(ex_t[0:1, bass.ds(u.number, 1)], min_val=0, max_val=E - 1)
                        if u.fixed and u.number == 0:
                            dve.wait_ge(bias_in, 16)
                        after(dve, y_out[u.slot], u.turn(16 * BH))
                        for h in range(BH):
                            dve.wait_ge(mm2_done[h], u.upto(1))
                            dve.tensor_tensor(y_sb[u.slot][:, h, :], y_ps[h], b2_b[:, bass.ds(expert * C, C)],
                                              ALU.add).then_inc(y_done, 1)
                u = t + 2
                if u.exists:
                    with if_used(dve, used, u):
                        dve.wait_ge(tx_done, u.upto(1))
                        after(dve, mm1_done, (u - 2).upto(FC // 2))
                        dve.tensor_copy(xTh[u.slot % 2][:], xT2_ps[:]).then_inc(txh_done, 1)
                        after(dve, y_out[u.slot], u.turn(16 * BH))
                        dve.tensor_copy(dest[u.slot][:], recs[u.slot][:, :, C:REC].rearrange("p h a -> p (h a)").bitcast(I32)).then_inc(table, 1)
                        dve.wait_ge(txh_done, u.upto(1))
                        dve.tensor_tensor(xTl[u.slot % 2][:], xT2_ps[:], xTh[u.slot % 2][:].bitcast(F32),
                                          ALU.subtract).then_inc(txl_done, 1)
                u = t + 1
                if u.exists:
                    with if_used(dve, used, u):
                        for h in range(BH):
                            after(dve, mm2_done[h], (u - 2).upto(1))
                        for b in range(FC // 2):
                            dve.wait_ge(aTh_done, u.upto(FC // 2, b + 1))
                            dve.tensor_tensor(aTl[u.slot % 2][:, 2 * b:2 * b + 2, :], act_T[:, 2 * b:2 * b + 2, :],
                                              aTh[u.slot % 2][:, 2 * b:2 * b + 2, :].bitcast(F32),
                                              ALU.subtract).then_inc(aTl_done, 1)

            dve.wait_ge(exp_done, 1)
            link(dve.tensor_scalar(score[:, :, 1:2], score_t[:, :, 0:1], 1.0, None, ALU.add))
            link(dve.reciprocal(score[:, :, 0:1], score[:, :, 1:2]))
            link(dve.tensor_tensor(score[:, :, 1:2], score_t[:, :, 0:1], score[:, :, 0:1], ALU.mult))
            blocks(dve, block_step)

            dve.wait_ge(xx_in, 16 * B)

            flat = score[:].rearrange("p n k -> p (n k)")

            def first_sum(i):
                dve.wait_ge(yy_in[i.slot], i.turn(16, 16))
                after(dve, c_res, (i - RING).upto(B))
                for b in range(B):
                    dve.scalar_tensor_tensor(
                        out=zz[i.slot][:, b, :], in0=yy[i.slot][:, b, 0:C], scalar=flat[:, bass.ds(column(i, b, 0), 1)],
                        in1=xx[:, bass.ds(i.number, 1), b, :].rearrange("p a c -> p (a c)"),
                        op0=ALU.mult, op1=ALU.add).then_inc(c_sum, 1)

            def second_sum(i):
                dve.wait_ge(c_sum, i.upto(B))
                dve.wait_ge(y2_done, i.upto(B))
                dve.tensor_tensor(zz[i.slot][:], zz[i.slot][:], y2[i.slot][:], ALU.add).then_inc(c_sum2, 1)

            def statistics(i):
                n = i.slot
                dve.wait_ge(c_sum2, i.upto(1))
                for b in range(B):
                    dve.bn_stats(stats_c[n][:, b, :], zz[n][:, b, :]).then_inc(c_bn, 1)

            def means(i):
                n = i.slot
                dve.wait_ge(c_bn, i.upto(B))
                after(dve, c_rstd, (i - RING).upto(1))
                take_wait(dve)
                for b in range(B):
                    dve.bn_aggr(mv_c[n][:, b, :], stats_c[n][:, b, :]).then_inc(c_mv, 1)

            def out_step(i):
                for stage, c in ((first_sum, i), (statistics, i - 1), (second_sum, i), (means, i - 1)):
                    if c.exists:
                        stage(c)

            pieces(dve, out_step)
            last = Step(None, PIECES - 1, RING, PIECES)
            statistics(last)
            means(last)


INPUTS = ["L0_attn_x", "L0_attn_time_decay", "L0_attn_time_first", "L0_attn_time_mix_k", "L0_attn_time_mix_v",
          "L0_attn_time_mix_r", "L0_attn_Wk", "L0_attn_Wv", "L0_attn_Wr", "L0_attn_Wo", "L0_ffn_W1", "L0_ffn_b1",
          "L0_ffn_W2", "L0_ffn_b2", "L0_ffn_Wg", "L0_ffn_bg"]
TRANSPOSED = {"L0_attn_Wk", "L0_attn_Wv", "L0_attn_Wr", "L0_attn_Wo"}


def kernel(**inputs):
    import concourse.bacc as bacc
    from concourse.bass_utils import run_bass_kernel_spmd

    nc = bacc.Bacc("TRN2", target_bir_lowering=False, num_devices=1)
    arrays, aps = {}, []
    for name in INPUTS:
        a = np.asarray(inputs[name])
        a = np.ascontiguousarray(a.T if name in TRANSPOSED else a)
        arrays[f"in_{name}"] = a
        aps.append(nc.dram_tensor(f"in_{name}", a.shape, mybir.dt.from_np(a.dtype), kind="ExternalInput").ap())
    shape = arrays["in_L0_attn_x"].shape
    aps.append(nc.dram_tensor("out", shape, F32, kind="ExternalOutput").ap())
    build(nc, *aps)
    return run_bass_kernel_spmd(nc, [arrays], core_ids=[0]).results[0]["out"]
```
